# Optimizing a Trainium2 kernel written in Bass

```python
import numpy as np
import jax
import jax.numpy as jnp

def _softmax(x, axis=-1):
    return jax.nn.softmax(x, axis=axis)

def _gelu(x):
    return jax.nn.gelu(x, approximate=True)

def _silu(x):
    return jax.nn.silu(x)

def _sigmoid(x):
    return jax.nn.sigmoid(x)

def _layernorm(x, axis=-1, eps=1e-05):
    m = jnp.mean(x, axis=axis, keepdims=True)
    v = jnp.var(x, axis=axis, keepdims=True)
    return (x - m) / jnp.sqrt(v + eps)

def _scatter_add(tgt, idx, src, axis=0):
    return tgt.at[idx].add(src)

def _segment_sum(src, seg, n):
    return jax.ops.segment_sum(src, seg, n)
kernel_name = 'mk_macaron_d1_jaxref_r4_9efb2f'

def setup_inputs(seed: int=0):
    np.random.seed(seed)
    _w = jnp.asarray

    def _L0_attn_setup():
        import jax, jax.numpy as jnp
        import numpy as np
        B, S, H = (1, 512, 1024)
        NH = 32
        QK_NOPE, QK_ROPE, V_DIM = (128, 64, 128)
        Q_LORA, KV_LORA = (384, 128)
        EPS = 1e-06

        def _rms_norm(x, w):
            return x * jax.lax.rsqrt(jnp.mean(x * x, axis=-1, keepdims=True) + EPS) * w

        def _rope_cos_sin(seqlen, dim):
            freqs = 1.0 / 10000.0 ** (jnp.arange(0, dim, 2, dtype=jnp.float32) / dim)
            t = jnp.arange(seqlen, dtype=jnp.float32)
            ang = jnp.outer(t, freqs)
            return (jnp.cos(ang), jnp.sin(ang))

        def _apply_rope(x, cos, sin):
            x1 = x[..., 0::2]
            x2 = x[..., 1::2]
            r1 = x1 * cos - x2 * sin
            r2 = x1 * sin + x2 * cos
            return jnp.stack([r1, r2], axis=-1).reshape(x.shape)
        key = jax.random.key(seed)
        ks = jax.random.split(key, 7)
        s = 0.02
        return {'x': jax.random.normal(ks[0], (B, S, H), jnp.float32), 'wq_a': jax.random.normal(ks[1], (Q_LORA, H), jnp.float32) * s, 'q_norm_w': jnp.ones((Q_LORA,), jnp.float32), 'wq_b': jax.random.normal(ks[2], (NH * (QK_NOPE + QK_ROPE), Q_LORA), jnp.float32) * s, 'wkv_a': jax.random.normal(ks[3], (KV_LORA + QK_ROPE, H), jnp.float32) * s, 'kv_norm_w': jnp.ones((KV_LORA,), jnp.float32), 'wkv_b': jax.random.normal(ks[4], (NH * (QK_NOPE + V_DIM), KV_LORA), jnp.float32) * s, 'wo': jax.random.normal(ks[5], (H, NH * V_DIM), jnp.float32) * s}
    _L0_attn_in = _L0_attn_setup()

    def _L0_ffn_setup():
        import jax, jax.numpy as jnp
        import numpy as np
        B_, S, D = (4, 1024, 1024)
        E, R, O = (8, 16, 1024)
        TOP_K = 2
        SCALING = 8.0 / R
        key = jax.random.key(seed)
        ks = jax.random.split(key, 5)
        x = jax.random.normal(ks[0], (B_, S, D), dtype=jnp.float32)
        router_w = jax.random.normal(ks[1], (E, D), dtype=jnp.float32) * (1.0 / np.sqrt(D))
        router_b = jax.random.normal(ks[2], (E,), dtype=jnp.float32) * 0.01
        A = jax.random.normal(ks[3], (E, R, D), dtype=jnp.float32) * (1.0 / np.sqrt(D))
        Bm = jax.random.normal(ks[4], (E, O, R), dtype=jnp.float32) * 0.02
        return {'x': x, 'router_w': router_w, 'router_b': router_b, 'A': A, 'Bm': Bm}
    _L0_ffn_in = _L0_ffn_setup()
    _d = {'L0_attn_x': _L0_attn_in['x'], 'L0_attn_wq_a': _L0_attn_in['wq_a'], 'L0_attn_q_norm_w': _L0_attn_in['q_norm_w'], 'L0_attn_wq_b': _L0_attn_in['wq_b'], 'L0_attn_wkv_a': _L0_attn_in['wkv_a'], 'L0_attn_kv_norm_w': _L0_attn_in['kv_norm_w'], 'L0_attn_wkv_b': _L0_attn_in['wkv_b'], 'L0_attn_wo': _L0_attn_in['wo'], 'L0_ffn_router_w': _L0_ffn_in['router_w'], 'L0_ffn_router_b': _L0_ffn_in['router_b'], 'L0_ffn_A': _L0_ffn_in['A'], 'L0_ffn_Bm': _L0_ffn_in['Bm']}
    _x0 = _d['L0_attn_x']
    _d['L0_attn_x'] = jax.random.normal(jax.random.fold_in(jax.random.key(seed), 1), (4, 512, 1024), dtype=_x0.dtype)
    del _x0
    return _d

def reference(L0_attn_x, L0_attn_wq_a, L0_attn_q_norm_w, L0_attn_wq_b, L0_attn_wkv_a, L0_attn_kv_norm_w, L0_attn_wkv_b, L0_attn_wo, L0_ffn_router_w, L0_ffn_router_b, L0_ffn_A, L0_ffn_Bm):

    def _L0_attn_ref(x, wq_a, q_norm_w, wq_b, wkv_a, kv_norm_w, wkv_b, wo):
        import jax, jax.numpy as jnp
        import numpy as np
        B, S, H = (1, 512, 1024)
        NH = 32
        QK_NOPE, QK_ROPE, V_DIM = (128, 64, 128)
        Q_LORA, KV_LORA = (384, 128)
        EPS = 1e-06

        def _rms_norm(x, w):
            return x * jax.lax.rsqrt(jnp.mean(x * x, axis=-1, keepdims=True) + EPS) * w

        def _rope_cos_sin(seqlen, dim):
            freqs = 1.0 / 10000.0 ** (jnp.arange(0, dim, 2, dtype=jnp.float32) / dim)
            t = jnp.arange(seqlen, dtype=jnp.float32)
            ang = jnp.outer(t, freqs)
            return (jnp.cos(ang), jnp.sin(ang))

        def _apply_rope(x, cos, sin):
            x1 = x[..., 0::2]
            x2 = x[..., 1::2]
            r1 = x1 * cos - x2 * sin
            r2 = x1 * sin + x2 * cos
            return jnp.stack([r1, r2], axis=-1).reshape(x.shape)
        b, s, _ = x.shape
        cos, sin = _rope_cos_sin(s, QK_ROPE)
        q = _rms_norm(x @ wq_a.T, q_norm_w) @ wq_b.T
        q = q.reshape(b, s, NH, QK_NOPE + QK_ROPE)
        q_nope, q_pe = (q[..., :QK_NOPE], q[..., QK_NOPE:])
        q_pe = _apply_rope(q_pe, cos[None, :, None, :], sin[None, :, None, :])
        kv = x @ wkv_a.T
        kv_c, k_pe = (kv[..., :KV_LORA], kv[..., KV_LORA:])
        k_pe = _apply_rope(k_pe, cos[None, :, :], sin[None, :, :])
        kv_up = _rms_norm(kv_c, kv_norm_w) @ wkv_b.T
        kv_up = kv_up.reshape(b, s, NH, QK_NOPE + V_DIM)
        k_nope, v = (kv_up[..., :QK_NOPE], kv_up[..., QK_NOPE:])
        scale = 1.0 / jnp.sqrt(jnp.float32(QK_NOPE + QK_ROPE))
        scores = (jnp.einsum('bshd,bthd->bhst', q_nope, k_nope) + jnp.einsum('bshd,btd->bhst', q_pe, k_pe)) * scale
        causal = jnp.tril(jnp.ones((s, s), bool))
        scores = jnp.where(causal[None, None], scores, jnp.finfo(scores.dtype).min)
        probs = jax.nn.softmax(scores, axis=-1)
        out = jnp.einsum('bhst,bthd->bshd', probs, v).reshape(b, s, NH * V_DIM)
        return out @ wo.T

    def _L0_ffn_ref(x, router_w, router_b, A, Bm):
        import jax, jax.numpy as jnp
        import numpy as np
        B_, S, D = (4, 1024, 1024)
        E, R, O = (8, 16, 1024)
        TOP_K = 2
        SCALING = 8.0 / R
        flat = x.reshape(-1, x.shape[-1])
        N = flat.shape[0]
        logits = flat @ router_w.T + router_b
        probs = jax.nn.softmax(logits, axis=-1)
        topv, topi = jax.lax.top_k(probs, TOP_K)
        gates = topv / jnp.sum(topv, axis=-1, keepdims=True)
        w = jnp.zeros((N, E), dtype=flat.dtype).at[jnp.arange(N)[:, None], topi].add(gates)
        h = jnp.einsum('nd,erd->ner', flat, A)
        hw = h * w[:, :, None]
        out = jnp.einsum('ner,eor->no', hw, Bm) * SCALING
        return out.reshape(*x.shape[:-1], O)
    x = L0_attn_x
    x = x + 0.5 * _L0_ffn_ref(_layernorm(x, axis=-1), L0_ffn_router_w, L0_ffn_router_b, L0_ffn_A, L0_ffn_Bm)
    x = x + _L0_attn_ref(_layernorm(x, axis=-1), L0_attn_wq_a, L0_attn_q_norm_w, L0_attn_wq_b, L0_attn_wkv_a, L0_attn_kv_norm_w, L0_attn_wkv_b, L0_attn_wo)
    x = x + 0.5 * _L0_ffn_ref(_layernorm(x, axis=-1), L0_ffn_router_w, L0_ffn_router_b, L0_ffn_A, L0_ffn_Bm)
    return x

_drawn_inputs = setup_inputs


def setup_inputs(seed=0):
    import zlib

    import numpy as np

    out = dict(_drawn_inputs(seed))
    spreads = {'L0_attn_q_norm_w': (1.0, 0.6), 'L0_attn_kv_norm_w': (1.0, 0.6)}
    factors = {'L0_attn_wq_a': 8.0, 'L0_attn_wq_b': 8.0, 'L0_ffn_router_b': 8.0}
    for name, (base, spread) in spreads.items():
        noise = np.random.default_rng([zlib.crc32(name.encode()), seed]).standard_normal(out[name].shape)
        drawn = base * np.exp(spread * noise) if base else spread * noise
        out[name] = jnp.asarray(drawn.astype(out[name].dtype))
    for name, factor in factors.items():
        out[name] = (out[name] * factor).astype(out[name].dtype)
    return out
```

```python
from contextlib import ExitStack

import concourse.bass as bass
from concourse import mybir

ALU = mybir.AluOpType
ACT = mybir.ActivationFunctionType
F32 = mybir.dt.float32
F32R = mybir.dt.float32r
AX_X = mybir.AxisListType.X

P = 128
MASKED = -1.0e30
LN_EPS = 1e-5
RMS_EPS = 1e-6


def build_macaron(nc, x, wzkv, qnorm, kvnorm, wqn, wpe, wk, wv, wo, ra, rb, bm,
                  c_ident, c_mask, c_tri, c_tok, c_pos, out):
    TOK, D = x.shape
    SEQ = c_pos.shape[2]
    NPAIR = TOK // SEQ // 2
    NT = 2 * SEQ // P
    PT_ = 2 * SEQ
    KD = D // P
    NH, _, QL = wqn.shape
    KQ = QL // P
    L = wk.shape[2]
    RO = c_tok.shape[2]
    ZK = QL + L + RO
    NG = NH // 2
    E = rb.shape[0]
    R = (ra.shape[1] - E) // E
    ER = E * R
    RA = E + ER
    NS = SEQ // P
    HALF = 512
    QSCALE = float((P + RO) ** -0.5)
    FFN_SCALE = 0.5 * 8.0 / R
    EV = 8
    EVD = 6

    xt = x.rearrange("(t p) d -> t p d", p=P)
    outt = out.rearrange("(t p) d -> t p d", p=P)

    def poff(i):
        return P * i * (i + 1) // 2

    with ExitStack() as ctx:
        def sb(name, shape, dt=F32):
            return ctx.enter_context(nc.sbuf_tensor(name, shape, dt))

        def sem(name):
            return ctx.enter_context(nc.semaphore(name))

        xacc = sb("xacc", [P, NT, D])
        zT = sb("zT", [P, 2, KQ, PT_], F32R)
        keyT = sb("keyT", [P, 2, PT_], F32R)
        ropeT = sb("ropeT", [P, 2, PT_], F32R)
        lat = sb("lat", [P, 2, NT, L], F32R)
        ident = sb("ident", [P, P])
        ident_r = sb("ident_r", [P, P], F32R)
        mask_f = sb("mask_f", [P, P])
        mask_r = sb("mask_r", [P, P], F32R)
        tri = sb("tri", [P, E, E])
        tok_tab = sb("tok_tab", [P, NT, 2, RO])
        pos_tab = sb("pos_tab", [P, 2, SEQ])
        qn_bc = sb("qn_bc", [P, QL])
        kvn_bc = sb("kvn_bc", [P, L])
        rb_bc = sb("rb_bc", [P, E])
        neg_half = sb("neg_half", [P, 2])
        n_ffn = 2 * KD * ZK + 2 * KD * RA + 2 * D + 4 * KD * P + 4 * P
        n_att = 4 * D + 4 * QL + 2 * QL + 4 * SEQ + 4 * SEQ + 8 * SEQ + 2 * NS * SEQ + 2 * SEQ
        arena = sb("arena", [P, max(n_ffn, n_att)], F32R)
        at = [0]

        def take(t, *dims):
            n = 1
            for d in dims:
                n *= d
            ap = t[:, at[0]:at[0] + n]
            at[0] += n
            names = "abcd"[:len(dims)]
            if len(dims) > 1:
                ap = ap.rearrange(f"p ({' '.join(names)}) -> p {' '.join(names)}",
                                  **{c: d for c, d in zip(names, dims)})
            return ap

        w_lat = take(arena, 2, KD, ZK)
        w_ra = take(arena, 2, KD, RA)
        w_bm = take(arena, 2, D)
        xnT = take(arena, 2, 2, KD * P)
        hwT = take(arena, 2, 2, P)
        at[0] = 0
        w_out = take(arena, 2, 2, D)
        w_q = take(arena, 2, 2, QL)
        w_pe = take(arena, 2, QL)
        qT = take(arena, 2, 2, SEQ)
        qst = take(arena, 2, 2, SEQ)
        oT = take(arena, 2, 2, 2, SEQ)
        pT = take(arena, 2, NS, SEQ)
        rope_r = take(arena, 2, SEQ)
        n_ffn = 2 * ZK + KD * RA + D + 2 * D + NT * RA + 2 * ZK + RO
        n_att = 2 * QL + 2 * L + 2 * L + 2 * D + QL + 2 * poff(NS) + 3 * SEQ
        stage = sb("stage", [P, max(n_ffn, n_att)])
        at[0] = 0
        s_lat = take(stage, 2, ZK)
        s_ra = take(stage, KD, RA)
        s_bm = take(stage, D)
        xn = take(stage, 2, D)
        cmp = xn.rearrange("p b (t e f) -> p b t e f", e=E, f=E)[:, :, 0:NT]
        hb = take(stage, NT, RA)
        zr = take(stage, ZK)
        zck = take(stage, ZK + RO)
        at[0] = 0
        s_wqn = take(stage, 2, QL)
        s_wk = take(stage, 2, L)
        s_wv = take(stage, 2, L)
        s_wo = take(stage, 2, D)
        s_wpe = take(stage, KQ, P)
        prob = take(stage, 2, poff(NS))
        rope_f = take(stage, 3, SEQ)
        stats = sb("stats", [P, 2, 6])
        mv = sb("mv", [P, 2])
        mom = sb("mom", [P, NT, 4])
        lgt = sb("lgt", [P, 3, NT, E])
        rank = sb("rank", [P, NT, E])
        gsc = sb("gsc", [P, 3, NT])
        hw = sb("hw", [P, ER])
        ssq = sb("ssq", [P, 2, 2])
        rms = sb("rms", [P, 2])
        junk = sb("junk", [P, QL])
        rtmp = sb("rtmp", [P, 2, RO])
        negmax = sb("negmax", [P, 2, NS])
        rowsum = sb("rowsum", [P, 2, NS])
        rrec = sb("rrec", [P, 2, NS])

        ps = ctx.enter_context(nc.psum_tensor("ps", [P, 8, HALF], F32))
        bx = ps[:, 0:2, :].rearrange("p a b -> p (a b)")
        bh = ps[:, 2, 0:RA]
        bz = ps[:, 2, 0:QL]
        bkv = ps[:, 3, 0:L + RO]
        bt = ps[:, 4, :]
        bhw = ps[:, 7, 0:P]
        bkk = ps[:, 7, P:2 * P]

        def bout(half):
            return ps[:, 5 + half, :]

        def bank_s(i):
            return ps[:, i % 2, :]

        def bank_t(i):
            return ps[:, 2 + i % 2, :]
        bank_pv = ps[:, 4, :]
        bank_q = ps[:, 5, :]

        def bank_y(j):
            return ps[:, 6 + j % 2, :]

        consts_in = sem("consts_in")
        consts_ready = sem("consts_ready")
        vec_const = sem("vec_const")
        half_ready = sem("half_ready")
        settled = sem("settled")
        phase_end = sem("phase_end")
        fw_in = sem("fw_in")
        wl_in = sem("wl_in")
        wl_hi = sem("wl_hi")
        wl_lo = sem("wl_lo")
        pool_chain = sem("pool_chain")
        h_read = sem("h_read")
        gates_ready = sem("gates_ready")
        z_read = sem("z_read")
        fw_hi = sem("fw_hi")
        fw_lo = sem("fw_lo")
        x_in = sem("x_in")
        ln_chain = sem("ln_chain")
        ln_rstd = sem("ln_rstd")
        xn_ready = sem("xn_ready")
        xt_done = sem("xt_done")
        xt_hi = sem("xt_hi")
        xt_lo = sem("xt_lo")
        h_done = sem("h_done")
        gate_chain = sem("gate_chain")
        gate_exp = sem("gate_exp")
        hw_ready = sem("hw_ready")
        hwt_done = sem("hwt_done")
        hwt_hi = sem("hwt_hi")
        hwt_lo = sem("hwt_lo")
        ffn_done = sem("ffn_done")
        ffn_added = sem("ffn_added")
        stored = sem("stored")
        zk_done = sem("zk_done")
        ssq_ready = sem("ssq_ready")
        rms_chain = sem("rms_chain")
        rms_ready = sem("rms_ready")
        tok_chain = sem("tok_chain")
        zck_ready = sem("zck_ready")
        zckt_done = sem("zckt_done")
        lat_hi = sem("lat_hi")
        lat_lo = sem("lat_lo")
        wq_in = sem("wq_in")
        wo_in = sem("wo_in")
        wpe_hi = sem("wpe_hi")
        wpe_lo = sem("wpe_lo")
        scores_done = sem("scores_done")
        max_ready = sem("max_ready")
        exp_done = sem("exp_done")
        rec_ready = sem("rec_ready")
        prob_ready = sem("prob_ready")
        pt_done = sem("pt_done")
        pt_hi = sem("pt_hi")
        pt_lo = sem("pt_lo")
        q_full = sem("q_full")
        q_act = sem("q_act")
        q_dve = sem("q_dve")
        swap_in = sem("swap_in")
        rope_chain = sem("rope_chain")
        rope_ready = sem("rope_ready")
        qst_in = sem("qst_in")
        pv_done = sem("pv_done")
        o_hi = sem("o_hi")
        o_lo = sem("o_lo")
        y_done = sem("y_done")
        y_added = sem("y_added")
        m_done = sem("m_done")
        m_hi = sem("m_hi")
        m_lo = sem("m_lo")

        block = ctx.enter_context(nc.Block())
        NLN = 3 * NT
        NF = 2 * NT
        GATE_STEPS = 13

        def ln_n(p, u):
            return p * NLN + u

        def ffn_n(p, f):
            return p * NF + f

        def lat_n(p, t):
            return p * NT + t

        def slot_n(p, g, k):
            return (p * NG + g) * 4 + k

        def phases(eng, p, n, engine_count=5):
            eng.wait_ge(phase_end, (p * 3 + n + 1) * engine_count)
            settle(eng)

        def settle(eng):
            eng.sem_inc(settled, 1)

        def starts(n):
            return isinstance(n, int) and n == 0

        def end_phase(eng):
            eng.drain().then_inc(phase_end, 1)

        def q_events(last):
            seq = [("q1", 1), ("pe1", 0), ("q2", 1), ("w0", 1), ("q3", 1), ("pe0", 0), ("q0", 1), ("w1", 1)]
            if last:
                seq = [s for s in seq if s[0] in ("q1", "pe1", "q2", "q3")]
            found, a, d = {}, 0, 0
            for name, dve in seq:
                found[name] = (a, d)
                a, d = a + 1, d + dve
            return found
        PRO = {"w0": (-4, -3), "pe0": (-3, -2), "q0": (-2, -2), "w1": (-1, -1)}

        def qbase(p, g):
            return p * EV * NG + EV * g + 4

        def qbase_d(p, g):
            return p * EVD * NG + EVD * g + 3

        FIRST_FILL = ["q1", "q2", "q3", "q0"]
        LAST_FILL = ["pe1", "w0", "pe0", "w1"]

        def y_slot(g, k):
            return [(0, 2), (1, 0), (1, 2), (0, 0)][k]

        def y_n(p, g, k):
            return p * 16 * NG + 16 * g + 4 * k - 12

        @block.sync
        def _(sp):
            end_phase(sp)
            sp.dma_start(ident[:, :], c_ident).then_inc(consts_in, 16)
            sp.dma_start(mask_f[:, :], c_mask).then_inc(consts_in, 16)
            sp.dma_start(tri[:, :, :], c_tri).then_inc(consts_in, 16)
            for b in range(2):
                sp.dma_start(tok_tab[:, b * NS:(b + 1) * NS, :, :],
                             c_tok.rearrange("p (n r) w -> p n r w", n=NS)).then_inc(consts_in, 16)
            sp.dma_start(pos_tab[:, :, :], c_pos).then_inc(consts_in, 16)
            sp.dma_start(qn_bc[:, :], qnorm.partition_broadcast(P)).then_inc(consts_in, 16)
            sp.dma_start(kvn_bc[:, :], kvnorm.partition_broadcast(P)).then_inc(consts_in, 16)
            sp.dma_start(rb_bc[:, :], rb.partition_broadcast(P)).then_inc(consts_in, 16)

            def load_ffn():
                sp.dma_start(s_ra, ra.rearrange("(k p) n -> p k n", p=P)).then_inc(fw_in, 16)
                sp.dma_start(s_bm, bm).then_inc(fw_in, 16)

            def load_wq(g):
                sp.dma_start(s_wqn, wqn[bass.ds(2 * g, 2)].rearrange("h p n -> p h n")).then_inc(wq_in, 16)
                sp.dma_start(s_wk, wk[bass.ds(2 * g, 2)].rearrange("h p n -> p h n")).then_inc(wq_in, 16)
                sp.dma_start(s_wpe, wpe[bass.ds(g, 1)].rearrange("a (k p) n -> p (a k) n", p=P)).then_inc(wq_in, 16)

            def load_wo(g):
                sp.dma_start(s_wv, wv[bass.ds(2 * g, 2)].rearrange("h p n -> p h n")).then_inc(wo_in, 16)
                sp.dma_start(s_wo, wo[bass.ds(2 * g, 2)].rearrange("h p n -> p h n")).then_inc(wo_in, 16)

            def body(p, g, first=False, last=False):
                ev = q_events(last)
                if not first:
                    sp.wait_ge(m_done, 4 * (p * NG + g))
                    settle(sp)
                load_wo(g)
                sp.wait_ge(wo_in, 32 * (p * NG + g + 1))
                settle(sp)
                if not last:
                    sp.wait_ge(q_full, qbase(p, g))
                    settle(sp)
                    sp.wait_ge(wpe_hi, p * NG + g + 1)
                    settle(sp)
                    sp.wait_ge(wpe_lo, p * NG + g + 1)
                    settle(sp)
                    load_wq(g + 1)
                    sp.wait_ge(wq_in, 48 * (p * NG + g + 2))
                    settle(sp)
                n = p * 2 * NG + 2 * g
                sp.wait_ge(q_act, qbase(p, g) + ev["pe1"][0] + 1)
                settle(sp)
                rotary(n + 1, 1, None if first else 4 * slot_n(p, g, 0))
                if not last:
                    sp.wait_ge(q_act, qbase(p, g) + ev["pe0"][0] + 1)
                    settle(sp)
                    rotary(n + 2, 0, 4 * slot_n(p, g, 2))

            def rotary(n, b, used):
                for q in range(4):
                    o = q ^ 1
                    sp.dma_start(rope_f[32 * q:32 * q + 32, 1, :], rope_f[32 * o:32 * o + 32, 0, :])\
                      .then_inc(swap_in, 16)
                sp.wait_ge(rope_ready, n + 1)
                settle(sp)
                if used is not None:
                    sp.wait_ge(scores_done, used)
                    settle(sp)
                for h in range(2):
                    for part in range(2):
                        dst = 64 * (part ^ h)
                        sp.dma_start(qst[dst:dst + 64, b, h, :].bitcast(F32),
                                     rope_r[64 * h:64 * h + 64, part, :].bitcast(F32)).then_inc(qst_in, 16)
                sp.wait_ge(qst_in, 64 * (n + 1))
                settle(sp)

            with sp.Fori(0, NPAIR) as p:
                phases(sp, p, 0)
                def load_x(j):
                    sp.dma_start(xacc[:, bass.ds(2 * j, 2), :],
                                 xt[bass.ds(p * NT + 2 * j, 2)].rearrange("a p d -> p a d")).then_inc(x_in, 16)

                def load_lat(j):
                    sp.dma_start(s_lat, wzkv.rearrange("(k p) n -> p k n", p=P)[:, bass.ds(2 * j, 2), :])\
                      .then_inc(wl_in, 16)
                load_x(0)
                load_ffn()
                load_lat(0)
                sp.wait_ge(x_in, 16 * (p * (NT // 2) + 1))
                settle(sp)
                sp.wait_ge(wl_in, 16 * (p * (NT // 2) + 1))
                settle(sp)
                with sp.Fori(1, NT // 2) as j:
                    load_x(j)
                    sp.wait_ge(wl_hi, p * KD + 2 * j)
                    settle(sp)
                    sp.wait_ge(wl_lo, p * KD + 2 * j)
                    settle(sp)
                    load_lat(j)
                    sp.wait_ge(x_in, 16 * (p * (NT // 2) + j + 1))
                    settle(sp)
                    sp.wait_ge(wl_in, 16 * (p * (NT // 2) + j + 1))
                    settle(sp)
                end_phase(sp)
                phases(sp, p, 1)
                load_wq(0)
                sp.wait_ge(wq_in, 48 * (p * NG + 1))
                settle(sp)
                sp.wait_ge(q_act, qbase(p, 0) - 2)
                settle(sp)
                rotary(p * 2 * NG, 0, None)
                body(p, 0, first=True)
                with sp.Fori(1, NG - 1) as g:
                    body(p, g)
                body(p, NG - 1, last=True)
                end_phase(sp)
                phases(sp, p, 2)
                load_ffn()
                with sp.Fori(0, NT) as t:
                    sp.wait_ge(ffn_added, 2 * ffn_n(p, NT + t + 1))
                    settle(sp)
                    sp.dma_start(outt[bass.ds(p * NT + t, 1)].rearrange("a p d -> p a d"),
                                 xacc[:, bass.ds(t, 1), :]).then_inc(stored, 16)
                sp.wait_ge(stored, 16 * NT * (p + 1))
                settle(sp)
                end_phase(sp)

        @block.tensor
        def _(pe):
            def products(dst, passes, start=True, stop=True, skip=False):
                for n, (w, m) in enumerate(passes):
                    last = nc.tensor.matmul(dst, w, m, start=start and n == 0,
                                            stop=stop and n == len(passes) - 1, skip_group_check=skip)
                return last

            def three(w_hi, w_lo, m_hi_, m_lo_):
                return [(w_hi, m_hi_), (w_hi, m_lo_), (w_lo, m_hi_)]

            def turn_x(p, u, t, buf):
                pe.wait_ge(xn_ready, ln_n(p, u + t) + 1)
                if not starts(u + t):
                    pe.wait_ge(xt_hi, ln_n(p, u + t))
                    pe.wait_ge(xt_lo, ln_n(p, u + t))
                for k in range(KD):
                    last = nc.tensor.transpose(bx[:, k * P:(k + 1) * P], xn[:, buf, k * P:(k + 1) * P], ident[:, :])
                last.then_inc(xt_done, 1)

            def ffn_up(p, u, f, t, buf):
                pe.wait_ge(xt_hi, ln_n(p, u + t) + 1)
                pe.wait_ge(xt_lo, ln_n(p, u + t) + 1)
                if not starts(f + t):
                    pe.wait_ge(h_read, ffn_n(p, f + t))
                passes = []
                for k in range(KD):
                    passes += three(xnT[:, buf, 0, k * P:(k + 1) * P], xnT[:, buf, 1, k * P:(k + 1) * P],
                                    w_ra[:, 0, k, :], w_ra[:, 1, k, :])
                products(bh, passes).then_inc(h_done, 1)

            def turn_h(p, f, t):
                pe.wait_ge(hw_ready, ffn_n(p, f + t) + 1)
                if not starts(f + t):
                    pe.wait_ge(hwt_hi, ffn_n(p, f + t))
                    pe.wait_ge(hwt_lo, ffn_n(p, f + t))
                nc.tensor.transpose(bhw, hw[:, :], ident[:, :]).then_inc(hwt_done, 1)

            def ffn_down(p, f, t, buf):
                pe.wait_ge(hwt_hi, ffn_n(p, f + t) + 1)
                pe.wait_ge(hwt_lo, ffn_n(p, f + t) + 1)
                for n in range(2):
                    if not starts(f + t):
                        pe.wait_ge(ffn_added, 2 * ffn_n(p, f + t) - 1 + n)
                    s = slice(n * HALF, (n + 1) * HALF)
                    products(bout(n), three(hwT[:, buf, 0, :], hwT[:, buf, 1, :], w_bm[:, 0, s], w_bm[:, 1, s]))\
                        .then_inc(ffn_done, 1)

            def latents(p, t, buf):
                u = NT
                pe.wait_ge(xt_hi, ln_n(p, u + t) + 1)
                pe.wait_ge(xt_lo, ln_n(p, u + t) + 1)
                if not starts(t):
                    pe.wait_ge(z_read, 2 * lat_n(p, t))
                for k in range(KD):
                    for n, (xp, wp) in enumerate(((0, 0), (0, 1), (1, 0))):
                        for dst, c in ((bz, slice(0, QL)), (bkv, slice(QL, ZK))):
                            last = nc.tensor.matmul(dst, xnT[:, buf, xp, k * P:(k + 1) * P], w_lat[:, wp, k, c],
                                                    start=(k == 0 and n == 0), stop=(k == KD - 1 and n == 2))
                last.then_inc(zk_done, 1)

            def turn_latents(p, t, half):
                if half == 0:
                    pe.wait_ge(zck_ready, lat_n(p, t) + 2)
                    for n in range(4):
                        nc.tensor.transpose(bt[:, n * P:(n + 1) * P], zck[:, n * P:(n + 1) * P], ident[:, :])
                else:
                    nc.tensor.transpose(bkk, zck[:, 4 * P:5 * P], ident[:, :]).then_inc(zckt_done, 1)

            def norm_and_up(p, u, f):
                turn_x(p, u, 0, 0)
                with pe.Fori(0, NT // 2 - 1) as j:
                    turn_x(p, u, 2 * j + 1, 1)
                    up_even(p, u, f, j)
                    turn_x(p, u, 2 * j + 2, 0)
                    ffn_up(p, u, f, 2 * j + 1, 1)
                turn_x(p, u, NT - 1, 1)
                ffn_up(p, u, f, NT - 2, 0)
                ffn_up(p, u, f, NT - 1, 1)

            def up_even(p, u, f, j):
                ffn_up(p, u, f, 2 * j, 0)

            def tile_step(p, t, buf, has=(True, True, True)):
                one, two, back = has
                latents(p, t, buf)
                if one:
                    turn_x(p, NT, t + 1, 1 - buf)
                if two or back:
                    pe.wait_ge(lat_hi, 4 * lat_n(p, t - 1) + 1) if back else None
                    pe.wait_ge(lat_lo, 4 * lat_n(p, t - 1) + 1) if back else None
                if two:
                    turn_h(p, 0, t + 2)
                if back:
                    turn_latents(p, t - 1, 0)
                    if two:
                        pe.wait_ge(hwt_hi, ffn_n(p, t + 2) + 1)
                        pe.wait_ge(hwt_lo, ffn_n(p, t + 2) + 1)
                    turn_latents(p, t - 1, 1)
                if two:
                    ffn_down(p, 0, t + 2, buf)

            def q_free(p, g, a, d):
                pe.wait_ge(q_act, qbase(p, g) + a)
                pe.wait_ge(q_dve, qbase_d(p, g) + d)

            def fill(p, g, name, ev):
                a, d = ev[name]
                if not (ev is PRO and name == "w0"):
                    q_free(p, g, a, d)
                if name[0] == "q":
                    k = int(name[1])
                    h, b = k % 2, k // 2
                    s = slice(b * SEQ, (b + 1) * SEQ)
                    passes = []
                    for c in range(KQ):
                        cs = slice(c * P, (c + 1) * P)
                        passes += three(w_q[:, h, 0, cs], w_q[:, h, 1, cs], zT[:, 0, c, s], zT[:, 1, c, s])
                    products(bank_q, passes).then_inc(q_full, 1)
                elif name[:2] == "pe":
                    b = int(name[2])
                    n = p * NG + g + (1 if ev is PRO or name == "pe1" else 2)
                    pe.wait_ge(wpe_hi, n)
                    pe.wait_ge(wpe_lo, n)
                    s = slice(b * SEQ, (b + 1) * SEQ)
                    passes = []
                    for c in range(KQ):
                        cs = slice(c * P, (c + 1) * P)
                        passes += three(w_pe[:, 0, cs], w_pe[:, 1, cs], zT[:, 0, c, s], zT[:, 1, c, s])
                    products(bank_q, passes).then_inc(q_full, 1)
                else:
                    h = int(name[1])
                    pe.wait_ge(wq_in, 48 * (p * NG + g + (1 if ev is PRO else 2)))
                    for c in range(KQ):
                        last = nc.tensor.matmul(bank_q[:, c * P:(c + 1) * P], s_wqn[:, h, c * P:(c + 1) * P],
                                                s_wk[:, h, :], start=True, stop=True)
                    last.then_inc(q_full, 1)

            def scores(p, g, k, i, first, last):
                h, b = k % 2, k // 2
                n = slot_n(p, g, k)
                if i == 0:
                    a, d = q_events(last)[f"q{k}"] if k else (-2, -2)
                    pe.wait_ge(q_act, qbase(p, g) + a + 1)
                    pe.wait_ge(q_dve, qbase_d(p, g) + d + 1)
                    if h == 0:
                        pe.wait_ge(qst_in, 64 * (p * 2 * NG + 2 * g + b + 1))
                if not (first and k == 0 and i < 2):
                    pe.wait_ge(exp_done, 4 * n + i - 1)
                qs = slice(i * P, (i + 1) * P)
                ks = slice(b * SEQ, b * SEQ + (i + 1) * P)
                dst = bank_s(i)[:, 0:(i + 1) * P]
                products(dst, three(qT[:, h, 0, qs], qT[:, h, 1, qs], keyT[:, 0, ks], keyT[:, 1, ks])
                         + [(qst[:, b, h, qs], ropeT[:, 0, ks]), (qst[:, b, h, qs], ropeT[:, 1, ks])], stop=False)
                nc.tensor.matmul(dst[:, i * P:(i + 1) * P], ident_r[:, :], mask_r[:, :],
                                 start=False, stop=True).then_inc(scores_done, 1)

            def turn_probs(n, k, i, first):
                pe.wait_ge(prob_ready, 4 * n + i + 1)
                if not (first and i < 2):
                    pe.wait_ge(pt_hi, 4 * n + i - 1)
                    pe.wait_ge(pt_lo, 4 * n + i - 1)
                for j in range(i + 1):
                    last = nc.tensor.transpose(bank_t(i)[:, j * P:(j + 1) * P],
                                               prob[:, k % 2, poff(i) + j * P:poff(i) + (j + 1) * P], ident[:, :])
                last.then_inc(pt_done, 1)

            def values(n, k, first):
                b = k // 2
                pe.wait_ge(pt_hi, 4 * n + 4)
                pe.wait_ge(pt_lo, 4 * n + 4)
                if not first:
                    pe.wait_ge(o_hi, n)
                    pe.wait_ge(o_lo, n)
                for j in range(NS):
                    t = b * NS + j
                    s = slice(j * P, SEQ)
                    last = products(bank_pv[:, s], three(lat[:, 0, t, :], lat[:, 1, t, :], pT[:, 0, j, s], pT[:, 1, j, s]),
                                    start=(j == 0), stop=(j == NS - 1))
                last.then_inc(pv_done, 1)

            def output(p, g, k, j, first):
                b, t0 = y_slot(g, k)
                tt, half = t0 + j // 2, j % 2
                n = y_n(p, g, k) + j
                if j == 0 and k == 3:
                    pe.wait_ge(m_hi, 4 * (p * NG + g + 1))
                    pe.wait_ge(m_lo, 4 * (p * NG + g + 1))
                if j == 0 and k % 2 == 1:
                    pe.wait_ge(o_hi, slot_n(p, g, k) - 1)
                    pe.wait_ge(o_lo, slot_n(p, g, k) - 1)
                if not (first and j < 2):
                    pe.wait_ge(y_added, n - 1)
                ts = slice(tt * P, (tt + 1) * P)
                hs = slice(half * HALF, (half + 1) * HALF)
                passes = []
                for h in range(2):
                    passes += three(oT[:, b, h, 0, ts], oT[:, b, h, 1, ts], w_out[:, h, 0, hs], w_out[:, h, 1, hs])
                products(bank_y(j), passes).then_inc(y_done, 1)

            def out_weights(p, g, first):
                pe.wait_ge(wo_in, 32 * (p * NG + g + 1))
                if not first:
                    pe.wait_ge(y_added, y_n(p, g, 3))
                for j in range(4):
                    h, half = j // 2, j % 2
                    if j >= 2:
                        pe.wait_ge(m_hi, 4 * (p * NG + g) + j - 1)
                        pe.wait_ge(m_lo, 4 * (p * NG + g) + j - 1)
                    nc.tensor.matmul(bank_y(j), s_wv[:, h, :], s_wo[:, h, half * HALF:(half + 1) * HALF],
                                     start=True, stop=True).then_inc(m_done, 1)

            def slot(p, g, k, first=False, last=False, drained=False):
                n, before = slot_n(p, g, k) - 1, (k - 1) % 4
                ev = {} if drained else q_events(last)
                turn = not (first and k == 0) and not (drained and k > 0)
                out_ = not first or k == 3
                if not drained:
                    scores(p, g, k, 0, first, last)
                    scores(p, g, k, 1, first, last)
                if turn:
                    turn_probs(n, before, 0, first and k == 1)
                    turn_probs(n, before, 1, first and k == 1)
                if out_:
                    output(p, g, k, 0, first)
                if not drained:
                    scores(p, g, k, 2, first, last)
                if turn:
                    turn_probs(n, before, 2, False)
                if out_:
                    output(p, g, k, 1, first)
                if not drained:
                    scores(p, g, k, 3, first, last)
                if turn:
                    turn_probs(n, before, 3, False)
                if FIRST_FILL[k] in ev:
                    fill(p, g, FIRST_FILL[k], ev)
                if out_:
                    output(p, g, k, 2, first)
                if turn:
                    values(n, before, first and k == 1)
                if LAST_FILL[k] in ev:
                    fill(p, g, LAST_FILL[k], ev)
                if out_:
                    output(p, g, k, 3, first)
                if k == 2 and not drained:
                    out_weights(p, g, first)

            def body(p, g, first=False, last=False):
                for k in range(4):
                    slot(p, g, k, first, last)

            end_phase(pe)
            pe.wait_ge(consts_ready, 2)
            pe.wait_ge(consts_in, 16 * 9)
            with pe.Fori(0, NPAIR) as p:
                phases(pe, p, 0)
                pe.wait_ge(fw_hi, p * 4 + 2)
                pe.wait_ge(fw_lo, p * 4 + 2)
                norm_and_up(p, 0, 0)
                turn_h(p, 0, 0)
                ffn_down(p, 0, 0, 0)
                turn_h(p, 0, 1)
                ffn_down(p, 0, 1, 1)
                turn_x(p, NT, 0, 0)
                pe.wait_ge(wl_hi, (p + 1) * KD)
                pe.wait_ge(wl_lo, (p + 1) * KD)
                tile_step(p, 0, 0, (True, True, False))
                with pe.Fori(0, NT // 2 - 2) as j:
                    tile_step(p, 2 * j + 1, 1)
                    tile_step(p, 2 * j + 2, 0)
                tile_step(p, NT - 3, 1)
                tile_step(p, NT - 2, 0, (True, False, True))
                tile_step(p, NT - 1, 1, (False, False, True))
                pe.wait_ge(lat_hi, 4 * lat_n(p, NT - 1) + 1)
                pe.wait_ge(lat_lo, 4 * lat_n(p, NT - 1) + 1)
                turn_latents(p, NT - 1, 0)
                turn_latents(p, NT - 1, 1)
                end_phase(pe)
                phases(pe, p, 1)
                for name in ("w0", "pe0", "q0", "w1"):
                    fill(p, 0, name, PRO)
                body(p, 0, first=True)
                with pe.Fori(1, NG - 1) as g:
                    body(p, g)
                body(p, NG - 1, last=True)
                for k in range(3):
                    slot(p, NG, k, drained=True)
                end_phase(pe)
                phases(pe, p, 2)
                pe.wait_ge(fw_hi, p * 4 + 4)
                pe.wait_ge(fw_lo, p * 4 + 4)
                norm_and_up(p, 2 * NT, NT)
                turn_h(p, NT, 0)
                with pe.Fori(0, NT // 2 - 1) as j:
                    turn_h(p, NT, 2 * j + 1)
                    ffn_down(p, NT, 2 * j, 0)
                    turn_h(p, NT, 2 * j + 2)
                    ffn_down(p, NT, 2 * j + 1, 1)
                turn_h(p, NT, NT - 1)
                ffn_down(p, NT, NT - 2, 0)
                ffn_down(p, NT, NT - 1, 1)
                end_phase(pe)

        @block.scalar
        def _(act):
            def hi(dst, src):
                return nc.scalar.activation(dst, src, ACT.Copy)

            def normalise(p, u, t, buf):
                act.wait_ge(ln_rstd, ln_n(p, u + t) + 1)
                if not starts(u + t) and not (isinstance(t, int) and u + t == 1):
                    act.wait_ge(xt_done, ln_n(p, u + t) - 1)
                one = bass.ds(t, 1)
                nc.scalar.activation(xn[:, buf, :], xacc[:, one, :].rearrange("p a d -> p (a d)"), ACT.Identity,
                                     bias=mom[:, one, 3:4].rearrange("p a b -> p (a b)"),
                                     scale=mom[:, one, 2:3].rearrange("p a b -> p (a b)")).then_inc(xn_ready, 1)

            def turned_x(p, u, t, buf):
                act.wait_ge(xt_done, ln_n(p, u + t) + 1)
                hi(xnT[:, buf, 0, :], bx).then_inc(xt_hi, 1)

            def keep_h(p, f, t):
                act.wait_ge(h_done, ffn_n(p, f + t) + 1)
                hi(hb[:, bass.ds(t, 1), :].rearrange("p a n -> p (a n)"), bh).then_inc(h_read, 1)

            def lat_weights(p, k, buf):
                act.wait_ge(wl_in, 16 * (p * (NT // 2)) + 8 * (k - buf) + 16)
                hi(w_lat[:, 0, bass.ds(k, 1), :].rearrange("p a n -> p (a n)"), s_lat[:, buf, :]).then_inc(wl_hi, 1)

            def norm_and_up(p, u, f, weights):
                normalise(p, u, 0, 0)
                normalise(p, u, 1, 1)
                turned_x(p, u, 0, 0)
                with act.Fori(0, NT // 2 - 1) as j:
                    if weights:
                        lat_weights(p, 2 * j, 0)
                    normalise(p, u, 2 * j + 2, 0)
                    turned_x(p, u, 2 * j + 1, 1)
                    keep_h(p, f, 2 * j)
                    if weights:
                        lat_weights(p, 2 * j + 1, 1)
                    normalise(p, u, 2 * j + 3, 1)
                    turned_x(p, u, 2 * j + 2, 0)
                    keep_h(p, f, 2 * j + 1)
                turned_x(p, u, NT - 1, 1)
                keep_h(p, f, NT - 2)
                if weights:
                    lat_weights(p, NT - 2, 0)
                    lat_weights(p, NT - 1, 1)
                keep_h(p, f, NT - 1)

            def gates(p, n):
                act.wait_ge(gate_chain, (2 * p + n) * GATE_STEPS + 3)
                nc.scalar.activation(lgt[:, 1], lgt[:, 0], ACT.Exp).then_inc(gate_exp, 1)

            def turned_h(p, f, t, buf):
                act.wait_ge(hwt_done, ffn_n(p, f + t) + 1)
                hi(hwT[:, buf, 0, :], bhw).then_inc(hwt_hi, 1)

            def keep_latents(p, t):
                act.wait_ge(zk_done, lat_n(p, t) + 1)
                act.wait_ge(zck_ready, lat_n(p, t) + 1)
                hi(zr[:, 0:QL], bz).then_inc(z_read, 1)
                hi(zr[:, QL:ZK], bkv).then_inc(z_read, 1)
                act.wait_ge(rms_ready, lat_n(p, t) + 1)
                act.wait_ge(z_read, 2 * lat_n(p, t) + 1)
                nc.scalar.activation(junk[:, 0:QL], zr[:, 0:QL], ACT.Square, scale=float(QL ** -0.5),
                                     accum_out=ssq[:, 0, 0:1]).then_inc(ssq_ready, 1)
                act.wait_ge(z_read, 2 * lat_n(p, t) + 2)
                act.wait_ge(ssq_ready, 2 * lat_n(p, t) + 1)
                nc.scalar.activation(junk[:, 0:L], zr[:, QL:QL + L], ACT.Square, scale=float(L ** -0.5),
                                     accum_out=ssq[:, 0, 1:2]).then_inc(ssq_ready, 1)

            def latents(p, t):
                act.wait_ge(zckt_done, lat_n(p, t) + 1)
                ts = bass.ds(t * P, P)
                hi(lat[:, 0, bass.ds(t, 1), :].rearrange("p a l -> p (a l)"), zck[:, QL:QL + L]).then_inc(lat_hi, 1)
                hi(zT[:, 0, :, ts], bt[:, 0:QL].rearrange("p (k t) -> p k t", k=KQ)).then_inc(lat_hi, 1)
                hi(keyT[:, 0, ts], bt[:, QL:QL + P]).then_inc(lat_hi, 1)
                hi(ropeT[:, 0, ts], bkk).then_inc(lat_hi, 1)

            def tile_step(p, t, buf, has=(True, True, True)):
                one, two, back = has
                if back:
                    keep_latents(p, t - 1)
                if one:
                    normalise(p, NT, t + 1, 1 - buf)
                    turned_x(p, NT, t + 1, 1 - buf)
                if two:
                    turned_h(p, 0, t + 2, buf)
                if back:
                    latents(p, t - 1)

            def read_fill(p, g, name, ev):
                a, d = ev[name]
                act.wait_ge(q_full, qbase(p, g) + a + 1)
                if name[0] == "q":
                    dst = qT[:, int(name[1]) % 2, 0, :]
                    src = bank_q
                elif name[:2] == "pe":
                    if ev is not PRO:
                        act.wait_ge(rope_ready, p * 2 * NG + 2 * g + (1 if name == "pe1" else 2))
                    dst, src = rope_f[:, 0, :], bank_q
                else:
                    dst, src = w_q[:, int(name[1]), 0, :], bank_q[:, 0:QL]
                hi(dst, src).then_inc(q_act, 1)

            def exps(p, g, k, i):
                n = slot_n(p, g, k)
                act.wait_ge(max_ready, 4 * n + i + 1)
                nc.scalar.activation(prob[:, k % 2, poff(i):poff(i + 1)], bank_s(i)[:, 0:(i + 1) * P], ACT.Exp,
                                     bias=negmax[:, k % 2, i:i + 1],
                                     accum_out=rowsum[:, k % 2, i:i + 1]).then_inc(exp_done, 1)

            def turned(n, i):
                act.wait_ge(pt_done, 4 * n + i + 1)
                hi(pT[:, 0, 0:i + 1, i * P:(i + 1) * P],
                   bank_t(i)[:, 0:(i + 1) * P].rearrange("p (j s) -> p j s", s=P)).then_inc(pt_hi, 1)

            def valued(n, k):
                act.wait_ge(pv_done, n + 1)
                hi(oT[:, k // 2, k % 2, 0, :], bank_pv).then_inc(o_hi, 1)

            def split_wpe(p, g):
                act.wait_ge(wq_in, 48 * (p * NG + g + 1))
                hi(w_pe[:, 0, :], s_wpe.rearrange("p k n -> p (k n)")).then_inc(wpe_hi, 1)

            def body(p, g, first=False, last=False):
                ev = q_events(last)
                for k in range(4):
                    n, before = slot_n(p, g, k) - 1, (k - 1) % 4
                    turn = not (first and k == 0)
                    exps(p, g, k, 0)
                    exps(p, g, k, 1)
                    if turn:
                        turned(n, 0)
                        turned(n, 1)
                    exps(p, g, k, 2)
                    if turn:
                        turned(n, 2)
                    exps(p, g, k, 3)
                    if turn:
                        turned(n, 3)
                    if FIRST_FILL[k] in ev:
                        read_fill(p, g, FIRST_FILL[k], ev)
                    if k == 1 and not last:
                        split_wpe(p, g + 1)
                    if turn:
                        valued(n, before)
                    if LAST_FILL[k] in ev:
                        read_fill(p, g, LAST_FILL[k], ev)
                    if k == 2:
                        for j in range(4):
                            act.wait_ge(m_done, 4 * (p * NG + g) + j + 1)
                            hi(w_out[:, j // 2, 0, (j % 2) * HALF:(j % 2 + 1) * HALF], bank_y(j)).then_inc(m_hi, 1)

            end_phase(act)
            act.sem_inc(lat_hi, 1)
            act.wait_ge(consts_in, 16 * 9)
            hi(ident_r[:, :], ident[:, :]).then_inc(consts_ready, 1)
            hi(mask_r[:, :], mask_f[:, :]).then_inc(consts_ready, 1)
            with act.Fori(0, NPAIR) as p:
                phases(act, p, 0)
                act.wait_ge(fw_in, 16 * (p * 4 + 2))
                for n, (w, s) in enumerate(((w_ra, s_ra), (w_bm, s_bm))):
                    hi(w[:, 0], s).then_inc(fw_hi, 1)
                norm_and_up(p, 0, 0, True)
                gates(p, 0)
                turned_h(p, 0, 0, 0)
                turned_h(p, 0, 1, 1)
                normalise(p, NT, 0, 0)
                turned_x(p, NT, 0, 0)
                tile_step(p, 0, 0, (True, True, False))
                with act.Fori(0, NT // 2 - 2) as j:
                    tile_step(p, 2 * j + 1, 1)
                    tile_step(p, 2 * j + 2, 0)
                tile_step(p, NT - 3, 1)
                tile_step(p, NT - 2, 0, (True, False, True))
                tile_step(p, NT - 1, 1, (False, False, True))
                keep_latents(p, NT - 1)
                latents(p, NT - 1)
                end_phase(act)
                phases(act, p, 1)
                split_wpe(p, 0)
                for name in ("w0", "pe0", "q0", "w1"):
                    read_fill(p, 0, name, PRO)
                body(p, 0, first=True)
                with act.Fori(1, NG - 1) as g:
                    body(p, g)
                body(p, NG - 1, last=True)
                for i in range(NS):
                    turned(slot_n(p, NG, 0) - 1, i)
                valued(slot_n(p, NG, 0) - 1, 3)
                end_phase(act)
                phases(act, p, 2)
                act.wait_ge(fw_in, 16 * (p * 4 + 4))
                for n, (w, s) in enumerate(((w_ra, s_ra), (w_bm, s_bm))):
                    hi(w[:, 0], s).then_inc(fw_hi, 1)
                norm_and_up(p, 2 * NT, NT, False)
                gates(p, 1)
                with act.Fori(0, NT // 2) as j:
                    turned_h(p, NT, 2 * j, 0)
                    turned_h(p, NT, 2 * j + 1, 1)
                end_phase(act)

        @block.vector
        def _(dve):
            def lo(dst, src, part):
                return nc.vector.tensor_tensor(dst, src, part.bitcast(F32), ALU.subtract)

            def moments(p, u, t, loaded=None, added=None):
                if loaded is not None:
                    dve.wait_ge(x_in, loaded)
                    settle(dve)
                if added is not None:
                    dve.wait_ge(ffn_added, added)
                    settle(dve)
                one = bass.ds(t, 1)
                xs = xacc[:, one, :].rearrange("p a d -> p (a d)")

                def m(a, b):
                    return mom[:, one, a:b].rearrange("p a b -> p (a b)")
                base = ln_n(p, u + t) * 5
                for n in range(2):
                    nc.vector.bn_stats(stats[:, n, :], xs[:, n * HALF:(n + 1) * HALF]).then_inc(ln_chain, 1)
                dve.wait_ge(ln_chain, base + 2)
                settle(dve)
                nc.vector.bn_aggr(mv[:, :], stats[:, :, :]).then_inc(ln_chain, 1)
                dve.wait_ge(ln_chain, base + 3)
                nc.vector.tensor_scalar_add(m(0, 1), mv[:, 1:2], LN_EPS).then_inc(ln_chain, 1)
                nc.vector.tensor_scalar(m(1, 2), mv[:, 0:1], -1.0, None, ALU.mult).then_inc(ln_chain, 1)

            def turned_x(p, u, t, buf):
                dve.wait_ge(xt_hi, ln_n(p, u + t) + 1)
                lo(xnT[:, buf, 1, :], bx, xnT[:, buf, 0, :]).then_inc(xt_lo, 1)

            def norm_and_up(p, u, load):
                def tile(t, pair):
                    moments(p, u, t, loaded=16 * (p * (NT // 2) + pair + 1) if load else None)
                tile(0, 0)
                tile(1, 0)
                with dve.Fori(0, NT // 2 - 1) as j:
                    tile(2 * j + 2, j + 1)
                    turned_x(p, u, 2 * j, 0)
                    tile(2 * j + 3, j + 1)
                    turned_x(p, u, 2 * j + 1, 1)
                turned_x(p, u, NT - 2, 0)
                turned_x(p, u, NT - 1, 1)

            def gates(p, n, f):
                base = (2 * p + n) * GATE_STEPS
                step = [0]

                def link(ins):
                    step[0] += 1
                    ins.then_inc(gate_chain, 1)
                    dve.wait_ge(gate_chain, base + step[0])
                V = nc.vector
                dve.wait_ge(h_read, ffn_n(p, f + NT))

                def wide(ap, k):
                    return ap.rearrange("p t (e a) -> p t e a", a=1).to_broadcast([P, NT, E, k])
                per_tile = [gsc[:, i, :].rearrange("p (t a) -> p t a", a=1).to_broadcast([P, NT, E]) for i in range(3)]
                ex = lgt[:, 1]
                link(V.tensor_tensor(lgt[:, 0], hb[:, :, 0:E],
                                     rb_bc[:, :].rearrange("p (a e) -> p a e", a=1).to_broadcast([P, NT, E]), ALU.add))
                link(V.tensor_reduce(gsc[:, 0, :], lgt[:, 0], AX_X, ALU.max))
                link(V.tensor_tensor(lgt[:, 0], lgt[:, 0], per_tile[0], ALU.subtract))
                dve.wait_ge(gate_exp, 2 * p + n + 1)
                mine = wide(ex, E)
                other = ex.rearrange("p t (a e) -> p t a e", a=1).to_broadcast([P, NT, E, E])
                before = tri[:, :, :].rearrange("p (a e) f -> p a e f", a=1).to_broadcast([P, NT, E, E])
                link(V.tensor_tensor(cmp[:, 0], other, mine, ALU.is_gt))
                link(V.tensor_tensor(cmp[:, 1], other, mine, ALU.is_equal))
                link(V.tensor_tensor(cmp[:, 1], cmp[:, 1], before, ALU.mult))
                link(V.tensor_tensor(cmp[:, 0], cmp[:, 0], cmp[:, 1], ALU.add))
                link(V.tensor_reduce(rank[:, :, :], cmp[:, 0], AX_X, ALU.add))
                link(V.scalar_tensor_tensor(lgt[:, 2], rank[:, :, :], 1.5, ex, ALU.is_lt, ALU.mult))
                link(V.tensor_reduce(gsc[:, 1, :], lgt[:, 2], AX_X, ALU.add))
                link(V.reciprocal(gsc[:, 2, :], gsc[:, 1, :]))
                link(V.tensor_scalar(gsc[:, 2, :], gsc[:, 2, :], FFN_SCALE, None, ALU.mult))
                link(V.tensor_tensor(lgt[:, 2], lgt[:, 2], per_tile[2], ALU.mult))
                assert step[0] == GATE_STEPS

            def gate_h(p, f, t):
                one = bass.ds(t, 1)
                if not starts(f + t):
                    dve.wait_ge(hwt_done, ffn_n(p, f + t))
                w = lgt[:, 2, one, :].rearrange("p t (e a) -> p (t e) a", a=1).to_broadcast([P, E, R])
                nc.vector.tensor_tensor(hw[:, :].rearrange("p (e r) -> p e r", r=R),
                                        hb[:, one, E:RA].rearrange("p t (e r) -> p (t e) r", r=R), w,
                                        ALU.mult).then_inc(hw_ready, 1)

            def turned_h(p, f, t, buf):
                dve.wait_ge(hwt_hi, ffn_n(p, f + t) + 1)
                lo(hwT[:, buf, 1, :], bhw, hwT[:, buf, 0, :]).then_inc(hwt_lo, 1)

            def ffn_add(p, f, t):
                for n in range(2):
                    dve.wait_ge(ffn_done, 2 * ffn_n(p, f + t) + n + 1)
                    xs = xacc[:, bass.ds(t, 1), n * HALF:(n + 1) * HALF].rearrange("p a d -> p (a d)")
                    nc.vector.tensor_tensor(xs, bout(n), xs, ALU.add).then_inc(ffn_added, 1)

            def tokens(p, t):
                V = nc.vector
                dve.wait_ge(z_read, 2 * lat_n(p, t) + 2)
                cs = tok_tab[:, bass.ds(t, 1), 0, :].rearrange("p a w -> p (a w)")
                sn = tok_tab[:, bass.ds(t, 1), 1, :].rearrange("p a w -> p (a w)")
                H = RO // 2
                k0 = QL + L
                V.tensor_tensor(rtmp[:, 0, :], zr[:, k0:ZK], cs, ALU.mult)
                V.tensor_tensor(rtmp[:, 1, 0:H], zr[:, k0 + H:ZK], sn[:, 0:H], ALU.mult)
                V.tensor_tensor(rtmp[:, 1, H:RO], zr[:, k0:k0 + H], sn[:, H:RO], ALU.mult).then_inc(tok_chain, 1)
                dve.wait_ge(lat_lo, 4 * lat_n(p, t) + 1)
                dve.wait_ge(rms_ready, lat_n(p, t) + 2)
                V.scalar_tensor_tensor(zck[:, 0:QL], zr[:, 0:QL], rms[:, 0:1], qn_bc[:, :], ALU.mult, ALU.mult)
                V.scalar_tensor_tensor(zck[:, QL:QL + L], zr[:, QL:QL + L], rms[:, 1:2], kvn_bc[:, :],
                                       ALU.mult, ALU.mult)
                dve.wait_ge(tok_chain, lat_n(p, t) + 1)
                twice = [rtmp[:, n, :].rearrange("p (a w) -> p a w", a=1).to_broadcast([P, 2, RO]) for n in range(2)]
                V.tensor_tensor(zck[:, QL + L:ZK + RO].rearrange("p (a w) -> p a w", a=2),
                                twice[0], twice[1], ALU.add).then_inc(zck_ready, 1)

            def latents(p, t):
                ts = bass.ds(t * P, P)
                n = 4 * lat_n(p, t) + 1
                dve.wait_ge(lat_hi, n + 1)
                one = bass.ds(t, 1)
                lo(lat[:, 1, one, :].rearrange("p a l -> p (a l)"), zck[:, QL:QL + L],
                   lat[:, 0, one, :].rearrange("p a l -> p (a l)")).then_inc(lat_lo, 1)
                dve.wait_ge(lat_hi, n + 3)
                lo(zT[:, 1, :, ts], bt[:, 0:QL].rearrange("p (k t) -> p k t", k=KQ), zT[:, 0, :, ts]).then_inc(lat_lo, 1)
                lo(keyT[:, 1, ts], bt[:, QL:QL + P], keyT[:, 0, ts]).then_inc(lat_lo, 1)
                dve.wait_ge(lat_hi, n + 4)
                lo(ropeT[:, 1, ts], bkk, ropeT[:, 0, ts]).then_inc(lat_lo, 1)

            def tile_step(p, t, buf, has=(True, True, True)):
                one, two, back = has
                if one:
                    moments(p, NT, t + 1, added=2 * ffn_n(p, t + 2))
                if two:
                    gate_h(p, 0, t + 2)
                if back:
                    tokens(p, t - 1)
                if one:
                    turned_x(p, NT, t + 1, 1 - buf)
                if two:
                    turned_h(p, 0, t + 2, buf)
                if back:
                    latents(p, t - 1)
                if two:
                    ffn_add(p, 0, t + 2)

            def read_fill(p, g, name, ev):
                a, d = ev[name]
                if name[:2] == "pe":
                    return
                dve.wait_ge(q_act, qbase(p, g) + a + 1)
                if name[0] == "q":
                    h = int(name[1]) % 2
                    lo(qT[:, h, 1, :], bank_q, qT[:, h, 0, :]).then_inc(q_dve, 1)
                else:
                    h = int(name[1])
                    lo(w_q[:, h, 1, :], bank_q[:, 0:QL], w_q[:, h, 0, :]).then_inc(q_dve, 1)

            def maxima(p, g, k, i):
                n = slot_n(p, g, k)
                dve.wait_ge(scores_done, 4 * n + i + 1)
                nc.vector.tensor_reduce(negmax[:, k % 2, i:i + 1], bank_s(i)[:, 0:(i + 1) * P], AX_X, ALU.max,
                                        negate=True).then_inc(max_ready, 1)

            def norms(p, g, k):
                n = slot_n(p, g, k)
                dve.wait_ge(exp_done, 4 * n + NS)
                nc.vector.reciprocal(rrec[:, k % 2, :], rowsum[:, k % 2, :]).then_inc(rec_ready, 1)
                dve.wait_ge(rec_ready, n + 1)
                for i in range(NS):
                    pr = prob[:, k % 2, poff(i):poff(i + 1)]
                    nc.vector.tensor_scalar(pr, pr, rrec[:, k % 2, i:i + 1], None, ALU.mult).then_inc(prob_ready, 1)

            def pt_split(n, i):
                dve.wait_ge(pt_hi, 4 * n + i + 1)
                ap = [pT[:, part, 0:i + 1, i * P:(i + 1) * P] for part in range(2)]
                lo(ap[1], bank_t(i)[:, 0:(i + 1) * P].rearrange("p (j s) -> p j s", s=P), ap[0]).then_inc(pt_lo, 1)

            def y_add(p, g, k, j):
                b, t0 = y_slot(g, k)
                dve.wait_ge(y_done, y_n(p, g, k) + j + 1)
                xs = xacc[:, b * NS + t0 + j // 2, (j % 2) * HALF:(j % 2 + 1) * HALF]
                nc.vector.tensor_tensor(xs, bank_y(j), xs, ALU.add).then_inc(y_added, 1)

            def o_split(n, k):
                dve.wait_ge(o_hi, n + 1)
                lo(oT[:, k // 2, k % 2, 1, :], bank_pv, oT[:, k // 2, k % 2, 0, :]).then_inc(o_lo, 1)

            def split_wpe(p, g):
                dve.wait_ge(wpe_hi, p * NG + g + 1)
                lo(w_pe[:, 1, :], s_wpe.rearrange("p k n -> p (k n)"), w_pe[:, 0, :]).then_inc(wpe_lo, 1)

            def slot(p, g, k, first=False, last=False, drained=False):
                n, before = slot_n(p, g, k) - 1, (k - 1) % 4
                ev = {} if drained else q_events(last)
                turn = not (first and k == 0) and not (drained and k > 0)
                out_ = not first or k == 3
                if not drained:
                    maxima(p, g, k, 0)
                    maxima(p, g, k, 1)
                if turn:
                    pt_split(n, 0)
                    pt_split(n, 1)
                if out_:
                    y_add(p, g, k, 0)
                if not drained:
                    maxima(p, g, k, 2)
                if turn:
                    pt_split(n, 2)
                if out_:
                    y_add(p, g, k, 1)
                if not drained:
                    maxima(p, g, k, 3)
                if turn:
                    pt_split(n, 3)
                if FIRST_FILL[k] in ev:
                    read_fill(p, g, FIRST_FILL[k], ev)
                if k == 1 and not last and not drained:
                    split_wpe(p, g + 1)
                if out_:
                    y_add(p, g, k, 2)
                if not drained:
                    norms(p, g, k)
                if turn:
                    o_split(n, before)
                if LAST_FILL[k] in ev:
                    read_fill(p, g, LAST_FILL[k], ev)
                if out_:
                    y_add(p, g, k, 3)
                if k == 2 and not drained:
                    for j in range(4):
                        dve.wait_ge(m_hi, 4 * (p * NG + g) + j + 1)
                        s = slice((j % 2) * HALF, (j % 2 + 1) * HALF)
                        lo(w_out[:, j // 2, 1, s], bank_y(j), w_out[:, j // 2, 0, s]).then_inc(m_lo, 1)

            def body(p, g, first=False, last=False):
                for k in range(4):
                    slot(p, g, k, first, last)

            end_phase(dve)
            dve.sem_inc(lat_lo, 1)
            dve.sem_inc(zck_ready, 1)
            dve.wait_ge(consts_in, 16 * 9)
            nc.vector.tensor_scalar(qn_bc[:, :], qn_bc[:, :], QSCALE, None, ALU.mult).then_inc(vec_const, 1)
            dve.wait_ge(vec_const, 1)
            with dve.Fori(0, NPAIR) as p:
                phases(dve, p, 0)
                for n, (w, s) in enumerate(((w_ra, s_ra), (w_bm, s_bm))):
                    dve.wait_ge(fw_hi, p * 4 + n + 1)
                    lo(w[:, 1], s, w[:, 0]).then_inc(fw_lo, 1)
                norm_and_up(p, 0, True)
                gates(p, 0, 0)
                gate_h(p, 0, 0)
                turned_h(p, 0, 0, 0)
                gate_h(p, 0, 1)
                ffn_add(p, 0, 0)
                moments(p, NT, 0, added=2 * ffn_n(p, 1))
                turned_h(p, 0, 1, 1)
                ffn_add(p, 0, 1)
                turned_x(p, NT, 0, 0)
                tile_step(p, 0, 0, (True, True, False))
                with dve.Fori(0, NT // 2 - 2) as j:
                    tile_step(p, 2 * j + 1, 1)
                    tile_step(p, 2 * j + 2, 0)
                tile_step(p, NT - 3, 1)
                tile_step(p, NT - 2, 0, (True, False, True))
                tile_step(p, NT - 1, 1, (False, False, True))
                tokens(p, NT - 1)
                latents(p, NT - 1)
                end_phase(dve)
                phases(dve, p, 1)
                split_wpe(p, 0)
                for name in ("w0", "pe0", "q0", "w1"):
                    read_fill(p, 0, name, PRO)
                body(p, 0, first=True)
                with dve.Fori(1, NG - 1) as g:
                    body(p, g)
                body(p, NG - 1, last=True)
                for k in range(3):
                    slot(p, NG, k, drained=True)
                end_phase(dve)
                phases(dve, p, 2)
                for n, (w, s) in enumerate(((w_ra, s_ra), (w_bm, s_bm))):
                    dve.wait_ge(fw_hi, p * 4 + 2 + n + 1)
                    lo(w[:, 1], s, w[:, 0]).then_inc(fw_lo, 1)
                norm_and_up(p, 2 * NT, False)
                gates(p, 1, NT)
                gate_h(p, NT, 0)
                turned_h(p, NT, 0, 0)
                with dve.Fori(0, NT // 2 - 1) as j:
                    gate_h(p, NT, 2 * j + 1)
                    turned_h(p, NT, 2 * j + 1, 1)
                    ffn_add(p, NT, 2 * j)
                    gate_h(p, NT, 2 * j + 2)
                    turned_h(p, NT, 2 * j + 2, 0)
                    ffn_add(p, NT, 2 * j + 1)
                gate_h(p, NT, NT - 1)
                turned_h(p, NT, NT - 1, 1)
                ffn_add(p, NT, NT - 2)
                ffn_add(p, NT, NT - 1)
                end_phase(dve)

        @block.gpsimd
        def _(pool):
            G = nc.gpsimd

            def ln(p, u, t):
                one = bass.ds(t, 1)

                def m(a):
                    return mom[:, one, a:a + 1].rearrange("p a b -> p (a b)")
                pool.wait_ge(ln_chain, 5 * ln_n(p, u + t) + 5)
                G.tensor_tensor(m(2), m(0), neg_half[:, 0:1], ALU.pow).then_inc(pool_chain, 1)
                pool.wait_ge(pool_chain, ln_n(p, u + t) + 1)
                G.tensor_tensor(m(3), m(1), m(2), ALU.mult).then_inc(ln_rstd, 1)

            def lat_weights(p, k, buf):
                pool.wait_ge(wl_hi, p * KD + k + 1)
                one = bass.ds(k, 1)
                G.tensor_tensor(w_lat[:, 1, one, :].rearrange("p a n -> p (a n)"), s_lat[:, buf, :],
                                w_lat[:, 0, one, :].rearrange("p a n -> p (a n)").bitcast(F32),
                                ALU.subtract).then_inc(wl_lo, 1)

            def rms_norm(p, t):
                pool.wait_ge(ssq_ready, 2 * lat_n(p, t) + 2)
                settle(pool)
                G.tensor_scalar_add(ssq[:, 1, :], ssq[:, 0, :], RMS_EPS).then_inc(rms_chain, 1)
                pool.wait_ge(rms_chain, lat_n(p, t) + 1)
                settle(pool)
                pool.wait_ge(zck_ready, lat_n(p, t) + 1)
                settle(pool)
                G.tensor_tensor(rms[:, :], ssq[:, 1, :], neg_half[:, :], ALU.pow).then_inc(rms_ready, 1)

            def rotate(n, a_wait, first=False):
                step = [4 * n]

                def link(ins):
                    step[0] = step[0] + 1
                    ins.then_inc(rope_chain, 1)
                    pool.wait_ge(rope_chain, step[0])
                    settle(pool)
                pool.wait_ge(swap_in, 64 * (n + 1))
                settle(pool)
                pool.wait_ge(q_act, a_wait)
                settle(pool)
                if not first:
                    pool.wait_ge(qst_in, 64 * n)
                    settle(pool)
                link(G.tensor_tensor(rope_f[:, 2, :], rope_f[:, 0, :], pos_tab[:, 0, :], ALU.mult))
                link(G.tensor_tensor(rope_f[:, 1, :], rope_f[:, 1, :], pos_tab[:, 1, :], ALU.mult))
                link(G.tensor_tensor(rope_f[:, 2, :], rope_f[:, 2, :], rope_f[:, 1, :], ALU.add))
                link(G.tensor_copy(rope_r[:, 0, :], rope_f[:, 2, :]))
                G.tensor_tensor(rope_r[:, 1, :], rope_f[:, 2, :], rope_r[:, 0, :].bitcast(F32),
                                ALU.subtract).then_inc(rope_ready, 1)

            def body(p, g, last=False):
                ev = q_events(last)
                n = p * 2 * NG + 2 * g
                rotate(n + 1, qbase(p, g) + ev["pe1"][0] + 1)
                if not last:
                    rotate(n + 2, qbase(p, g) + ev["pe0"][0] + 1)

            end_phase(pool)
            pool.sem_inc(rms_ready, 1)
            G.memset(neg_half[:, :], -0.5).then_inc(half_ready, 1)
            pool.wait_ge(half_ready, 1)
            pool.wait_ge(consts_in, 16 * 9)
            with pool.Fori(0, NPAIR) as p:
                phases(pool, p, 0)
                ln(p, 0, 0)
                ln(p, 0, 1)
                with pool.Fori(0, NT // 2 - 1) as j:
                    for n in range(2):
                        ln(p, 0, 2 * j + 2 + n)
                        lat_weights(p, 2 * j + n, n)
                lat_weights(p, NT - 2, 0)
                lat_weights(p, NT - 1, 1)
                ln(p, NT, 0)
                ln(p, NT, 1)
                with pool.Fori(0, NT - 2) as t:
                    ln(p, NT, t + 2)
                    rms_norm(p, t)
                rms_norm(p, NT - 2)
                rms_norm(p, NT - 1)
                end_phase(pool)
                phases(pool, p, 1)
                rotate(p * 2 * NG, qbase(p, 0) - 2, first=True)
                with pool.Fori(0, NG - 1) as g:
                    body(p, g)
                body(p, NG - 1, last=True)
                end_phase(pool)
                phases(pool, p, 2)
                with pool.Fori(0, NT) as t:
                    ln(p, 2 * NT, t)
                end_phase(pool)


def kernel(L0_attn_x, L0_attn_wq_a, L0_attn_q_norm_w, L0_attn_wq_b, L0_attn_wkv_a, L0_attn_kv_norm_w,
           L0_attn_wkv_b, L0_attn_wo, L0_ffn_router_w, L0_ffn_router_b, L0_ffn_A, L0_ffn_Bm):
    import numpy as np
    import concourse.bacc as bacc
    from concourse import mybir as mb
    from concourse.bass_utils import run_bass_kernel_spmd

    B, S, D = np.shape(L0_attn_x)
    QL = np.shape(L0_attn_wq_a)[0]
    L = np.shape(L0_attn_kv_norm_w)[0]
    RO = np.shape(L0_attn_wkv_a)[0] - L
    NOPE = 128
    NH = np.shape(L0_attn_wq_b)[0] // (NOPE + RO)
    E, R, _ = np.shape(L0_ffn_A)
    pairs = np.r_[0:RO:2, 1:RO:2]

    wkv_a = np.asarray(L0_attn_wkv_a)
    wkv_a = np.concatenate([wkv_a[:L], wkv_a[L:][pairs]])
    wq_b = np.asarray(L0_attn_wq_b).reshape(NH, NOPE + RO, QL)
    rot = wq_b[:, NOPE:][:, pairs].reshape(NH // 2, 2 * RO, QL)
    wkv_b = np.asarray(L0_attn_wkv_b).reshape(NH, 2 * NOPE, L)

    freq = (1.0 / np.float32(10000.0) ** (np.arange(0, RO, 2, dtype=np.float32) / np.float32(RO))).astype(np.float32)
    ang = np.outer(np.arange(S, dtype=np.float32), freq).astype(np.float32)
    cos, sin = np.cos(ang), np.sin(ang)
    tok = np.stack([np.concatenate([cos, cos], 1), np.concatenate([-sin, sin], 1)], 1)
    pos = np.stack([np.concatenate([cos, cos, cos, cos], 1), np.concatenate([-sin, sin, -sin, sin], 1)], 0)
    row = np.arange(128)
    arrays = {
        "x": np.asarray(L0_attn_x).reshape(B * S, D),
        "wzkv": np.concatenate([np.asarray(L0_attn_wq_a), wkv_a]).T,
        "qnorm": np.asarray(L0_attn_q_norm_w),
        "kvnorm": np.asarray(L0_attn_kv_norm_w),
        "wqn": wq_b[:, :NOPE],
        "wpe": rot.transpose(0, 2, 1),
        "wk": wkv_b[:, :NOPE],
        "wv": wkv_b[:, NOPE:],
        "wo": np.asarray(L0_attn_wo).T.reshape(NH, NOPE, D),
        "ra": np.concatenate([np.asarray(L0_ffn_router_w), np.asarray(L0_ffn_A).reshape(E * R, D)]).T,
        "rb": np.asarray(L0_ffn_router_b),
        "bm": np.asarray(L0_ffn_Bm).transpose(0, 2, 1).reshape(E * R, D),
        "c_ident": np.eye(128, dtype=np.float32),
        "c_mask": np.where(row[None, :] <= row[:, None], 0.0, MASKED).astype(np.float32),
        "c_tri": np.broadcast_to(np.tri(E, k=-1, dtype=np.float32), (128, E, E)),
        "c_tok": tok.reshape(S // 128, 128, 2, RO).transpose(1, 0, 2, 3).reshape(128, S // 128 * 2, RO),
        "c_pos": pos.transpose(2, 0, 1),
    }
    nc = bacc.Bacc("TRN2", target_bir_lowering=False, num_devices=1)
    feeds, args = {}, []
    for name, a in arrays.items():
        a = np.ascontiguousarray(a)
        feeds[f"in_{name}"] = a
        args.append(nc.dram_tensor(f"in_{name}", a.shape, mb.dt.from_np(a.dtype), kind="ExternalInput").ap())
    names = list(arrays)
    out = nc.dram_tensor("out_0", (B * S, D), mb.dt.float32, kind="ExternalOutput").ap()
    build_macaron(nc, **dict(zip(names, args)), out=out)
    r = run_bass_kernel_spmd(nc, [feeds], core_ids=[0])
    return r.results[0]["out_0"].reshape(B, S, D)
```

```python
from contextlib import ExitStack

import concourse.bass as bass
from concourse import mybir

ALU = mybir.AluOpType
ACT = mybir.ActivationFunctionType
F32 = mybir.dt.float32
F32R = mybir.dt.float32r
AX_X = mybir.AxisListType.X

P = 128
MASKED = -1.0e30
LN_EPS = 1e-5
RMS_EPS = 1e-6


def build_macaron(nc, x, wzkv, qnorm, kvnorm, wqn, wpe, wk, wv, wo, ra, rb, bm,
                  c_ident, c_mask, c_tri, c_tok, c_pos, out):
    TOK, D = x.shape
    SEQ = c_pos.shape[2]
    NPAIR = TOK // SEQ // 2
    NT = 2 * SEQ // P
    PT_ = 2 * SEQ
    KD = D // P
    NH, _, QL = wqn.shape
    KQ = QL // P
    L = wk.shape[2]
    RO = c_tok.shape[2]
    ZK = QL + L + RO
    NG = NH // 2
    E = rb.shape[0]
    R = (ra.shape[1] - E) // E
    ER = E * R
    RA = E + ER
    NS = SEQ // P
    HALF = 512
    QSCALE = float((P + RO) ** -0.5)
    FFN_SCALE = 0.5 * 8.0 / R
    EV = 12
    EVD = 10

    xt = x.rearrange("(t p) d -> t p d", p=P)
    outt = out.rearrange("(t p) d -> t p d", p=P)

    def poff(i):
        return P * i * (i + 1) // 2

    with ExitStack() as ctx:
        def sb(name, shape, dt=F32):
            return ctx.enter_context(nc.sbuf_tensor(name, shape, dt))

        def sem(name):
            return ctx.enter_context(nc.semaphore(name))

        xacc = sb("xacc", [P, NT, D])
        zT = sb("zT", [P, 2, KQ, PT_], F32R)
        keyT = sb("keyT", [P, 2, PT_], F32R)
        ropeT = sb("ropeT", [P, 2, PT_], F32R)
        lat = sb("lat", [P, 2, NT, L], F32R)
        ident = sb("ident", [P, P])
        ident_r = sb("ident_r", [P, P], F32R)
        mask_f = sb("mask_f", [P, P])
        mask_r = sb("mask_r", [P, P], F32R)
        tri = sb("tri", [P, E, E])
        tok_tab = sb("tok_tab", [P, NT, 2, RO])
        pos_tab = sb("pos_tab", [P, 2, SEQ])
        qn_bc = sb("qn_bc", [P, QL])
        kvn_bc = sb("kvn_bc", [P, L])
        rb_bc = sb("rb_bc", [P, E])
        neg_half = sb("neg_half", [P, 2])
        n_ffn = 2 * KD * ZK + 2 * KD * RA + 2 * D + 4 * KD * P + 2 * NT * P
        n_att = 4 * D + 4 * QL + 2 * QL + 4 * SEQ + 4 * SEQ + 8 * SEQ + 2 * NS * SEQ + 2 * SEQ
        arena = sb("arena", [P, max(n_ffn, n_att)], F32R)
        at = [0]

        def take(t, *dims):
            n = 1
            for d in dims:
                n *= d
            ap = t[:, at[0]:at[0] + n]
            at[0] += n
            names = "abcd"[:len(dims)]
            if len(dims) > 1:
                ap = ap.rearrange(f"p ({' '.join(names)}) -> p {' '.join(names)}",
                                  **{c: d for c, d in zip(names, dims)})
            return ap

        w_lat = take(arena, 2, KD, ZK)
        w_ra = take(arena, 2, KD, RA)
        w_bm = take(arena, 2, D)
        xnT = take(arena, 2, 2, KD * P)
        hwT = take(arena, 2, NT * P)
        at[0] = 0
        w_out = take(arena, 2, 2, D)
        w_q = take(arena, 2, 2, QL)
        w_pe = take(arena, 2, QL)
        qT = take(arena, 2, 2, SEQ)
        qst = take(arena, 2, 2, SEQ)
        oT = take(arena, 2, 2, 2, SEQ)
        pT = take(arena, 2, NS, SEQ)
        rope_r = take(arena, 2, SEQ)
        n_ffn = 2 * ZK + KD * RA + D + 2 * D + NT * RA + 2 * ZK + RO
        n_att = 2 * QL + 2 * L + 2 * L + 2 * D + QL + 2 * poff(NS) + 3 * SEQ
        stage = sb("stage", [P, max(n_ffn, n_att)])
        at[0] = 0
        s_lat = take(stage, 2, ZK)
        s_ra = take(stage, KD, RA)
        s_bm = take(stage, D)
        xn = take(stage, 2, D)
        cmp = xn.rearrange("p b (t e f) -> p b t e f", e=E, f=E)[:, :, 0:NT]
        hw = xn[:, 0].rearrange("p (t n) -> p t n", t=NT)
        hb = take(stage, NT, RA)
        zr = take(stage, ZK)
        zck = take(stage, ZK + RO)
        at[0] = 0
        s_wqn = take(stage, 2, QL)
        s_wk = take(stage, 2, L)
        s_wpe = take(stage, KQ, P)
        s_wv = take(stage, 2, L)
        s_wo = take(stage, 2, D)
        prob = take(stage, 2, poff(NS))
        rope_f = take(stage, 3, SEQ)
        stats = sb("stats", [P, 2, 6])
        mv = sb("mv", [P, 2])
        mom = sb("mom", [P, NT, 4])
        lgt = sb("lgt", [P, 3, NT, E])
        rank = sb("rank", [P, NT, E])
        gsc = sb("gsc", [P, 3, NT])
        ssq = sb("ssq", [P, 2, 2])
        rms = sb("rms", [P, 2])
        junk = sb("junk", [P, QL])
        rtmp = sb("rtmp", [P, 2, RO])
        negmax = sb("negmax", [P, 2, NS])
        rowsum = sb("rowsum", [P, 2, NS])
        rrec = sb("rrec", [P, 2, NS])

        ps = ctx.enter_context(nc.psum_tensor("ps", [P, 8, HALF], F32))
        bxs = [ps[:, n:n + 2, :].rearrange("p a b -> p (a b)") for n in (0, 5)]
        bh = ps[:, 2, 0:RA]
        bz = ps[:, 2, 0:QL]
        bkv = ps[:, 3, 0:L + RO]
        bt = ps[:, 4, :]
        bkk = ps[:, 7, 0:P]

        def bout(half):
            return ps[:, 5 + half, :]

        def bank_s(i):
            return ps[:, i % 2, :]

        def bank_t(i):
            return ps[:, 2 + i % 2, :]
        bank_pv = ps[:, 4, :]
        bank_q = ps[:, 5, :]

        def bank_y(j):
            return ps[:, 6 + j % 2, :]

        consts_in = sem("consts_in")
        consts_ready = sem("consts_ready")
        vec_const = sem("vec_const")
        half_ready = sem("half_ready")
        settled = sem("settled")
        phase_end = sem("phase_end")
        fw_in = sem("fw_in")
        wl_in = sem("wl_in")
        wl_hi = sem("wl_hi")
        wl_lo = sem("wl_lo")
        pool_chain = sem("pool_chain")
        h_read = sem("h_read")
        gates_ready = sem("gates_ready")
        z_read = sem("z_read")
        fw_hi = sem("fw_hi")
        fw_lo = sem("fw_lo")
        x_first = sem("x_first")
        x_rest = sem("x_rest")
        ln_chain = sem("ln_chain")
        ln_rstd = sem("ln_rstd")
        xn_ready = sem("xn_ready")
        xt_done = sem("xt_done")
        xt_hi = sem("xt_hi")
        xt_lo = sem("xt_lo")
        h_done = sem("h_done")
        gate_chain = sem("gate_chain")
        gate_exp = sem("gate_exp")
        hw_ready = sem("hw_ready")
        hwt_done = sem("hwt_done")
        hwt_hi = sem("hwt_hi")
        hwt_lo = sem("hwt_lo")
        ffn_done = sem("ffn_done")
        ffn_added = sem("ffn_added")
        stored = sem("stored")
        zk_done = sem("zk_done")
        ssq_ready = sem("ssq_ready")
        rms_chain = sem("rms_chain")
        rms_ready = sem("rms_ready")
        tok_chain = sem("tok_chain")
        zck_ready = sem("zck_ready")
        zckt_done = sem("zckt_done")
        lat_hi = sem("lat_hi")
        lat_lo = sem("lat_lo")
        wq_in = sem("wq_in")
        wo_in = sem("wo_in")
        wpe_hi = sem("wpe_hi")
        wpe_lo = sem("wpe_lo")
        scores_done = sem("scores_done")
        max_ready = sem("max_ready")
        exp_done = sem("exp_done")
        rec_ready = sem("rec_ready")
        prob_ready = sem("prob_ready")
        pt_done = sem("pt_done")
        pt_hi = sem("pt_hi")
        pt_lo = sem("pt_lo")
        q_full = sem("q_full")
        q_act = sem("q_act")
        q_dve = sem("q_dve")
        swap_in = sem("swap_in")
        rope_chain = sem("rope_chain")
        rope_ready = sem("rope_ready")
        qst_in = sem("qst_in")
        pv_done = sem("pv_done")
        o_hi = sem("o_hi")
        o_lo = sem("o_lo")
        y_done = sem("y_done")
        y_added = sem("y_added")

        block = ctx.enter_context(nc.Block())
        NLN = 3 * NT
        NF = 2 * NT
        GATE_STEPS = 13

        def ln_n(p, u):
            return p * NLN + u

        def ffn_n(p, f):
            return p * NF + f

        def lat_n(p, t):
            return p * NT + t

        def slot_n(p, g, k):
            return (p * NG + g) * 4 + k

        def phases(eng, p, n, engine_count=5):
            eng.wait_ge(phase_end, (p * 3 + n + 1) * engine_count)
            settle(eng)

        def settle(eng):
            eng.sem_inc(settled, 1)

        def starts(n):
            return isinstance(n, int) and n == 0

        def end_phase(eng):
            eng.drain().then_inc(phase_end, 1)

        def q_events(last):
            seq = ["q1", "pe1", "q2", "w0", "pe0", "m0", "q3", "m1", "m2", "m3", "q0", "w1"]
            if last:
                seq = [name for name in seq if name not in ("w0", "pe0", "q0", "w1")]
            found, a, d = {}, 0, 0
            for name in seq:
                found[name] = (a, d)
                a, d = a + 1, d + (name[:2] != "pe")
            return found
        PRO = {"pe0": (-4, -3), "w0": (-3, -3), "q0": (-2, -2), "w1": (-1, -1)}

        def qbase(p, g):
            return p * EV * NG + EV * g + 4

        def qbase_d(p, g):
            return p * EVD * NG + EVD * g + 3

        FIRST_FILL = ["q1", "q2", "pe0", "q0"]
        LAST_FILL = ["pe1", "w0", "q3", "w1"]

        def y_slot(k, j):
            b, t0 = [(0, 2), (1, 0), (1, 2), (0, 0)][k]
            return b, t0 + j % 2, j // 2

        def y_n(p, g, k):
            return p * 16 * NG + 16 * g + 4 * k - 12

        @block.sync
        def _(sp):
            end_phase(sp)
            sp.dma_start(ident[:, :], c_ident).then_inc(consts_in, 16)
            sp.dma_start(mask_f[:, :], c_mask).then_inc(consts_in, 16)
            sp.dma_start(tri[:, :, :], c_tri).then_inc(consts_in, 16)
            for b in range(2):
                sp.dma_start(tok_tab[:, b * NS:(b + 1) * NS, :, :],
                             c_tok.rearrange("p (n r) w -> p n r w", n=NS)).then_inc(consts_in, 16)
            sp.dma_start(pos_tab[:, :, :], c_pos).then_inc(consts_in, 16)
            sp.dma_start(qn_bc[:, :], qnorm.partition_broadcast(P)).then_inc(consts_in, 16)
            sp.dma_start(kvn_bc[:, :], kvnorm.partition_broadcast(P)).then_inc(consts_in, 16)
            sp.dma_start(rb_bc[:, :], rb.partition_broadcast(P)).then_inc(consts_in, 16)

            def load_ffn():
                sp.dma_start(s_ra, ra.rearrange("(k p) n -> p k n", p=P)).then_inc(fw_in, 16)
                sp.dma_start(s_bm, bm).then_inc(fw_in, 16)

            def load_wq(g):
                sp.dma_start(s_wqn, wqn[bass.ds(2 * g, 2)].rearrange("h p n -> p h n")).then_inc(wq_in, 16)
                sp.dma_start(s_wk, wk[bass.ds(2 * g, 2)].rearrange("h p n -> p h n")).then_inc(wq_in, 16)
                sp.dma_start(s_wpe, wpe[bass.ds(g, 1)].rearrange("a (k p) n -> p (a k) n", p=P)).then_inc(wq_in, 16)

            def load_wo(g):
                sp.dma_start(s_wv, wv[bass.ds(2 * g, 2)].rearrange("h p n -> p h n")).then_inc(wo_in, 16)
                sp.dma_start(s_wo, wo[bass.ds(2 * g, 2)].rearrange("h p n -> p h n")).then_inc(wo_in, 16)

            def body(p, g, first=False, last=False):
                ev = q_events(last)
                if not first:
                    sp.wait_ge(q_full, qbase(p, g - 1) + q_events(False)["m3"][0] + 1)
                    settle(sp)
                load_wo(g)
                sp.wait_ge(wo_in, 32 * (p * NG + g + 1))
                settle(sp)
                if not last:
                    sp.wait_ge(q_full, qbase(p, g))
                    settle(sp)
                    sp.wait_ge(wpe_hi, p * NG + g + 1)
                    settle(sp)
                    sp.wait_ge(wpe_lo, p * NG + g + 1)
                    settle(sp)
                    load_wq(g + 1)
                    sp.wait_ge(wq_in, 48 * (p * NG + g + 2))
                    settle(sp)
                n = p * 2 * NG + 2 * g
                sp.wait_ge(q_act, qbase(p, g) + ev["pe1"][0] + 1)
                settle(sp)
                rotary(n + 1, 1, None if first else 4 * slot_n(p, g, 0))
                if not last:
                    sp.wait_ge(q_act, qbase(p, g) + ev["pe0"][0] + 1)
                    settle(sp)
                    rotary(n + 2, 0, 4 * slot_n(p, g, 2))

            def rotary(n, b, used):
                for q in range(4):
                    o = q ^ 1
                    sp.dma_start(rope_f[32 * q:32 * q + 32, 1, :], rope_f[32 * o:32 * o + 32, 0, :])\
                      .then_inc(swap_in, 16)
                sp.wait_ge(rope_ready, n + 1)
                settle(sp)
                if used is not None:
                    sp.wait_ge(scores_done, used)
                    settle(sp)
                for h in range(2):
                    for part in range(2):
                        dst = 64 * (part ^ h)
                        sp.dma_start(qst[dst:dst + 64, b, h, :].bitcast(F32),
                                     rope_r[64 * h:64 * h + 64, part, :].bitcast(F32)).then_inc(qst_in, 16)
                sp.wait_ge(qst_in, 64 * (n + 1))
                settle(sp)

            def load_x(p, j):
                sp.dma_start(xacc[:, 2 * j:2 * j + 2, :], xt[p * NT + 2 * j:p * NT + 2 * j + 2]
                             .rearrange("a p d -> p a d")).then_inc(x_rest if j else x_first, 16)

            def load_lat(n, j):
                sp.dma_start(s_lat, wzkv.rearrange("(k p) n -> p k n", p=P)[:, bass.ds(2 * j, 2), :])\
                  .then_inc(wl_in, 16)
                sp.wait_ge(wl_in, 16 * (n * (NT // 2) + j + 1))
                settle(sp)

            def load_lats(n):
                load_lat(n, 0)
                with sp.Fori(1, NT // 2) as j:
                    sp.wait_ge(wl_hi, n * KD + 2 * j)
                    settle(sp)
                    sp.wait_ge(wl_lo, n * KD + 2 * j)
                    settle(sp)
                    load_lat(n, j)

            for p in range(NPAIR):
                phases(sp, p, 0)
                if p == 0:
                    load_x(p, 0)
                    load_ffn()
                    for j in range(1, NT // 2):
                        load_x(p, j)
                    load_lats(0)
                sp.wait_ge(wl_hi, (p + 1) * KD)
                settle(sp)
                sp.wait_ge(wl_lo, (p + 1) * KD)
                settle(sp)
                sp.wait_ge(fw_hi, 2 * (p + 1))
                settle(sp)
                sp.wait_ge(fw_lo, 2 * (p + 1))
                settle(sp)
                load_wq(0)
                sp.wait_ge(wq_in, 48 * (p * NG + 1))
                settle(sp)
                end_phase(sp)
                phases(sp, p, 1)
                sp.wait_ge(q_act, qbase(p, 0) - 3)
                settle(sp)
                rotary(p * 2 * NG, 0, None)
                body(p, 0, first=True)
                with sp.Fori(1, NG - 1) as g:
                    body(p, g)
                body(p, NG - 1, last=True)
                end_phase(sp)
                phases(sp, p, 2)
                load_ffn()
                if p + 1 < NPAIR:
                    load_lats(p + 1)
                    for j in range(NT // 2):
                        sp.wait_ge(ffn_added, 2 * ffn_n(p, NT + 2 * j + 2))
                        settle(sp)
                        t = p * NT + 2 * j
                        sp.dma_start(outt[t:t + 2].rearrange("a p d -> p a d"), xacc[:, 2 * j:2 * j + 2, :])\
                          .then_inc(stored, 32)
                        sp.wait_ge(stored, 16 * (t + 2))
                        settle(sp)
                        load_x(p + 1, j)
                else:
                    with sp.Fori(0, NT) as t:
                        sp.wait_ge(ffn_added, 2 * ffn_n(p, NT + t + 1))
                        settle(sp)
                        sp.dma_start(outt[bass.ds(p * NT + t, 1)].rearrange("a p d -> p a d"),
                                     xacc[:, bass.ds(t, 1), :]).then_inc(stored, 16)
                    sp.wait_ge(stored, 16 * NT * (p + 1))
                    settle(sp)
                end_phase(sp)

        @block.tensor
        def _(pe):
            def products(dst, passes, start=True, stop=True, skip=False):
                for n, (w, m) in enumerate(passes):
                    last = nc.tensor.matmul(dst, w, m, start=start and n == 0,
                                            stop=stop and n == len(passes) - 1, skip_group_check=skip)
                return last

            def three(w_hi, w_lo, m_hi_, m_lo_):
                return [(w_hi, m_hi_), (w_hi, m_lo_), (w_lo, m_hi_)]

            def turn_x(p, u, t, buf, two=False):
                pe.wait_ge(xn_ready, ln_n(p, u + t) + 1)
                if not (two and isinstance(t, int) and t < 2):
                    pe.wait_ge(xt_hi, ln_n(p, u + t) - two)
                    pe.wait_ge(xt_lo, ln_n(p, u + t) - two)
                bx = bxs[buf if two else 0]
                for k in range(KD):
                    last = nc.tensor.transpose(bx[:, k * P:(k + 1) * P], xn[:, buf, k * P:(k + 1) * P], ident[:, :])
                last.then_inc(xt_done, 1)

            def ffn_up(p, u, f, t, buf):
                pe.wait_ge(xt_hi, ln_n(p, u + t) + 1)
                pe.wait_ge(xt_lo, ln_n(p, u + t) + 1)
                if not starts(f + t):
                    pe.wait_ge(h_read, ffn_n(p, f + t))
                passes = []
                for k in range(KD):
                    passes += three(xnT[:, buf, 0, k * P:(k + 1) * P], xnT[:, buf, 1, k * P:(k + 1) * P],
                                    w_ra[:, 0, k, :], w_ra[:, 1, k, :])
                products(bh, passes).then_inc(h_done, 1)

            def turn_h(p, n):
                pe.wait_ge(hw_ready, 2 * p + n + 1)
                for t in range(NT):
                    last = nc.tensor.transpose(bxs[0][:, t * P:(t + 1) * P], hw[:, t, :], ident[:, :])
                last.then_inc(hwt_done, 1)
                pe.wait_ge(hwt_hi, 2 * p + n + 1)
                pe.wait_ge(hwt_lo, 2 * p + n + 1)

            def ffn_down(p, f, t):
                hT = [hwT[:, part, t * P:(t + 1) * P] for part in range(2)]
                for n in range(2):
                    if not starts(f + t):
                        pe.wait_ge(ffn_added, 2 * ffn_n(p, f + t) - 1 + n)
                    s = slice(n * HALF, (n + 1) * HALF)
                    products(bout(n), three(hT[0], hT[1], w_bm[:, 0, s], w_bm[:, 1, s]))\
                        .then_inc(ffn_done, 1)

            def latents(p, t, buf, k0, k1):
                if k0 == 0:
                    pe.wait_ge(xt_hi, ln_n(p, NT + t) + 1)
                    pe.wait_ge(xt_lo, ln_n(p, NT + t) + 1)
                    if not starts(t):
                        pe.wait_ge(z_read, 2 * lat_n(p, t))
                for k in range(k0, k1):
                    for n, (xp, wp) in enumerate(((0, 0), (0, 1), (1, 0))):
                        for dst, c in ((bz, slice(0, QL)), (bkv, slice(QL, ZK))):
                            last = nc.tensor.matmul(dst, xnT[:, buf, xp, k * P:(k + 1) * P], w_lat[:, wp, k, c],
                                                    start=(k == 0 and n == 0), stop=(k == KD - 1 and n == 2))
                if k1 == KD:
                    last.then_inc(zk_done, 1)

            def turn_latents(p, t, half):
                if half == 0:
                    pe.wait_ge(zck_ready, lat_n(p, t) + 2)
                    for n in range(4):
                        nc.tensor.transpose(bt[:, n * P:(n + 1) * P], zck[:, n * P:(n + 1) * P], ident[:, :])
                else:
                    nc.tensor.transpose(bkk, zck[:, 4 * P:5 * P], ident[:, :]).then_inc(zckt_done, 1)

            def norm_and_up(p, u, f):
                turn_x(p, u, 0, 0, two=True)
                turn_x(p, u, 1, 1, two=True)
                with pe.Fori(0, NT // 2 - 1) as j:
                    for n in range(2):
                        ffn_up(p, u, f, 2 * j + n, n)
                        turn_x(p, u, 2 * j + n + 2, n, two=True)
                ffn_up(p, u, f, NT - 2, 0)
                ffn_up(p, u, f, NT - 1, 1)

            def tile_step(p, t):
                buf, one, two, back = t % 2, t + 1 < NT, t + 2 < NT, t > 0
                latents(p, t, buf, 0, 6)
                if back:
                    pe.wait_ge(lat_hi, 4 * lat_n(p, t - 1) + 1)
                    pe.wait_ge(lat_lo, 4 * lat_n(p, t - 1) + 1)
                    turn_latents(p, t - 1, 0)
                latents(p, t, buf, 6, 7)
                if one:
                    turn_x(p, NT, t + 1, 1 - buf)
                latents(p, t, buf, 7, KD)
                if back:
                    turn_latents(p, t - 1, 1)
                if two:
                    ffn_down(p, 0, t + 2)

            def q_free(p, g, a, d):
                pe.wait_ge(q_act, qbase(p, g) + a)
                pe.wait_ge(q_dve, qbase_d(p, g) + d)

            def fill(p, g, name, ev):
                a, d = ev[name]
                if not (ev is PRO and name == "pe0"):
                    q_free(p, g, a, d)
                if name[0] == "q":
                    k = int(name[1])
                    h, b = k % 2, k // 2
                    s = slice(b * SEQ, (b + 1) * SEQ)
                    passes = []
                    for c in range(KQ):
                        cs = slice(c * P, (c + 1) * P)
                        passes += three(w_q[:, h, 0, cs], w_q[:, h, 1, cs], zT[:, 0, c, s], zT[:, 1, c, s])
                    products(bank_q, passes).then_inc(q_full, 1)
                elif name[:2] == "pe":
                    b = int(name[2])
                    n = p * NG + g + (1 if ev is PRO or name == "pe1" else 2)
                    pe.wait_ge(wpe_hi, n)
                    pe.wait_ge(wpe_lo, n)
                    s = slice(b * SEQ, (b + 1) * SEQ)
                    passes = []
                    for c in range(KQ):
                        cs = slice(c * P, (c + 1) * P)
                        passes += three(w_pe[:, 0, cs], w_pe[:, 1, cs], zT[:, 0, c, s], zT[:, 1, c, s])
                    products(bank_q, passes).then_inc(q_full, 1)
                elif name[0] == "m":
                    h, half = int(name[1]) % 2, int(name[1]) // 2
                    pe.wait_ge(wo_in, 32 * (p * NG + g + 1))
                    nc.tensor.matmul(bank_q, s_wv[:, h, :], s_wo[:, h, half * HALF:(half + 1) * HALF],
                                     start=True, stop=True).then_inc(q_full, 1)
                else:
                    h = int(name[1])
                    pe.wait_ge(wq_in, 48 * (p * NG + g + (1 if ev is PRO else 2)))
                    for c in range(KQ):
                        last = nc.tensor.matmul(bank_q[:, c * P:(c + 1) * P], s_wqn[:, h, c * P:(c + 1) * P],
                                                s_wk[:, h, :], start=True, stop=True)
                    last.then_inc(q_full, 1)

            def scores(p, g, k, i, first, last):
                h, b = k % 2, k // 2
                n = slot_n(p, g, k)
                if i == 0:
                    a, d = q_events(last)[f"q{k}"] if k else (-2, -2)
                    pe.wait_ge(q_act, qbase(p, g) + a + 1)
                    pe.wait_ge(q_dve, qbase_d(p, g) + d + 1)
                    if h == 0:
                        pe.wait_ge(qst_in, 64 * (p * 2 * NG + 2 * g + b + 1))
                if not (first and k == 0 and i < 2):
                    pe.wait_ge(exp_done, 4 * n + i - 1)
                qs = slice(i * P, (i + 1) * P)
                ks = slice(b * SEQ, b * SEQ + (i + 1) * P)
                dst = bank_s(i)[:, 0:(i + 1) * P]
                products(dst, three(qT[:, h, 0, qs], qT[:, h, 1, qs], keyT[:, 0, ks], keyT[:, 1, ks])
                         + [(qst[:, b, h, qs], ropeT[:, 0, ks]), (qst[:, b, h, qs], ropeT[:, 1, ks])], stop=False)
                nc.tensor.matmul(dst[:, i * P:(i + 1) * P], ident_r[:, :], mask_r[:, :],
                                 start=False, stop=True).then_inc(scores_done, 1)

            def turn_probs(n, k, i, first):
                pe.wait_ge(prob_ready, 4 * n + i + 1)
                if not (first and i < 2):
                    pe.wait_ge(pt_hi, 4 * n + i - 1)
                    pe.wait_ge(pt_lo, 4 * n + i - 1)
                for j in range(i + 1):
                    last = nc.tensor.transpose(bank_t(i)[:, j * P:(j + 1) * P],
                                               prob[:, k % 2, poff(i) + j * P:poff(i) + (j + 1) * P], ident[:, :])
                last.then_inc(pt_done, 1)

            def values(n, k, first):
                b = k // 2
                pe.wait_ge(pt_hi, 4 * n + 4)
                pe.wait_ge(pt_lo, 4 * n + 4)
                if not first:
                    pe.wait_ge(o_hi, n)
                    pe.wait_ge(o_lo, n)
                for j in range(NS):
                    t = b * NS + j
                    s = slice(j * P, SEQ)
                    last = products(bank_pv[:, s], three(lat[:, 0, t, :], lat[:, 1, t, :], pT[:, 0, j, s], pT[:, 1, j, s]),
                                    start=(j == 0), stop=(j == NS - 1))
                last.then_inc(pv_done, 1)

            def output(p, g, k, j, first, last):
                b, tt, half = y_slot(k, j)
                n = y_n(p, g, k) + j
                if k == 3 and j % 2 == 0:
                    a, d = q_events(last)["m3" if half else "m1"]
                    pe.wait_ge(q_act, qbase(p, g) + a + 1)
                    pe.wait_ge(q_dve, qbase_d(p, g) + d + 1)
                if j == 0 and k % 2 == 1:
                    pe.wait_ge(o_hi, slot_n(p, g, k) - 1)
                    pe.wait_ge(o_lo, slot_n(p, g, k) - 1)
                if not (first and j < 2):
                    pe.wait_ge(y_added, n - 1)
                ts = slice(tt * P, (tt + 1) * P)
                hs = slice(half * HALF, (half + 1) * HALF)
                passes = []
                for h in range(2):
                    passes += three(oT[:, b, h, 0, ts], oT[:, b, h, 1, ts], w_out[:, h, 0, hs], w_out[:, h, 1, hs])
                products(bank_y(j), passes).then_inc(y_done, 1)

            def slot(p, g, k, first=False, last=False, drained=False):
                n, before = slot_n(p, g, k) - 1, (k - 1) % 4
                ev = {} if drained else q_events(last)
                turn = not (first and k == 0) and not (drained and k > 0)
                out_ = not first or k == 3
                if not drained:
                    scores(p, g, k, 0, first, last)
                    scores(p, g, k, 1, first, last)
                if k == 3:
                    fill(p, g, "m2", ev)
                if turn:
                    turn_probs(n, before, 0, first and k == 1)
                    turn_probs(n, before, 1, first and k == 1)
                if out_:
                    output(p, g, k, 0, first, last)
                if not drained:
                    scores(p, g, k, 2, first, last)
                if turn:
                    turn_probs(n, before, 2, False)
                if k == 3:
                    fill(p, g, "m3", ev)
                if out_:
                    output(p, g, k, 1, first, last)
                if not drained:
                    scores(p, g, k, 3, first, last)
                if turn:
                    turn_probs(n, before, 3, False)
                if FIRST_FILL[k] in ev:
                    fill(p, g, FIRST_FILL[k], ev)
                if out_:
                    output(p, g, k, 2, first, last)
                if k == 2 and not drained:
                    fill(p, g, "m0", ev)
                if turn:
                    values(n, before, first and k == 1)
                if LAST_FILL[k] in ev:
                    fill(p, g, LAST_FILL[k], ev)
                if out_:
                    output(p, g, k, 3, first, last)
                if k == 2 and not drained:
                    fill(p, g, "m1", ev)

            def body(p, g, first=False, last=False):
                for k in range(4):
                    slot(p, g, k, first, last)

            end_phase(pe)
            pe.wait_ge(consts_ready, 2)
            pe.wait_ge(consts_in, 16 * 9)
            for p in range(NPAIR):
                phases(pe, p, 0)
                pe.wait_ge(fw_hi, 2 * (p + 1))
                pe.wait_ge(fw_lo, 2 * (p + 1))
                norm_and_up(p, 0, 0)
                turn_h(p, 0)
                ffn_down(p, 0, 0)
                ffn_down(p, 0, 1)
                turn_x(p, NT, 0, 0)
                pe.wait_ge(wl_hi, (p + 1) * KD)
                pe.wait_ge(wl_lo, (p + 1) * KD)
                for t in range(NT):
                    tile_step(p, t)
                pe.wait_ge(lat_hi, 4 * lat_n(p, NT - 1) + 1)
                pe.wait_ge(lat_lo, 4 * lat_n(p, NT - 1) + 1)
                turn_latents(p, NT - 1, 0)
                turn_latents(p, NT - 1, 1)
                end_phase(pe)
                phases(pe, p, 1)
                for name in ("pe0", "w0", "q0", "w1"):
                    fill(p, 0, name, PRO)
                body(p, 0, first=True)
                with pe.Fori(1, NG - 1) as g:
                    body(p, g)
                body(p, NG - 1, last=True)
                for k in range(3):
                    slot(p, NG, k, drained=True)
                end_phase(pe)
                phases(pe, p, 2)
                pe.wait_ge(fw_hi, 2 * (p + 2))
                pe.wait_ge(fw_lo, 2 * (p + 2))
                norm_and_up(p, 2 * NT, NT)
                turn_h(p, 1)
                for t in range(NT):
                    ffn_down(p, NT, t)
                end_phase(pe)

        @block.scalar
        def _(act):
            def hi(dst, src):
                return nc.scalar.activation(dst, src, ACT.Copy)

            def split_ffn(n):
                act.wait_ge(fw_in, 32 * (n + 1))
                for w, s in ((w_ra, s_ra), (w_bm, s_bm)):
                    hi(w[:, 0], s).then_inc(fw_hi, 1)

            def normalise(p, u, t, buf):
                act.wait_ge(ln_rstd, ln_n(p, u + t) + 1)
                if not starts(u + t) and not (isinstance(t, int) and u + t == 1):
                    act.wait_ge(xt_done, ln_n(p, u + t) - 1)
                one = bass.ds(t, 1)
                nc.scalar.activation(xn[:, buf, :], xacc[:, one, :].rearrange("p a d -> p (a d)"), ACT.Identity,
                                     bias=mom[:, one, 3:4].rearrange("p a b -> p (a b)"),
                                     scale=mom[:, one, 2:3].rearrange("p a b -> p (a b)")).then_inc(xn_ready, 1)

            def turned_x(p, u, t, buf, two=False):
                act.wait_ge(xt_done, ln_n(p, u + t) + 1)
                hi(xnT[:, buf, 0, :], bxs[buf if two else 0]).then_inc(xt_hi, 1)

            def keep_h(p, f, t):
                act.wait_ge(h_done, ffn_n(p, f + t) + 1)
                hi(hb[:, bass.ds(t, 1), :].rearrange("p a n -> p (a n)"), bh).then_inc(h_read, 1)

            def lat_weights(n, k, buf):
                act.wait_ge(wl_in, 16 * (n * (NT // 2)) + 8 * (k - buf) + 16)
                hi(w_lat[:, 0, bass.ds(k, 1), :].rearrange("p a n -> p (a n)"), s_lat[:, buf, :]).then_inc(wl_hi, 1)

            def norm_and_up(p, u, f, weights):
                normalise(p, u, 0, 0)
                normalise(p, u, 1, 1)
                turned_x(p, u, 0, 0, two=True)
                with act.Fori(0, NT // 2 - 1) as j:
                    for n in range(2):
                        normalise(p, u, 2 * j + 2 + n, n)
                        turned_x(p, u, 2 * j + 1 + n, 1 - n, two=True)
                        if weights is not None:
                            lat_weights(weights, 2 * j + n, n)
                        keep_h(p, f, 2 * j + n)
                turned_x(p, u, NT - 1, 1, two=True)
                keep_h(p, f, NT - 2)
                if weights is not None:
                    lat_weights(weights, NT - 2, 0)
                    lat_weights(weights, NT - 1, 1)
                keep_h(p, f, NT - 1)

            def gates(p, n):
                act.wait_ge(gate_chain, (2 * p + n) * GATE_STEPS + 3)
                nc.scalar.activation(lgt[:, 1], lgt[:, 0], ACT.Exp).then_inc(gate_exp, 1)

            def turned_h(p, n):
                act.wait_ge(hwt_done, 2 * p + n + 1)
                hi(hwT[:, 0, :], bxs[0]).then_inc(hwt_hi, 1)

            def keep_latents(p, t):
                act.wait_ge(zk_done, lat_n(p, t) + 1)
                act.wait_ge(zck_ready, lat_n(p, t) + 1)
                hi(zr[:, 0:QL], bz).then_inc(z_read, 1)
                hi(zr[:, QL:ZK], bkv).then_inc(z_read, 1)

            def squares(p, t):
                act.wait_ge(rms_ready, lat_n(p, t) + 1)
                act.wait_ge(z_read, 2 * lat_n(p, t) + 1)
                nc.scalar.activation(junk[:, 0:QL], zr[:, 0:QL], ACT.Square, scale=float(QL ** -0.5),
                                     accum_out=ssq[:, 0, 0:1]).then_inc(ssq_ready, 1)
                act.wait_ge(z_read, 2 * lat_n(p, t) + 2)
                act.wait_ge(ssq_ready, 2 * lat_n(p, t) + 1)
                nc.scalar.activation(junk[:, 0:L], zr[:, QL:QL + L], ACT.Square, scale=float(L ** -0.5),
                                     accum_out=ssq[:, 0, 1:2]).then_inc(ssq_ready, 1)

            def latents(p, t):
                act.wait_ge(zckt_done, lat_n(p, t) + 1)
                ts = bass.ds(t * P, P)
                hi(lat[:, 0, bass.ds(t, 1), :].rearrange("p a l -> p (a l)"), zck[:, QL:QL + L]).then_inc(lat_hi, 1)
                hi(zT[:, 0, :, ts], bt[:, 0:QL].rearrange("p (k t) -> p k t", k=KQ)).then_inc(lat_hi, 1)
                hi(keyT[:, 0, ts], bt[:, QL:QL + P]).then_inc(lat_hi, 1)
                hi(ropeT[:, 0, ts], bkk).then_inc(lat_hi, 1)

            def tile_step(p, t, buf, one=True, back=True):
                if one:
                    normalise(p, NT, t + 1, 1 - buf)
                    turned_x(p, NT, t + 1, 1 - buf)
                keep_latents(p, t)
                squares(p, t)
                if back:
                    latents(p, t - 1)

            def read_fill(p, g, name, ev):
                a, d = ev[name]
                act.wait_ge(q_full, qbase(p, g) + a + 1)
                if name[0] == "q":
                    dst = qT[:, int(name[1]) % 2, 0, :]
                    src = bank_q
                elif name[:2] == "pe":
                    if ev is not PRO:
                        act.wait_ge(rope_ready, p * 2 * NG + 2 * g + (1 if name == "pe1" else 2))
                    dst, src = rope_f[:, 0, :], bank_q
                elif name[0] == "m":
                    h, half = int(name[1]) % 2, int(name[1]) // 2
                    dst, src = w_out[:, h, 0, half * HALF:(half + 1) * HALF], bank_q
                else:
                    dst, src = w_q[:, int(name[1]), 0, :], bank_q[:, 0:QL]
                hi(dst, src).then_inc(q_act, 1)

            def exps(p, g, k, i):
                n = slot_n(p, g, k)
                act.wait_ge(max_ready, 4 * n + i + 1)
                nc.scalar.activation(prob[:, k % 2, poff(i):poff(i + 1)], bank_s(i)[:, 0:(i + 1) * P], ACT.Exp,
                                     bias=negmax[:, k % 2, i:i + 1],
                                     accum_out=rowsum[:, k % 2, i:i + 1]).then_inc(exp_done, 1)

            def turned(n, i):
                act.wait_ge(pt_done, 4 * n + i + 1)
                hi(pT[:, 0, 0:i + 1, i * P:(i + 1) * P],
                   bank_t(i)[:, 0:(i + 1) * P].rearrange("p (j s) -> p j s", s=P)).then_inc(pt_hi, 1)

            def valued(n, k):
                act.wait_ge(pv_done, n + 1)
                hi(oT[:, k // 2, k % 2, 0, :], bank_pv).then_inc(o_hi, 1)

            def split_wpe(p, g):
                act.wait_ge(wq_in, 48 * (p * NG + g + 1))
                hi(w_pe[:, 0, :], s_wpe.rearrange("p k n -> p (k n)")).then_inc(wpe_hi, 1)

            def body(p, g, first=False, last=False):
                ev = q_events(last)
                for k in range(4):
                    n, before = slot_n(p, g, k) - 1, (k - 1) % 4
                    turn = not (first and k == 0)
                    exps(p, g, k, 0)
                    exps(p, g, k, 1)
                    if k == 3:
                        read_fill(p, g, "m2", ev)
                    if turn:
                        turned(n, 0)
                        turned(n, 1)
                    exps(p, g, k, 2)
                    if turn:
                        turned(n, 2)
                    if k == 3:
                        read_fill(p, g, "m3", ev)
                    exps(p, g, k, 3)
                    if turn:
                        turned(n, 3)
                    if FIRST_FILL[k] in ev:
                        read_fill(p, g, FIRST_FILL[k], ev)
                    if k == 1 and not last:
                        split_wpe(p, g + 1)
                    if k == 2:
                        read_fill(p, g, "m0", ev)
                    if turn:
                        valued(n, before)
                    if LAST_FILL[k] in ev:
                        read_fill(p, g, LAST_FILL[k], ev)
                    if k == 2:
                        read_fill(p, g, "m1", ev)

            end_phase(act)
            act.sem_inc(lat_hi, 1)
            act.wait_ge(consts_in, 16 * 9)
            hi(ident_r[:, :], ident[:, :]).then_inc(consts_ready, 1)
            hi(mask_r[:, :], mask_f[:, :]).then_inc(consts_ready, 1)
            for p in range(NPAIR):
                phases(act, p, 0)
                if p == 0:
                    split_ffn(0)
                norm_and_up(p, 0, 0, 0 if p == 0 else None)
                gates(p, 0)
                turned_h(p, 0)
                normalise(p, NT, 0, 0)
                turned_x(p, NT, 0, 0)
                tile_step(p, 0, 0, back=False)
                with act.Fori(0, NT // 2 - 1) as j:
                    tile_step(p, 2 * j + 1, 1)
                    tile_step(p, 2 * j + 2, 0)
                tile_step(p, NT - 1, 1, one=False)
                latents(p, NT - 1)
                end_phase(act)
                phases(act, p, 1)
                split_wpe(p, 0)
                for name in ("pe0", "w0", "q0", "w1"):
                    read_fill(p, 0, name, PRO)
                body(p, 0, first=True)
                with act.Fori(1, NG - 1) as g:
                    body(p, g)
                body(p, NG - 1, last=True)
                for i in range(NS):
                    turned(slot_n(p, NG, 0) - 1, i)
                valued(slot_n(p, NG, 0) - 1, 3)
                end_phase(act)
                phases(act, p, 2)
                split_ffn(p + 1)
                norm_and_up(p, 2 * NT, NT, p + 1 if p + 1 < NPAIR else None)
                gates(p, 1)
                turned_h(p, 1)
                end_phase(act)

        @block.vector
        def _(dve):
            def lo(dst, src, part):
                return nc.vector.tensor_tensor(dst, src, part.bitcast(F32), ALU.subtract)

            def split_ffn(n):
                for m, (w, s) in enumerate(((w_ra, s_ra), (w_bm, s_bm))):
                    dve.wait_ge(fw_hi, 2 * n + m + 1)
                    lo(w[:, 1], s, w[:, 0]).then_inc(fw_lo, 1)

            def moments(p, u, t, added=None):
                if added is not None:
                    dve.wait_ge(ffn_added, added)
                    settle(dve)
                one = bass.ds(t, 1)
                xs = xacc[:, one, :].rearrange("p a d -> p (a d)")

                def m(a, b):
                    return mom[:, one, a:b].rearrange("p a b -> p (a b)")
                base = ln_n(p, u + t) * 5
                for n in range(2):
                    nc.vector.bn_stats(stats[:, n, :], xs[:, n * HALF:(n + 1) * HALF]).then_inc(ln_chain, 1)
                dve.wait_ge(ln_chain, base + 2)
                settle(dve)
                nc.vector.bn_aggr(mv[:, :], stats[:, :, :]).then_inc(ln_chain, 1)
                dve.wait_ge(ln_chain, base + 3)
                nc.vector.tensor_scalar_add(m(0, 1), mv[:, 1:2], LN_EPS).then_inc(ln_chain, 1)
                nc.vector.tensor_scalar(m(1, 2), mv[:, 0:1], -1.0, None, ALU.mult).then_inc(ln_chain, 1)

            def turned_x(p, u, t, buf, two=False):
                dve.wait_ge(xt_hi, ln_n(p, u + t) + 1)
                lo(xnT[:, buf, 1, :], bxs[buf if two else 0], xnT[:, buf, 0, :]).then_inc(xt_lo, 1)

            def norm_and_up(p, u, load):
                if load:
                    dve.wait_ge(x_first, 16 * (p + 1))
                    settle(dve)
                moments(p, u, 0)
                moments(p, u, 1)
                if load:
                    dve.wait_ge(x_rest, 16 * (NT // 2 - 1) * (p + 1))
                    settle(dve)
                with dve.Fori(0, NT // 2 - 1) as j:
                    for n in range(2):
                        moments(p, u, 2 * j + 2 + n)
                        turned_x(p, u, 2 * j + n, n, two=True)
                turned_x(p, u, NT - 2, 0, two=True)
                turned_x(p, u, NT - 1, 1, two=True)

            def gates(p, n, f):
                base = (2 * p + n) * GATE_STEPS
                step = [0]

                def link(ins):
                    step[0] += 1
                    ins.then_inc(gate_chain, 1)
                    dve.wait_ge(gate_chain, base + step[0])
                V = nc.vector
                dve.wait_ge(h_read, ffn_n(p, f + NT))

                def wide(ap, k):
                    return ap.rearrange("p t (e a) -> p t e a", a=1).to_broadcast([P, NT, E, k])
                per_tile = [gsc[:, i, :].rearrange("p (t a) -> p t a", a=1).to_broadcast([P, NT, E]) for i in range(3)]
                ex = lgt[:, 1]
                link(V.tensor_tensor(lgt[:, 0], hb[:, :, 0:E],
                                     rb_bc[:, :].rearrange("p (a e) -> p a e", a=1).to_broadcast([P, NT, E]), ALU.add))
                link(V.tensor_reduce(gsc[:, 0, :], lgt[:, 0], AX_X, ALU.max))
                link(V.tensor_tensor(lgt[:, 0], lgt[:, 0], per_tile[0], ALU.subtract))
                dve.wait_ge(gate_exp, 2 * p + n + 1)
                mine = wide(ex, E)
                other = ex.rearrange("p t (a e) -> p t a e", a=1).to_broadcast([P, NT, E, E])
                before = tri[:, :, :].rearrange("p (a e) f -> p a e f", a=1).to_broadcast([P, NT, E, E])
                link(V.tensor_tensor(cmp[:, 0], other, mine, ALU.is_gt))
                link(V.tensor_tensor(cmp[:, 1], other, mine, ALU.is_equal))
                link(V.tensor_tensor(cmp[:, 1], cmp[:, 1], before, ALU.mult))
                link(V.tensor_tensor(cmp[:, 0], cmp[:, 0], cmp[:, 1], ALU.add))
                link(V.tensor_reduce(rank[:, :, :], cmp[:, 0], AX_X, ALU.add))
                link(V.scalar_tensor_tensor(lgt[:, 2], rank[:, :, :], 1.5, ex, ALU.is_lt, ALU.mult))
                link(V.tensor_reduce(gsc[:, 1, :], lgt[:, 2], AX_X, ALU.add))
                link(V.reciprocal(gsc[:, 2, :], gsc[:, 1, :]))
                link(V.tensor_scalar(gsc[:, 2, :], gsc[:, 2, :], FFN_SCALE, None, ALU.mult))
                link(V.tensor_tensor(lgt[:, 2], lgt[:, 2], per_tile[2], ALU.mult))
                assert step[0] == GATE_STEPS

            def gate_h(p, n):
                w = lgt[:, 2].rearrange("p t (e a) -> p t e a", a=1).to_broadcast([P, NT, E, R])
                nc.vector.tensor_tensor(hw.rearrange("p t (e r) -> p t e r", r=R),
                                        hb[:, :, E:RA].rearrange("p t (e r) -> p t e r", r=R), w,
                                        ALU.mult).then_inc(hw_ready, 1)

            def turned_h(p, n):
                dve.wait_ge(hwt_hi, 2 * p + n + 1)
                lo(hwT[:, 1, :], bxs[0], hwT[:, 0, :]).then_inc(hwt_lo, 1)

            def ffn_add(p, f, t):
                for n in range(2):
                    dve.wait_ge(ffn_done, 2 * ffn_n(p, f + t) + n + 1)
                    xs = xacc[:, bass.ds(t, 1), n * HALF:(n + 1) * HALF].rearrange("p a d -> p (a d)")
                    nc.vector.tensor_tensor(xs, bout(n), xs, ALU.add).then_inc(ffn_added, 1)

            def tokens(p, t):
                V = nc.vector
                dve.wait_ge(z_read, 2 * lat_n(p, t) + 2)
                cs = tok_tab[:, bass.ds(t, 1), 0, :].rearrange("p a w -> p (a w)")
                sn = tok_tab[:, bass.ds(t, 1), 1, :].rearrange("p a w -> p (a w)")
                H = RO // 2
                k0 = QL + L
                V.tensor_tensor(rtmp[:, 0, :], zr[:, k0:ZK], cs, ALU.mult)
                V.tensor_tensor(rtmp[:, 1, 0:H], zr[:, k0 + H:ZK], sn[:, 0:H], ALU.mult)
                V.tensor_tensor(rtmp[:, 1, H:RO], zr[:, k0:k0 + H], sn[:, H:RO], ALU.mult).then_inc(tok_chain, 1)
                dve.wait_ge(lat_lo, 4 * lat_n(p, t) + 1)
                dve.wait_ge(rms_ready, lat_n(p, t) + 2)
                V.scalar_tensor_tensor(zck[:, 0:QL], zr[:, 0:QL], rms[:, 0:1], qn_bc[:, :], ALU.mult, ALU.mult)
                V.scalar_tensor_tensor(zck[:, QL:QL + L], zr[:, QL:QL + L], rms[:, 1:2], kvn_bc[:, :],
                                       ALU.mult, ALU.mult)
                dve.wait_ge(tok_chain, lat_n(p, t) + 1)
                twice = [rtmp[:, n, :].rearrange("p (a w) -> p a w", a=1).to_broadcast([P, 2, RO]) for n in range(2)]
                V.tensor_tensor(zck[:, QL + L:ZK + RO].rearrange("p (a w) -> p a w", a=2),
                                twice[0], twice[1], ALU.add).then_inc(zck_ready, 1)

            def latents(p, t):
                ts = bass.ds(t * P, P)
                n = 4 * lat_n(p, t) + 1
                dve.wait_ge(lat_hi, n + 1)
                one = bass.ds(t, 1)
                lo(lat[:, 1, one, :].rearrange("p a l -> p (a l)"), zck[:, QL:QL + L],
                   lat[:, 0, one, :].rearrange("p a l -> p (a l)")).then_inc(lat_lo, 1)
                dve.wait_ge(lat_hi, n + 3)
                lo(zT[:, 1, :, ts], bt[:, 0:QL].rearrange("p (k t) -> p k t", k=KQ), zT[:, 0, :, ts]).then_inc(lat_lo, 1)
                lo(keyT[:, 1, ts], bt[:, QL:QL + P], keyT[:, 0, ts]).then_inc(lat_lo, 1)
                dve.wait_ge(lat_hi, n + 4)
                lo(ropeT[:, 1, ts], bkk, ropeT[:, 0, ts]).then_inc(lat_lo, 1)

            def tile_step(p, t, buf, one=True, two=True, back=2):
                if one:
                    moments(p, NT, t + 1, added=2 * ffn_n(p, t + 2))
                if back > 1:
                    latents(p, t - 2)
                if back:
                    tokens(p, t - 1)
                if one:
                    turned_x(p, NT, t + 1, 1 - buf)
                if two:
                    ffn_add(p, 0, t + 2)

            def read_fill(p, g, name, ev):
                a, d = ev[name]
                if name[:2] == "pe":
                    return
                dve.wait_ge(q_act, qbase(p, g) + a + 1)
                if name[0] == "q":
                    h = int(name[1]) % 2
                    lo(qT[:, h, 1, :], bank_q, qT[:, h, 0, :]).then_inc(q_dve, 1)
                elif name[0] == "m":
                    h, s = int(name[1]) % 2, slice(int(name[1]) // 2 * HALF, (int(name[1]) // 2 + 1) * HALF)
                    lo(w_out[:, h, 1, s], bank_q, w_out[:, h, 0, s]).then_inc(q_dve, 1)
                else:
                    h = int(name[1])
                    lo(w_q[:, h, 1, :], bank_q[:, 0:QL], w_q[:, h, 0, :]).then_inc(q_dve, 1)

            def maxima(p, g, k, i):
                n = slot_n(p, g, k)
                dve.wait_ge(scores_done, 4 * n + i + 1)
                nc.vector.tensor_reduce(negmax[:, k % 2, i:i + 1], bank_s(i)[:, 0:(i + 1) * P], AX_X, ALU.max,
                                        negate=True).then_inc(max_ready, 1)

            def norms(p, g, k):
                n = slot_n(p, g, k)
                dve.wait_ge(exp_done, 4 * n + NS)
                nc.vector.reciprocal(rrec[:, k % 2, :], rowsum[:, k % 2, :]).then_inc(rec_ready, 1)
                dve.wait_ge(rec_ready, n + 1)
                for i in range(NS):
                    pr = prob[:, k % 2, poff(i):poff(i + 1)]
                    nc.vector.tensor_scalar(pr, pr, rrec[:, k % 2, i:i + 1], None, ALU.mult).then_inc(prob_ready, 1)

            def pt_split(n, i):
                dve.wait_ge(pt_hi, 4 * n + i + 1)
                ap = [pT[:, part, 0:i + 1, i * P:(i + 1) * P] for part in range(2)]
                lo(ap[1], bank_t(i)[:, 0:(i + 1) * P].rearrange("p (j s) -> p j s", s=P), ap[0]).then_inc(pt_lo, 1)

            def y_add(p, g, k, j):
                b, tt, half = y_slot(k, j)
                dve.wait_ge(y_done, y_n(p, g, k) + j + 1)
                xs = xacc[:, b * NS + tt, half * HALF:(half + 1) * HALF]
                nc.vector.tensor_tensor(xs, bank_y(j), xs, ALU.add).then_inc(y_added, 1)

            def o_split(n, k):
                dve.wait_ge(o_hi, n + 1)
                lo(oT[:, k // 2, k % 2, 1, :], bank_pv, oT[:, k // 2, k % 2, 0, :]).then_inc(o_lo, 1)

            def split_wpe(p, g):
                dve.wait_ge(wpe_hi, p * NG + g + 1)
                lo(w_pe[:, 1, :], s_wpe.rearrange("p k n -> p (k n)"), w_pe[:, 0, :]).then_inc(wpe_lo, 1)

            def slot(p, g, k, first=False, last=False, drained=False):
                n, before = slot_n(p, g, k) - 1, (k - 1) % 4
                ev = {} if drained else q_events(last)
                turn = not (first and k == 0) and not (drained and k > 0)
                out_ = not first or k == 3
                if not drained:
                    maxima(p, g, k, 0)
                    maxima(p, g, k, 1)
                if k == 3:
                    read_fill(p, g, "m2", ev)
                if turn:
                    pt_split(n, 0)
                    pt_split(n, 1)
                if out_:
                    y_add(p, g, k, 0)
                if not drained:
                    maxima(p, g, k, 2)
                if turn:
                    pt_split(n, 2)
                if k == 3:
                    read_fill(p, g, "m3", ev)
                if out_:
                    y_add(p, g, k, 1)
                if not drained:
                    maxima(p, g, k, 3)
                if turn:
                    pt_split(n, 3)
                if FIRST_FILL[k] in ev:
                    read_fill(p, g, FIRST_FILL[k], ev)
                if k == 1 and not last and not drained:
                    split_wpe(p, g + 1)
                if out_:
                    y_add(p, g, k, 2)
                if k == 2 and not drained:
                    read_fill(p, g, "m0", ev)
                if not drained:
                    norms(p, g, k)
                if turn:
                    o_split(n, before)
                if LAST_FILL[k] in ev:
                    read_fill(p, g, LAST_FILL[k], ev)
                if out_:
                    y_add(p, g, k, 3)
                if k == 2 and not drained:
                    read_fill(p, g, "m1", ev)

            def body(p, g, first=False, last=False):
                for k in range(4):
                    slot(p, g, k, first, last)

            end_phase(dve)
            dve.sem_inc(lat_lo, 1)
            dve.sem_inc(zck_ready, 1)
            dve.wait_ge(consts_in, 16 * 9)
            nc.vector.tensor_scalar(qn_bc[:, :], qn_bc[:, :], QSCALE, None, ALU.mult).then_inc(vec_const, 1)
            dve.wait_ge(vec_const, 1)
            for p in range(NPAIR):
                phases(dve, p, 0)
                if p == 0:
                    split_ffn(0)
                norm_and_up(p, 0, True)
                gates(p, 0, 0)
                gate_h(p, 0)
                turned_h(p, 0)
                ffn_add(p, 0, 0)
                moments(p, NT, 0, added=2 * ffn_n(p, 1))
                ffn_add(p, 0, 1)
                turned_x(p, NT, 0, 0)
                tile_step(p, 0, 0, back=0)
                tile_step(p, 1, 1, back=1)
                with dve.Fori(1, NT // 2 - 1) as j:
                    tile_step(p, 2 * j, 0)
                    tile_step(p, 2 * j + 1, 1)
                tile_step(p, NT - 2, 0, two=False)
                tile_step(p, NT - 1, 1, one=False, two=False)
                latents(p, NT - 2)
                tokens(p, NT - 1)
                latents(p, NT - 1)
                end_phase(dve)
                phases(dve, p, 1)
                split_wpe(p, 0)
                for name in ("pe0", "w0", "q0", "w1"):
                    read_fill(p, 0, name, PRO)
                body(p, 0, first=True)
                with dve.Fori(1, NG - 1) as g:
                    body(p, g)
                body(p, NG - 1, last=True)
                for k in range(3):
                    slot(p, NG, k, drained=True)
                end_phase(dve)
                phases(dve, p, 2)
                split_ffn(p + 1)
                norm_and_up(p, 2 * NT, False)
                gates(p, 1, NT)
                gate_h(p, 1)
                turned_h(p, 1)
                with dve.Fori(0, NT) as t:
                    ffn_add(p, NT, t)
                end_phase(dve)

        @block.gpsimd
        def _(pool):
            G = nc.gpsimd

            def ln(p, u, t):
                one = bass.ds(t, 1)

                def m(a):
                    return mom[:, one, a:a + 1].rearrange("p a b -> p (a b)")
                pool.wait_ge(ln_chain, 5 * ln_n(p, u + t) + 5)
                G.tensor_tensor(m(2), m(0), neg_half[:, 0:1], ALU.pow).then_inc(pool_chain, 1)
                pool.wait_ge(pool_chain, ln_n(p, u + t) + 1)
                G.tensor_tensor(m(3), m(1), m(2), ALU.mult).then_inc(ln_rstd, 1)

            def lat_weights(n, k, buf):
                pool.wait_ge(wl_hi, n * KD + k + 1)
                one = bass.ds(k, 1)
                G.tensor_tensor(w_lat[:, 1, one, :].rearrange("p a n -> p (a n)"), s_lat[:, buf, :],
                                w_lat[:, 0, one, :].rearrange("p a n -> p (a n)").bitcast(F32),
                                ALU.subtract).then_inc(wl_lo, 1)

            def norms(p, u, weights):
                ln(p, u, 0)
                ln(p, u, 1)
                with pool.Fori(0, NT // 2 - 1) as j:
                    for n in range(2):
                        ln(p, u, 2 * j + 2 + n)
                        if weights is not None:
                            lat_weights(weights, 2 * j + n, n)
                if weights is not None:
                    lat_weights(weights, NT - 2, 0)
                    lat_weights(weights, NT - 1, 1)

            def rms_norm(p, t):
                pool.wait_ge(ssq_ready, 2 * lat_n(p, t) + 2)
                settle(pool)
                G.tensor_scalar_add(ssq[:, 1, :], ssq[:, 0, :], RMS_EPS).then_inc(rms_chain, 1)
                pool.wait_ge(rms_chain, lat_n(p, t) + 1)
                settle(pool)
                pool.wait_ge(zck_ready, lat_n(p, t) + 1)
                settle(pool)
                G.tensor_tensor(rms[:, :], ssq[:, 1, :], neg_half[:, :], ALU.pow).then_inc(rms_ready, 1)

            def rotate(n, a_wait, first=False):
                step = [4 * n]

                def link(ins):
                    step[0] = step[0] + 1
                    ins.then_inc(rope_chain, 1)
                    pool.wait_ge(rope_chain, step[0])
                    settle(pool)
                pool.wait_ge(q_act, a_wait)
                settle(pool)
                if not first:
                    pool.wait_ge(qst_in, 64 * n)
                    settle(pool)
                link(G.tensor_tensor(rope_f[:, 2, :], rope_f[:, 0, :], pos_tab[:, 0, :], ALU.mult))
                pool.wait_ge(swap_in, 64 * (n + 1))
                settle(pool)
                link(G.tensor_tensor(rope_f[:, 1, :], rope_f[:, 1, :], pos_tab[:, 1, :], ALU.mult))
                link(G.tensor_tensor(rope_r[:, 0, :], rope_f[:, 2, :], rope_f[:, 1, :], ALU.add))
                link(G.tensor_tensor(rope_f[:, 2, :], rope_f[:, 2, :], rope_f[:, 1, :], ALU.add))
                G.tensor_tensor(rope_r[:, 1, :], rope_f[:, 2, :], rope_r[:, 0, :].bitcast(F32),
                                ALU.subtract).then_inc(rope_ready, 1)

            def body(p, g, last=False):
                ev = q_events(last)
                n = p * 2 * NG + 2 * g
                rotate(n + 1, qbase(p, g) + ev["pe1"][0] + 1)
                if not last:
                    rotate(n + 2, qbase(p, g) + ev["pe0"][0] + 1)

            end_phase(pool)
            pool.sem_inc(rms_ready, 1)
            G.memset(neg_half[:, :], -0.5).then_inc(half_ready, 1)
            pool.wait_ge(half_ready, 1)
            pool.wait_ge(consts_in, 16 * 9)
            for p in range(NPAIR):
                phases(pool, p, 0)
                norms(p, 0, 0 if p == 0 else None)
                ln(p, NT, 0)
                ln(p, NT, 1)
                with pool.Fori(0, NT - 2) as t:
                    rms_norm(p, t)
                    ln(p, NT, t + 2)
                rms_norm(p, NT - 2)
                rms_norm(p, NT - 1)
                end_phase(pool)
                phases(pool, p, 1)
                rotate(p * 2 * NG, qbase(p, 0) - 2, first=True)
                with pool.Fori(0, NG - 1) as g:
                    body(p, g)
                body(p, NG - 1, last=True)
                end_phase(pool)
                phases(pool, p, 2)
                norms(p, 2 * NT, p + 1 if p + 1 < NPAIR else None)
                end_phase(pool)


def kernel(L0_attn_x, L0_attn_wq_a, L0_attn_q_norm_w, L0_attn_wq_b, L0_attn_wkv_a, L0_attn_kv_norm_w,
           L0_attn_wkv_b, L0_attn_wo, L0_ffn_router_w, L0_ffn_router_b, L0_ffn_A, L0_ffn_Bm):
    import numpy as np
    import concourse.bacc as bacc
    from concourse import mybir as mb
    from concourse.bass_utils import run_bass_kernel_spmd

    B, S, D = np.shape(L0_attn_x)
    QL = np.shape(L0_attn_wq_a)[0]
    L = np.shape(L0_attn_kv_norm_w)[0]
    RO = np.shape(L0_attn_wkv_a)[0] - L
    NOPE = 128
    NH = np.shape(L0_attn_wq_b)[0] // (NOPE + RO)
    E, R, _ = np.shape(L0_ffn_A)
    pairs = np.r_[0:RO:2, 1:RO:2]

    wkv_a = np.asarray(L0_attn_wkv_a)
    wkv_a = np.concatenate([wkv_a[:L], wkv_a[L:][pairs]])
    wq_b = np.asarray(L0_attn_wq_b).reshape(NH, NOPE + RO, QL)
    rot = wq_b[:, NOPE:][:, pairs].reshape(NH // 2, 2 * RO, QL)
    wkv_b = np.asarray(L0_attn_wkv_b).reshape(NH, 2 * NOPE, L)

    freq = (1.0 / np.float32(10000.0) ** (np.arange(0, RO, 2, dtype=np.float32) / np.float32(RO))).astype(np.float32)
    ang = np.outer(np.arange(S, dtype=np.float32), freq).astype(np.float32)
    cos, sin = np.cos(ang), np.sin(ang)
    tok = np.stack([np.concatenate([cos, cos], 1), np.concatenate([-sin, sin], 1)], 1)
    pos = np.stack([np.concatenate([cos, cos, cos, cos], 1), np.concatenate([-sin, sin, -sin, sin], 1)], 0)
    row = np.arange(128)
    arrays = {
        "x": np.asarray(L0_attn_x).reshape(B * S, D),
        "wzkv": np.concatenate([np.asarray(L0_attn_wq_a), wkv_a]).T,
        "qnorm": np.asarray(L0_attn_q_norm_w),
        "kvnorm": np.asarray(L0_attn_kv_norm_w),
        "wqn": wq_b[:, :NOPE],
        "wpe": rot.transpose(0, 2, 1),
        "wk": wkv_b[:, :NOPE],
        "wv": wkv_b[:, NOPE:],
        "wo": np.asarray(L0_attn_wo).T.reshape(NH, NOPE, D),
        "ra": np.concatenate([np.asarray(L0_ffn_router_w), np.asarray(L0_ffn_A).reshape(E * R, D)]).T,
        "rb": np.asarray(L0_ffn_router_b),
        "bm": np.asarray(L0_ffn_Bm).transpose(0, 2, 1).reshape(E * R, D),
        "c_ident": np.eye(128, dtype=np.float32),
        "c_mask": np.where(row[None, :] <= row[:, None], 0.0, MASKED).astype(np.float32),
        "c_tri": np.broadcast_to(np.tri(E, k=-1, dtype=np.float32), (128, E, E)),
        "c_tok": tok.reshape(S // 128, 128, 2, RO).transpose(1, 0, 2, 3).reshape(128, S // 128 * 2, RO),
        "c_pos": pos.transpose(2, 0, 1),
    }
    nc = bacc.Bacc("TRN2", target_bir_lowering=False, num_devices=1)
    feeds, args = {}, []
    for name, a in arrays.items():
        a = np.ascontiguousarray(a)
        feeds[f"in_{name}"] = a
        args.append(nc.dram_tensor(f"in_{name}", a.shape, mb.dt.from_np(a.dtype), kind="ExternalInput").ap())
    names = list(arrays)
    out = nc.dram_tensor("out_0", (B * S, D), mb.dt.float32, kind="ExternalOutput").ap()
    build_macaron(nc, **dict(zip(names, args)), out=out)
    r = run_bass_kernel_spmd(nc, [feeds], core_ids=[0])
    return r.results[0]["out_0"].reshape(B, S, D)
```

```python
from contextlib import ExitStack

import concourse.bass as bass
from concourse import mybir

ALU = mybir.AluOpType
ACT = mybir.ActivationFunctionType
F32 = mybir.dt.float32
F32R = mybir.dt.float32r
AX_X = mybir.AxisListType.X

P = 128
MASKED = -1.0e30
LN_EPS = 1e-5
RMS_EPS = 1e-6


def build_macaron(nc, x, wzkv, qnorm, kvnorm, wqn, wpe, wk, wv, wo, ra, rb, bm,
                  c_ident, c_mask, c_tri, c_tok, c_pos, kept_out, kept_q, out):
    TOK, D = x.shape
    SEQ = c_pos.shape[2]
    NPAIR = TOK // SEQ // 2
    NT = 2 * SEQ // P
    HT = NT // 2
    PAIR = 2 * SEQ
    KD = D // P
    NH, _, QL = wqn.shape
    KQ = QL // P
    L = wk.shape[2]
    RO = c_tok.shape[2]
    ZK = QL + L + RO
    NG = NH // 2
    E = rb.shape[0]
    R = (ra.shape[1] - E) // E
    ER = E * R
    RA = E + ER
    NS = SEQ // P
    HALF = 512
    QSCALE = float((P + RO) ** -0.5)
    FFN_SCALE = 0.5 * 8.0 / R

    xt = x.rearrange("(t p) d -> t p d", p=P)
    outt = out.rearrange("(t p) d -> t p d", p=P)

    def poff(i):
        return P * i * (i + 1) // 2

    with ExitStack() as ctx:
        def sb(name, shape, dt=F32):
            return ctx.enter_context(nc.sbuf_tensor(name, shape, dt))

        def sem(name):
            return ctx.enter_context(nc.semaphore(name))

        xacc = sb("xacc", [P, NT, D])
        zT = sb("zT", [P, 2, KQ, PAIR], F32R)
        keyT = sb("keyT", [P, 2, PAIR], F32R)
        ropeT = sb("ropeT", [P, 2, PAIR], F32R)
        lat = sb("lat", [P, 2, NT, L], F32R)
        ident = sb("ident", [P, P])
        mask = sb("mask", [P, P])
        tri = sb("tri", [P, E, E])
        tok_tab = sb("tok_tab", [P, NT, 2, RO])
        pos_tab = sb("pos_tab", [P, 2, SEQ])
        qn_bc = sb("qn_bc", [P, QL])
        kvn_bc = sb("kvn_bc", [P, L])
        rb_bc = sb("rb_bc", [P, E])
        neg_half = sb("neg_half", [P, 2])
        n_ffn = 2 * KD * ZK + 2 * KD * RA + 2 * D + 4 * KD * P + P + 2 * NT * P
        n_att = 4 * D + 4 * QL + 2 * QL + 4 * SEQ + 4 * SEQ + 8 * SEQ + 2 * NS * SEQ + 2 * SEQ
        arena = sb("arena", [P, max(n_ffn, n_att)], F32R)
        at = [0]

        def take(t, *dims):
            n = 1
            for d in dims:
                n *= d
            ap = t[:, at[0]:at[0] + n]
            at[0] += n
            names = "abcd"[:len(dims)]
            if len(dims) > 1:
                ap = ap.rearrange(f"p ({' '.join(names)}) -> p {' '.join(names)}",
                                  **{c: d for c, d in zip(names, dims)})
            return ap

        w_lat = take(arena, 2, KD, ZK)
        w_ra = take(arena, 2, KD, RA)
        w_bm = take(arena, 2, D)
        xnT = take(arena, 2, 2, KD * P)
        at[0] = 2 * KD * ZK + 2 * KD * RA + 2 * D + 4 * KD * P + P
        hwT = take(arena, 2, NT * P)
        at[0] = 0
        w_out = take(arena, 2, 2, D)
        pT = take(arena, 2, NS, SEQ)
        qT = [take(arena, 2, SEQ)]
        assert at[0] == 2 * KD * ZK
        w_pe = take(arena, 2, QL)
        rope_r = take(arena, 2, SEQ)
        w_q = take(arena, 2, 2, QL)
        assert at[0] <= 2 * KD * (ZK + RA) + 2 * D
        oT = take(arena, 2, 2, 2, SEQ)
        qT.append(take(arena, 2, SEQ))
        qst = take(arena, 2, 2, SEQ)
        n_ffn = 2 * ZK + KD * RA + D + 2 * D + NT * RA + 2 * ZK + RO
        n_att = 2 * QL + 2 * L + 2 * L + 2 * D + QL + 2 * poff(NS) + 3 * SEQ
        stage = sb("stage", [P, max(n_ffn, n_att)])
        at[0] = 0
        s_lat = take(stage, 2, ZK)
        s_ra = take(stage, KD, RA)
        s_bm = take(stage, D)
        xn = take(stage, 2, D)
        hb = take(stage, NT, RA)
        zr = take(stage, ZK)
        zck = take(stage, ZK + RO)
        at[0] = 0
        s_wqn = take(stage, 2, QL)
        s_wk = take(stage, 2, L)
        s_wpe = take(stage, KQ, P)
        assert at[0] <= 2 * ZK + KD * RA
        rope_f = take(stage, 3, SEQ)
        assert at[0] <= 2 * ZK + KD * RA + D
        s_wv = take(stage, 2, L)
        s_wo = take(stage, 2, D)
        prob = take(stage, 2, poff(NS))
        stats = sb("stats", [P, 2, 6])
        mv = sb("mv", [P, 2])
        mom = sb("mom", [P, NT, 4])
        lgt = sb("lgt", [P, 3, NT, E])
        rank = sb("rank", [P, NT, E])
        gsc = sb("gsc", [P, 3, NT])
        cmp = sb("cmp", [P, 2, HT, E, E])
        hw = sb("hw", [P, HT, ER])
        ssq = sb("ssq", [P, 2, 2])
        rms = sb("rms", [P, 2])
        junk = sb("junk", [P, QL])
        rtmp = sb("rtmp", [P, 2, RO])
        negmax = sb("negmax", [P, 2, NS])
        rowsum = sb("rowsum", [P, 2, NS])
        rrec = sb("rrec", [P, 2, NS])

        ps = ctx.enter_context(nc.psum_tensor("ps", [P, 8, HALF], F32))
        bxs = [ps[:, n:n + 2, :].rearrange("p a b -> p (a b)") for n in (0, 5)]
        bhs = [ps[:, 2 + n, 0:RA] for n in range(2)]
        ZH = ZK // 2
        bzs = [ps[:, 2 + n, 0:ZH] for n in range(2)]
        bt = ps[:, 4, :]
        bkk = ps[:, 7, 0:P]
        bhw = ps[:, 7, :]

        def bout(pair):
            return ps[:, (5, 3)[pair]:(5, 3)[pair] + 2, :]

        def bank_s(i):
            return ps[:, i % 2, :]

        def bank_t(i):
            return ps[:, 2 + i % 2, :]
        bank_pv = ps[:, 4, :]
        bank_q = ps[:, 5, :]

        def bank_y(j):
            return ps[:, 6 + j % 2, :]

        ident_in = sem("ident_in")
        consts_in = sem("consts_in")
        vec_const = sem("vec_const")
        half_ready = sem("half_ready")
        settled = sem("settled")
        phase_end = sem("phase_end")
        ra_in = sem("ra_in")
        bm_in = sem("bm_in")
        wl_in = [sem(f"wl_in{n}") for n in range(2)]
        wl_hi = sem("wl_hi")
        wl_lo = sem("wl_lo")
        pool_chain = sem("pool_chain")
        h_read = sem("h_read")
        z_read = sem("z_read")
        ra_hi = sem("ra_hi")
        ra_lo = sem("ra_lo")
        bm_hi = sem("bm_hi")
        bm_lo = sem("bm_lo")
        x_in = [sem(f"x_in{j}") for j in range(NT // 2)]
        ln_chain = sem("ln_chain")
        ln_rstd = sem("ln_rstd")
        xn_ready = sem("xn_ready")
        xt_done = sem("xt_done")
        xt_hi = sem("xt_hi")
        xt_lo = sem("xt_lo")
        h_done = sem("h_done")
        gate_chain = sem("gate_chain")
        gate_exp = sem("gate_exp")
        hw_ready = sem("hw_ready")
        hwt_done = sem("hwt_done")
        hwt_hi = sem("hwt_hi")
        hwt_lo = sem("hwt_lo")
        ffn_done = sem("ffn_done")
        ffn_added = sem("ffn_added")
        stored = sem("stored")
        zk_done = sem("zk_done")
        ssq_ready = sem("ssq_ready")
        rms_chain = sem("rms_chain")
        rms_ready = sem("rms_ready")
        tok_chain = sem("tok_chain")
        zck_ready = sem("zck_ready")
        zckt_done = sem("zckt_done")
        lat_hi = sem("lat_hi")
        lat_lo = sem("lat_lo")
        wq_in = sem("wq_in")
        wpe_in = sem("wpe_in")
        wq_kept = sem("wq_kept")
        wo_kept = sem("wo_kept")
        q_back = [sem(f"q_back{h}") for h in range(2)]
        o_back = [sem(f"o_back{n}") for n in range(2)]
        wo_in = sem("wo_in")
        wpe_hi = sem("wpe_hi")
        wpe_lo = sem("wpe_lo")
        scores_done = sem("scores_done")
        masked = sem("masked")
        max_ready = sem("max_ready")
        exp_done = sem("exp_done")
        rec_ready = sem("rec_ready")
        prob_ready = sem("prob_ready")
        pt_done = sem("pt_done")
        pt_hi = sem("pt_hi")
        pt_lo = sem("pt_lo")
        q_full = sem("q_full")
        q_act = sem("q_act")
        q_dve = sem("q_dve")
        swap_in = sem("swap_in")
        rope_chain = sem("rope_chain")
        rope_ready = sem("rope_ready")
        qst_in = sem("qst_in")
        pv_done = sem("pv_done")
        o_hi = sem("o_hi")
        o_lo = sem("o_lo")
        y_done = sem("y_done")
        y_added = sem("y_added")

        block = ctx.enter_context(nc.Block())
        NLN = 3 * NT
        NF = 2 * NT
        GATE_STEPS = 13

        def ln_n(p, u):
            return p * NLN + u

        def ffn_n(p, f):
            return p * NF + f

        def half_n(p, n, part):
            return 4 * p + 2 * n + part

        def lat_n(p, t):
            return p * NT + t

        def slot_n(p, g, k):
            return (p * NG + g) * 4 + k

        def phases(eng, p, n, engine_count=5):
            eng.wait_ge(phase_end, (p * 3 + n + 1) * engine_count)
            settle(eng)

        def settle(eng):
            eng.sem_inc(settled, 1)

        def starts(n):
            return isinstance(n, int) and n == 0

        def end_phase(eng):
            eng.drain().then_inc(phase_end, 1)

        FILLS = [{
            "output": [None, None, None, "m2"],
            "second": [None, None, "m0", "m3"],
            "first":  ["pe1", "q2", "pe0", "q0"],
            "third":  ["q1", None, "q3", None],
            "values": [None, "w0", "m1", "w1"],
        }] + [{
            "first":  ["pe1", "q2", "pe0", "q0"],
            "third":  ["q1", None, "q3", None],
        }] * (NPAIR - 1)

        def fill_at(p, place, k):
            return FILLS[p].get(place, [None] * 4)[k]

        def q_events(p, last):
            names = [row[k] for k in range(4) for row in FILLS[p].values() if row[k]]
            if last:
                names = [name for name in names if name not in ("w0", "pe0", "q0", "w1")]
            return counted(names, 0, 0)

        def counted(names, a, d):
            found = {}
            for name in names:
                found[name] = (a, d)
                a, d = a + 1, d + (name[:2] != "pe")
            return found

        BEFORE = [["pe0", "w0", "w1", "q0"]] + [["pe0", "q0"]] * (NPAIR - 1)
        PRO = [counted(names, -len(names), 1 - len(names)) for names in BEFORE]
        EV = [len(q_events(p, False)) for p in range(NPAIR)]
        EVD = [n - 2 for n in EV]

        def qbase(p, g):
            return sum(EV[:p]) * NG + EV[p] * g + len(BEFORE[p])

        def qbase_d(p, g):
            return sum(EVD[:p]) * NG + EVD[p] * g + len(BEFORE[p]) - 1

        def q_slot(p, g, k, first, last):
            if k:
                a, d = q_events(p, last)[f"q{k}"]
            elif first:
                a, d = PRO[p]["q0"]
            else:
                a, d = q_events(p, False)["q0"]
                a, d = a - EV[p], d - EVD[p]
            return qbase(p, g) + a + 1, qbase_d(p, g) + d + 1

        def y_slot(k, j):
            b, t0 = [(0, 2), (1, 0), (1, 2), (0, 0)][k]
            return b, t0 + j % 2, j // 2

        def y_n(p, g, k):
            return p * 16 * NG + 16 * g + 4 * k - 12

        @block.sync
        def _(sp):
            end_phase(sp)
            sp.dma_start(ident[:, :], c_ident).then_inc(ident_in, 16)

            def load_consts():
                sp.dma_start(rb_bc[:, :], rb.partition_broadcast(P)).then_inc(consts_in, 16)
                sp.dma_start(tri[:, :, :], c_tri).then_inc(consts_in, 16)
                sp.dma_start(qn_bc[:, :], qnorm.partition_broadcast(P)).then_inc(consts_in, 16)
                sp.dma_start(kvn_bc[:, :], kvnorm.partition_broadcast(P)).then_inc(consts_in, 16)
                sp.dma_start(mask[:, :], c_mask).then_inc(consts_in, 16)
                for b in range(2):
                    sp.dma_start(tok_tab[:, b * NS:(b + 1) * NS, :, :],
                                 c_tok.rearrange("p (n r) w -> p n r w", n=NS)).then_inc(consts_in, 16)
                sp.dma_start(pos_tab[:, :, :], c_pos).then_inc(consts_in, 16)

            def load_ra():
                sp.dma_start(s_ra, ra.rearrange("(k p) n -> p k n", p=P)).then_inc(ra_in, 16)

            def load_bm():
                sp.dma_start(s_bm, bm).then_inc(bm_in, 16)

            def load_wq(p, g):
                sp.dma_start(s_wpe, wpe[bass.ds(g, 1)].rearrange("a (k p) n -> p (a k) n", p=P)).then_inc(wpe_in, 16)
                if p == 0:
                    sp.dma_start(s_wqn, wqn[bass.ds(2 * g, 2)].rearrange("h p n -> p h n")).then_inc(wq_in, 16)
                    sp.dma_start(s_wk, wk[bass.ds(2 * g, 2)].rearrange("h p n -> p h n")).then_inc(wq_in, 16)

            def landed_wq(p, g):
                if p == 0:
                    sp.wait_ge(wq_in, 32 * (g + 1))
                    settle(sp)
                sp.wait_ge(wpe_in, 16 * (p * NG + g + 1))
                settle(sp)

            def load_wo(g):
                sp.dma_start(s_wv, wv[bass.ds(2 * g, 2)].rearrange("h p n -> p h n")).then_inc(wo_in, 16)
                sp.dma_start(s_wo, wo[bass.ds(2 * g, 2)].rearrange("h p n -> p h n")).then_inc(wo_in, 16)

            def keep_wq(g):
                sp.wait_ge(q_dve, qbase_d(0, g))
                settle(sp)
                sp.dma_start(kept_q[bass.ds(g, 1)].rearrange("a p h s n -> p (a h) s n"),
                             w_q.bitcast(F32)).then_inc(wq_kept, 16)

            def keep_wo(g, last):
                sp.wait_ge(q_dve, qbase_d(0, g) + q_events(0, last)["m3"][1] + 1)
                settle(sp)
                sp.dma_start(kept_out[bass.ds(g, 1)].rearrange("a p h s n -> p (a h) s n"),
                             w_out.bitcast(F32)).then_inc(wo_kept, 16)
                sp.wait_ge(wo_kept, 16 * (g + 1))
                settle(sp)

            def body(p, g, first=False, last=False):
                ev = q_events(p, last)
                if p == 0:
                    if not first:
                        sp.wait_ge(q_full, qbase(p, g - 1) + q_events(p, False)["m3"][0] + 1)
                        settle(sp)
                    load_wo(g)
                if not last:
                    if p == 0:
                        sp.wait_ge(q_full, qbase(p, g))
                        settle(sp)
                    sp.wait_ge(wpe_hi, p * NG + g + 1)
                    settle(sp)
                    sp.wait_ge(wpe_lo, p * NG + g + 1)
                    settle(sp)
                    load_wq(p, g + 1)
                if p == 0:
                    keep_wq(g)
                    sp.wait_ge(wo_in, 32 * (g + 1))
                    settle(sp)
                if not last:
                    landed_wq(p, g + 1)
                if p == 0:
                    sp.wait_ge(wq_kept, 16 * (g + 1))
                    settle(sp)
                n = p * 2 * NG + 2 * g
                sp.wait_ge(q_act, qbase(p, g) + ev["pe1"][0] + 1)
                settle(sp)
                rotary(n + 1, 1, None if first else 4 * slot_n(p, g, 0))
                if not last:
                    sp.wait_ge(q_act, qbase(p, g) + ev["pe0"][0] + 1)
                    settle(sp)
                    rotary(n + 2, 0, 4 * slot_n(p, g, 2))
                if p == 0:
                    keep_wo(g, last)

            def rotary(n, b, used):
                for q in range(4):
                    o = q ^ 1
                    sp.dma_start(rope_f[32 * q:32 * q + 32, 1, :], rope_f[32 * o:32 * o + 32, 0, :])\
                      .then_inc(swap_in, 16)
                sp.wait_ge(rope_ready, n + 1)
                settle(sp)
                if used is not None:
                    sp.wait_ge(scores_done, used)
                    settle(sp)
                for h in range(2):
                    for part in range(2):
                        dst = 64 * (part ^ h)
                        sp.dma_start(qst[dst:dst + 64, b, h, :].bitcast(F32),
                                     rope_r[64 * h:64 * h + 64, part, :].bitcast(F32)).then_inc(qst_in, 16)
                sp.wait_ge(qst_in, 64 * (n + 1))
                settle(sp)

            def load_x(p, j):
                sp.dma_start(xacc[:, 2 * j:2 * j + 2, :], xt[p * NT + 2 * j:p * NT + 2 * j + 2]
                             .rearrange("a p d -> p a d")).then_inc(x_in[j], 16)

            def load_lats(n):
                def load(k, buf):
                    sp.dma_start(s_lat[:, buf:buf + 1, :],
                                 wzkv.rearrange("(k p) n -> p k n", p=P)[:, bass.ds(k, 1), :]).then_inc(wl_in[buf], 16)
                load(0, 0)
                load(1, 1)
                with sp.Fori(1, KD // 2) as j:
                    for buf in range(2):
                        sp.wait_ge(wl_hi, n * KD + 2 * j + buf - 1)
                        settle(sp)
                        sp.wait_ge(wl_lo, n * KD + 2 * j + buf - 1)
                        settle(sp)
                        load(2 * j + buf, buf)

            for p in range(NPAIR):
                phases(sp, p, 0)
                if p == 0:
                    load_ra()
                    load_x(p, 0)
                    load_bm()
                    for j in range(1, NT // 2):
                        load_x(p, j)
                    load_consts()
                    load_lats(0)
                sp.wait_ge(wl_hi, (p + 1) * KD)
                settle(sp)
                sp.wait_ge(wl_lo, (p + 1) * KD)
                settle(sp)
                sp.wait_ge(ra_hi, p + 1)
                settle(sp)
                sp.wait_ge(ra_lo, p + 1)
                settle(sp)
                load_wq(p, 0)
                landed_wq(p, 0)
                sp.wait_ge(q_act, qbase(p, 0) + PRO[p]["pe0"][0] + 1)
                settle(sp)
                rotary(p * 2 * NG, 0, None)
                end_phase(sp)
                phases(sp, p, 1)
                body(p, 0, first=True)
                with sp.Fori(1, NG - 1) as g:
                    body(p, g)
                body(p, NG - 1, last=True)
                sp.wait_ge(q_dve, qbase_d(p, NG - 1) + EVD[p] + 1 - len(BEFORE[p]))
                settle(sp)
                load_ra()
                load_bm()
                end_phase(sp)
                phases(sp, p, 2)
                if p + 1 < NPAIR:
                    load_lats(p + 1)
                    end_phase(sp)
                    for j in range(NT // 2):
                        sp.wait_ge(ffn_added, ffn_n(p, NT + 2 * j + 2))
                        settle(sp)
                        t = p * NT + 2 * j
                        sp.dma_start(outt[t:t + 2].rearrange("a p d -> p a d"), xacc[:, 2 * j:2 * j + 2, :])\
                          .then_inc(stored, 32)
                        sp.wait_ge(stored, 16 * (t + 2))
                        settle(sp)
                        load_x(p + 1, j)
                else:
                    with sp.Fori(0, NT) as t:
                        sp.wait_ge(ffn_added, ffn_n(p, NT + t + 1))
                        settle(sp)
                        sp.dma_start(outt[bass.ds(p * NT + t, 1)].rearrange("a p d -> p a d"),
                                     xacc[:, bass.ds(t, 1), :]).then_inc(stored, 16)
                    sp.wait_ge(stored, 16 * NT * (p + 1))
                    settle(sp)
                    end_phase(sp)

        @block.tensor
        def _(pe):
            def products(dst, passes, start=True, stop=True, skip=False):
                for n, (w, m) in enumerate(passes):
                    last = nc.tensor.matmul(dst, w, m, start=start and n == 0,
                                            stop=stop and n == len(passes) - 1, skip_group_check=skip)
                return last

            def three(w_hi, w_lo, m_hi_, m_lo_):
                return [(w_hi, m_hi_), (w_hi, m_lo_), (w_lo, m_hi_)]

            def turn_x(p, u, t, buf, two=False):
                pe.wait_ge(xn_ready, ln_n(p, u + t) + 1)
                if not (two and isinstance(t, int) and t < 2):
                    pe.wait_ge(xt_hi, ln_n(p, u + t) - two)
                    pe.wait_ge(xt_lo, ln_n(p, u + t) - two)
                bx = bxs[buf if two else 0]
                for k in range(KD):
                    last = nc.tensor.transpose(bx[:, k * P:(k + 1) * P], xn[:, buf, k * P:(k + 1) * P], ident[:, :])
                last.then_inc(xt_done, 1)

            def ffn_up(p, u, f, t, buf):
                pe.wait_ge(xt_hi, ln_n(p, u + t) + 1)
                pe.wait_ge(xt_lo, ln_n(p, u + t) + 1)
                if not (isinstance(t, int) and t < 2):
                    pe.wait_ge(h_read, ffn_n(p, f + t) - 1)
                passes = []
                for k in range(KD):
                    passes += three(xnT[:, buf, 0, k * P:(k + 1) * P], xnT[:, buf, 1, k * P:(k + 1) * P],
                                    w_ra[:, 0, k, :], w_ra[:, 1, k, :])
                products(bhs[buf], passes).then_inc(h_done, 1)

            def turn_h(p, n, part):
                h = half_n(p, n, part)
                pe.wait_ge(hw_ready, h + 1)
                if part or p or n:
                    pe.wait_ge(hwt_hi, h)
                    pe.wait_ge(hwt_lo, h)
                for t in range(HT):
                    last = nc.tensor.transpose(bhw[:, t * P:(t + 1) * P], hw[:, t, :], ident[:, :])
                last.then_inc(hwt_done, 1)

            def ffn_down(p, f, t, pair, before):
                if t % HT == 0:
                    n = half_n(p, f // NT, t // HT) + 1
                    pe.wait_ge(hwt_hi, n)
                    pe.wait_ge(hwt_lo, n)
                if before is not None:
                    pe.wait_ge(ffn_added, ffn_n(p, f + before) + 1)
                hT = [hwT[:, part, t * P:(t + 1) * P] for part in range(2)]
                for n in range(2):
                    s = slice(n * HALF, (n + 1) * HALF)
                    last = products(bout(pair)[:, n, :], three(hT[0], hT[1], w_bm[:, 0, s], w_bm[:, 1, s]))
                last.then_inc(ffn_done, 1)

            def latents(p, t, buf, k0, k1):
                if k0 == 0:
                    pe.wait_ge(xt_hi, ln_n(p, NT + t) + 1)
                    pe.wait_ge(xt_lo, ln_n(p, NT + t) + 1)
                    if not starts(t):
                        pe.wait_ge(z_read, 2 * lat_n(p, t))
                for k in range(k0, k1):
                    for n, (xp, wp) in enumerate(((0, 0), (0, 1), (1, 0))):
                        for half in range(2):
                            last = nc.tensor.matmul(bzs[half], xnT[:, buf, xp, k * P:(k + 1) * P],
                                                    w_lat[:, wp, k, half * ZH:(half + 1) * ZH],
                                                    start=(k == 0 and n == 0), stop=(k == KD - 1 and n == 2))
                if k1 == KD:
                    last.then_inc(zk_done, 1)

            def turn_latents(p, t, half):
                if half == 0:
                    pe.wait_ge(zck_ready, lat_n(p, t) + 2)
                    for n in range(4):
                        nc.tensor.transpose(bt[:, n * P:(n + 1) * P], zck[:, n * P:(n + 1) * P], ident[:, :])
                else:
                    nc.tensor.transpose(bkk, zck[:, 4 * P:5 * P], ident[:, :]).then_inc(zckt_done, 1)

            def norm_and_up(p, u, f):
                turn_x(p, u, 0, 0, two=True)
                turn_x(p, u, 1, 1, two=True)
                loads = p + (1 if f else 0)
                pe.wait_ge(ra_hi, loads + 1)
                pe.wait_ge(ra_lo, loads + 1)
                for n in range(2):
                    ffn_up(p, u, f, n, n)
                    turn_x(p, u, n + 2, n, two=True)
                with pe.Fori(1, NT // 2 - 1) as j:
                    for n in range(2):
                        ffn_up(p, u, f, 2 * j + n, n)
                        turn_x(p, u, 2 * j + n + 2, n, two=True)
                ffn_up(p, u, f, NT - 2, 0)
                ffn_up(p, u, f, NT - 1, 1)

            def tile_step(p, t):
                buf, back = t % 2, t > 0
                latents(p, t, buf, 0, 6)
                if back:
                    pe.wait_ge(lat_hi, 4 * lat_n(p, t - 1) + 1)
                    pe.wait_ge(lat_lo, 4 * lat_n(p, t - 1) + 1)
                    turn_latents(p, t - 1, 0)
                latents(p, t, buf, 6, 7)
                if t + 1 < NT:
                    turn_x(p, NT, t + 1, 1 - buf)
                latents(p, t, buf, 7, KD)
                if back:
                    turn_latents(p, t - 1, 1)
                if t == 0:
                    turn_h(p, 0, 1)
                if t + 3 < NT:
                    ffn_down(p, 0, t + 3, 0, t + 2)
                if t == NT - 3:
                    pe.wait_ge(ffn_added, ffn_n(p, NT))
                    pe.wait_ge(lat_hi, 4 * lat_n(p, NS) + 1)
                    pe.wait_ge(lat_lo, 4 * lat_n(p, NS) + 1)
                    fill(p, 0, "pe0", PRO[p])
                if t == NT - 2 and p == 0:
                    fill(p, 0, "w0", PRO[p])
                if t == NT - 1 and p == 0:
                    fill(p, 0, "w1", PRO[p])

            def fill(p, g, name, ev):
                a, d = ev[name]
                if not (ev is PRO[p] and name == "pe0"):
                    pe.wait_ge(q_act, qbase(p, g) + a)
                    if not (ev is PRO[p] and name == "w0"):
                        pe.wait_ge(q_dve, qbase_d(p, g) + d)
                if name[0] == "q":
                    k = int(name[1])
                    h, b = k % 2, k // 2
                    if p > 0 and k < 2:
                        pe.wait_ge(q_back[h], 16 * (g + (2 if k == 0 and ev is not PRO[p] else 1)))
                    s = slice(b * SEQ, (b + 1) * SEQ)
                    passes = []
                    for c in range(KQ):
                        cs = slice(c * P, (c + 1) * P)
                        passes += three(w_q[:, h, 0, cs], w_q[:, h, 1, cs], zT[:, 0, c, s], zT[:, 1, c, s])
                    products(bank_q, passes).then_inc(q_full, 1)
                elif name[:2] == "pe":
                    b = int(name[2])
                    n = p * NG + g + (1 if ev is PRO[p] or name == "pe1" else 2)
                    pe.wait_ge(wpe_hi, n)
                    pe.wait_ge(wpe_lo, n)
                    s = slice(b * SEQ, (b + 1) * SEQ)
                    passes = []
                    for c in range(KQ):
                        cs = slice(c * P, (c + 1) * P)
                        passes += three(w_pe[:, 0, cs], w_pe[:, 1, cs], zT[:, 0, c, s], zT[:, 1, c, s])
                    products(bank_q, passes).then_inc(q_full, 1)
                elif name[0] == "m":
                    h, half = int(name[1]) % 2, int(name[1]) // 2
                    pe.wait_ge(wo_in, 32 * (g + 1))
                    nc.tensor.matmul(bank_q, s_wv[:, h, :], s_wo[:, h, half * HALF:(half + 1) * HALF],
                                     start=True, stop=True).then_inc(q_full, 1)
                else:
                    h = int(name[1])
                    pe.wait_ge(wq_in, 32 * (g + (1 if ev is PRO[p] else 2)))
                    for c in range(KQ):
                        last = nc.tensor.matmul(bank_q[:, c * P:(c + 1) * P], s_wqn[:, h, c * P:(c + 1) * P],
                                                s_wk[:, h, :], start=True, stop=True)
                    last.then_inc(q_full, 1)

            def scores(p, g, k, i, first, last):
                h, b = k % 2, k // 2
                n = slot_n(p, g, k)
                if i == 0:
                    a, d = q_slot(p, g, k, first, last)
                    pe.wait_ge(q_act, a)
                    pe.wait_ge(q_dve, d)
                    if h == 0:
                        pe.wait_ge(qst_in, 64 * (p * 2 * NG + 2 * g + b + 1))
                if not (first and k == 0 and i < 2):
                    pe.wait_ge(exp_done, 4 * n + i - 1)
                qs = slice(i * P, (i + 1) * P)
                ks = slice(b * SEQ, b * SEQ + (i + 1) * P)
                dst = bank_s(i)[:, 0:(i + 1) * P]
                products(dst, three(qT[h][:, 0, qs], qT[h][:, 1, qs], keyT[:, 0, ks], keyT[:, 1, ks])
                         + [(qst[:, b, h, qs], ropeT[:, 0, ks]), (qst[:, b, h, qs], ropeT[:, 1, ks])])\
                    .then_inc(scores_done, 1)

            def turn_probs(n, k, i, first):
                pe.wait_ge(prob_ready, 4 * n + i + 1)
                if not (first and i < 2):
                    pe.wait_ge(pt_hi, 4 * n + i - 1)
                    pe.wait_ge(pt_lo, 4 * n + i - 1)
                for j in range(i + 1):
                    last = nc.tensor.transpose(bank_t(i)[:, j * P:(j + 1) * P],
                                               prob[:, k % 2, poff(i) + j * P:poff(i) + (j + 1) * P], ident[:, :])
                last.then_inc(pt_done, 1)

            def values(n, k, first):
                b = k // 2
                pe.wait_ge(pt_hi, 4 * n + 4)
                pe.wait_ge(pt_lo, 4 * n + 4)
                if not first:
                    pe.wait_ge(o_hi, n)
                    pe.wait_ge(o_lo, n)
                for j in range(NS):
                    t = b * NS + j
                    s = slice(j * P, SEQ)
                    last = products(bank_pv[:, s], three(lat[:, 0, t, :], lat[:, 1, t, :], pT[:, 0, j, s], pT[:, 1, j, s]),
                                    start=(j == 0), stop=(j == NS - 1))
                last.then_inc(pv_done, 1)

            def output(p, g, k, j, first, last):
                b, tt, half = y_slot(k, j)
                n = y_n(p, g, k) + j
                if k == 3 and j % 2 == 0:
                    if p == 0:
                        a, d = q_events(p, last)["m3" if half else "m1"]
                        pe.wait_ge(q_act, qbase(p, g) + a + 1)
                        pe.wait_ge(q_dve, qbase_d(p, g) + d + 1)
                    else:
                        pe.wait_ge(o_back[half], 16 * (g + 1))
                if j == 0 and k % 2 == 1:
                    pe.wait_ge(o_hi, slot_n(p, g, k) - 1)
                    pe.wait_ge(o_lo, slot_n(p, g, k) - 1)
                if not (first and j < 2):
                    pe.wait_ge(y_added, n - 1)
                ts = slice(tt * P, (tt + 1) * P)
                hs = slice(half * HALF, (half + 1) * HALF)
                passes = []
                for h in range(2):
                    passes += three(oT[:, b, h, 0, ts], oT[:, b, h, 1, ts], w_out[:, h, 0, hs], w_out[:, h, 1, hs])
                products(bank_y(j), passes).then_inc(y_done, 1)

            def fills(p, g, k, place, ev):
                name = fill_at(p, place, k)
                if name in ev:
                    fill(p, g, name, ev)

            def slot(p, g, k, first=False, last=False, drained=False):
                n, before = slot_n(p, g, k) - 1, (k - 1) % 4
                ev = {} if drained else q_events(p, last)
                turn = not (first and k == 0) and not (drained and k > 0)
                out_ = not first or k == 3
                if not drained:
                    scores(p, g, k, 0, first, last)
                    scores(p, g, k, 1, first, last)
                if turn:
                    turn_probs(n, before, 0, first and k == 1)
                    turn_probs(n, before, 1, first and k == 1)
                if out_:
                    output(p, g, k, 0, first, last)
                fills(p, g, k, "output", ev)
                if not drained:
                    scores(p, g, k, 2, first, last)
                if turn:
                    turn_probs(n, before, 2, False)
                if out_:
                    output(p, g, k, 1, first, last)
                fills(p, g, k, "second", ev)
                if not drained:
                    scores(p, g, k, 3, first, last)
                if turn:
                    turn_probs(n, before, 3, False)
                fills(p, g, k, "first", ev)
                if out_:
                    output(p, g, k, 2, first, last)
                fills(p, g, k, "third", ev)
                if turn:
                    values(n, before, first and k == 1)
                fills(p, g, k, "values", ev)
                if out_:
                    output(p, g, k, 3, first, last)

            def body(p, g, first=False, last=False):
                for k in range(4):
                    slot(p, g, k, first, last)

            end_phase(pe)
            pe.wait_ge(ident_in, 16)
            for p in range(NPAIR):
                phases(pe, p, 0)
                norm_and_up(p, 0, 0)
                turn_h(p, 0, 0)
                pe.wait_ge(bm_hi, p + 1)
                pe.wait_ge(bm_lo, p + 1)
                ffn_down(p, 0, 0, 0, None)
                ffn_down(p, 0, 1, 1, None)
                ffn_down(p, 0, 2, 0, 0)
                turn_x(p, NT, 0, 0)
                pe.wait_ge(wl_hi, (p + 1) * KD)
                pe.wait_ge(wl_lo, (p + 1) * KD)
                for t in range(NT):
                    tile_step(p, t)
                pe.wait_ge(lat_hi, 4 * lat_n(p, NT - 1) + 1)
                pe.wait_ge(lat_lo, 4 * lat_n(p, NT - 1) + 1)
                fill(p, 0, "q0", PRO[p])
                turn_latents(p, NT - 1, 0)
                turn_latents(p, NT - 1, 1)
                end_phase(pe)
                phases(pe, p, 1)
                body(p, 0, first=True)
                with pe.Fori(1, NG - 1) as g:
                    body(p, g)
                body(p, NG - 1, last=True)
                for k in range(3):
                    slot(p, NG, k, drained=True)
                end_phase(pe)
                phases(pe, p, 2)
                norm_and_up(p, 2 * NT, NT)
                turn_h(p, 1, 0)
                pe.wait_ge(bm_hi, p + 2)
                pe.wait_ge(bm_lo, p + 2)
                for t in range(NT):
                    if t == HT:
                        turn_h(p, 1, 1)
                    ffn_down(p, NT, t, t % 2, t - 2 if t > 1 else None)
                end_phase(pe)

        @block.scalar
        def _(act):
            def hi(dst, src):
                return nc.scalar.activation(dst, src, ACT.Copy)

            def split_ra(n):
                act.wait_ge(ra_in, 16 * (n + 1))
                hi(w_ra[:, 0], s_ra).then_inc(ra_hi, 1)

            def split_bm(n):
                act.wait_ge(bm_in, 16 * (n + 1))
                hi(w_bm[:, 0], s_bm).then_inc(bm_hi, 1)

            def normalise(p, u, t, buf):
                act.wait_ge(ln_rstd, ln_n(p, u + t) + 1)
                if not starts(u + t) and not (isinstance(t, int) and u + t == 1):
                    act.wait_ge(xt_done, ln_n(p, u + t) - 1)
                one = bass.ds(t, 1)
                nc.scalar.activation(xn[:, buf, :], xacc[:, one, :].rearrange("p a d -> p (a d)"), ACT.Identity,
                                     bias=mom[:, one, 3:4].rearrange("p a b -> p (a b)"),
                                     scale=mom[:, one, 2:3].rearrange("p a b -> p (a b)")).then_inc(xn_ready, 1)

            def turned_x(p, u, t, buf, two=False):
                act.wait_ge(xt_done, ln_n(p, u + t) + 1)
                hi(xnT[:, buf, 0, :], bxs[buf if two else 0]).then_inc(xt_hi, 1)

            def keep_h(p, f, t, buf):
                act.wait_ge(h_done, ffn_n(p, f + t) + 1)
                hi(hb[:, bass.ds(t, 1), :].rearrange("p a n -> p (a n)"), bhs[buf]).then_inc(h_read, 1)

            def lat_weights(n, k, buf):
                act.wait_ge(wl_in[buf], 8 * (n * KD + k - buf) + 16)
                hi(w_lat[:, 0, bass.ds(k, 1), :].rearrange("p a n -> p (a n)"), s_lat[:, buf, :]).then_inc(wl_hi, 1)

            def norm_and_up(p, u, f, weights):
                if p == 0 and f == 0:
                    split_ra(0)
                normalise(p, u, 0, 0)
                normalise(p, u, 1, 1)
                turned_x(p, u, 0, 0, two=True)
                normalise(p, u, 2, 0)

                def tile(t, buf, one=True, three=True):
                    if one:
                        turned_x(p, u, t + 1, 1 - buf, two=True)
                    if three:
                        normalise(p, u, t + 3, 1 - buf)
                    if weights is not None:
                        lat_weights(weights, t, buf)
                    keep_h(p, f, t, buf)
                with act.Fori(0, NT // 2 - 2) as j:
                    tile(2 * j, 0)
                    tile(2 * j + 1, 1)
                for t in range(NT - 4, NT):
                    if t == NT - 4 and (f or p == 0):
                        split_bm(p + (1 if f else 0))
                    tile(t, t % 2, t + 1 < NT, t + 3 < NT)
                    if t == NT - 3:
                        gates(p, f // NT, 0)

            def gates(p, n, part):
                act.wait_ge(gate_chain, half_n(p, n, part) * GATE_STEPS + 3)
                ts = slice(part * HT, (part + 1) * HT)
                nc.scalar.activation(lgt[:, 1, ts], lgt[:, 0, ts], ACT.Exp).then_inc(gate_exp, 1)

            def turned_h(p, n, part):
                act.wait_ge(hwt_done, half_n(p, n, part) + 1)
                hi(hwT[:, 0, part * HALF:(part + 1) * HALF], bhw).then_inc(hwt_hi, 1)

            def keep_latents(p, t):
                act.wait_ge(zk_done, lat_n(p, t) + 1)
                act.wait_ge(zck_ready, lat_n(p, t) + 1)
                for half in range(2):
                    hi(zr[:, half * ZH:(half + 1) * ZH], bzs[half]).then_inc(z_read, 1)

            def squares(p, t):
                act.wait_ge(rms_ready, lat_n(p, t) + 1)
                act.wait_ge(z_read, 2 * lat_n(p, t) + 2)
                nc.scalar.activation(junk[:, 0:QL], zr[:, 0:QL], ACT.Square, scale=float(QL ** -0.5),
                                     accum_out=ssq[:, 0, 0:1]).then_inc(ssq_ready, 1)
                act.wait_ge(ssq_ready, 2 * lat_n(p, t) + 1)
                nc.scalar.activation(junk[:, 0:L], zr[:, QL:QL + L], ACT.Square, scale=float(L ** -0.5),
                                     accum_out=ssq[:, 0, 1:2]).then_inc(ssq_ready, 1)

            def latents(p, t):
                act.wait_ge(zckt_done, lat_n(p, t) + 1)
                ts = bass.ds(t * P, P)
                hi(lat[:, 0, bass.ds(t, 1), :].rearrange("p a l -> p (a l)"), zck[:, QL:QL + L]).then_inc(lat_hi, 1)
                hi(zT[:, 0, :, ts], bt[:, 0:QL].rearrange("p (k t) -> p k t", k=KQ)).then_inc(lat_hi, 1)
                hi(keyT[:, 0, ts], bt[:, QL:QL + P]).then_inc(lat_hi, 1)
                hi(ropeT[:, 0, ts], bkk).then_inc(lat_hi, 1)

            def tile_step(p, t):
                if t + 1 < NT:
                    turned_x(p, NT, t + 1, (t + 1) % 2)
                keep_latents(p, t)
                if t == 0:
                    turned_h(p, 0, 1)
                squares(p, t)
                if t > 0:
                    latents(p, t - 1)
                if t + 2 < NT:
                    normalise(p, NT, t + 2, t % 2)
                if t == NT - 4:
                    split_wpe(p, 0)
                if t == NT - 3:
                    read_fill(p, 0, "pe0", PRO[p])
                    if p > 0:
                        q_weights_back(0, 0)
                        q_weights_back(0, 1)
                if t == NT - 2 and p == 0:
                    read_fill(p, 0, "w0", PRO[p])
                if t == NT - 1 and p == 0:
                    read_fill(p, 0, "w1", PRO[p])

            def q_weights_back(g, h):
                act.dma_start(w_q[:, h].bitcast(F32), kept_q[bass.ds(g, 1), :, h].rearrange("a p s n -> p (a s) n"))\
                   .then_inc(q_back[h], 16)

            def out_weights_back(p, g, half, first):
                if not first:
                    act.wait_ge(y_done, y_n(p, g, 2) + 2 * half + 2)
                    settle(act)
                s = slice(half * HALF, (half + 1) * HALF)
                act.dma_start(w_out[:, :, :, s].rearrange("p h s n -> p (h s) n").bitcast(F32),
                              kept_out[bass.ds(g, 1), :, :, :, s].rearrange("a p h s n -> p (a h s) n"))\
                   .then_inc(o_back[half], 16)

            def read_fill(p, g, name, ev, first=False):
                a, d = ev[name]
                act.wait_ge(q_full, qbase(p, g) + a + 1)
                if name[0] == "q":
                    dst = qT[int(name[1]) % 2][:, 0, :]
                    src = bank_q
                elif name[:2] == "pe":
                    if ev is not PRO[p]:
                        act.wait_ge(rope_ready, p * 2 * NG + 2 * g + (1 if name == "pe1" else 2))
                    dst, src = rope_f[:, 0, :], bank_q
                elif name[0] == "m":
                    h, half = int(name[1]) % 2, int(name[1]) // 2
                    if name in ("m0", "m2") and not first:
                        act.wait_ge(wo_kept, 16 * g)
                    dst, src = w_out[:, h, 0, half * HALF:(half + 1) * HALF], bank_q
                else:
                    if name == "w0" and ev is not PRO[p]:
                        act.wait_ge(wq_kept, 16 * (g + 1))
                    dst, src = w_q[:, int(name[1]), 0, :], bank_q[:, 0:QL]
                hi(dst, src).then_inc(q_act, 1)

            def exps(p, g, k, i):
                n = slot_n(p, g, k)
                act.wait_ge(max_ready, 4 * n + i + 1)
                nc.scalar.activation(prob[:, k % 2, poff(i):poff(i + 1)], bank_s(i)[:, 0:(i + 1) * P], ACT.Exp,
                                     bias=negmax[:, k % 2, i:i + 1],
                                     accum_out=rowsum[:, k % 2, i:i + 1]).then_inc(exp_done, 1)

            def turned(n, i):
                act.wait_ge(pt_done, 4 * n + i + 1)
                hi(pT[:, 0, 0:i + 1, i * P:(i + 1) * P],
                   bank_t(i)[:, 0:(i + 1) * P].rearrange("p (j s) -> p j s", s=P)).then_inc(pt_hi, 1)

            def valued(n, k):
                act.wait_ge(pv_done, n + 1)
                hi(oT[:, k // 2, k % 2, 0, :], bank_pv).then_inc(o_hi, 1)

            def split_wpe(p, g):
                act.wait_ge(wpe_in, 16 * (p * NG + g + 1))
                hi(w_pe[:, 0, :], s_wpe.rearrange("p k n -> p (k n)")).then_inc(wpe_hi, 1)

            def body(p, g, first=False, last=False):
                ev = q_events(p, last)

                def fills(k, place):
                    name = fill_at(p, place, k)
                    if name in ev:
                        read_fill(p, g, name, ev, first)
                for k in range(4):
                    n, before = slot_n(p, g, k) - 1, (k - 1) % 4
                    turn = not (first and k == 0)
                    exps(p, g, k, 0)
                    exps(p, g, k, 1)
                    if turn:
                        turned(n, 0)
                        turned(n, 1)
                    fills(k, "output")
                    if turn:
                        turned(n, 2)
                    exps(p, g, k, 2)
                    fills(k, "second")
                    if k == 2 and p > 0:
                        out_weights_back(p, g, 0, first)
                    if turn:
                        turned(n, 3)
                    exps(p, g, k, 3)
                    fills(k, "first")
                    if k == 1 and not last:
                        split_wpe(p, g + 1)
                        if p > 0:
                            q_weights_back(g + 1, 0)
                    fills(k, "third")
                    if turn:
                        valued(n, before)
                    fills(k, "values")
                    if k == 2 and p > 0:
                        if not last:
                            q_weights_back(g + 1, 1)
                        out_weights_back(p, g, 1, first)

            end_phase(act)
            act.sem_inc(lat_hi, 1)
            for p in range(NPAIR):
                phases(act, p, 0)
                norm_and_up(p, 0, 0, 0 if p == 0 else None)
                turned_h(p, 0, 0)
                normalise(p, NT, 0, 0)
                gates(p, 0, 1)
                turned_x(p, NT, 0, 0)
                normalise(p, NT, 1, 1)
                for t in range(NT):
                    tile_step(p, t)
                read_fill(p, 0, "q0", PRO[p])
                latents(p, NT - 1)
                end_phase(act)
                phases(act, p, 1)
                body(p, 0, first=True)
                with act.Fori(1, NG - 1) as g:
                    body(p, g)
                body(p, NG - 1, last=True)
                for i in range(NS):
                    turned(slot_n(p, NG, 0) - 1, i)
                valued(slot_n(p, NG, 0) - 1, 3)
                split_ra(p + 1)
                end_phase(act)
                phases(act, p, 2)
                norm_and_up(p, 2 * NT, NT, p + 1 if p + 1 < NPAIR else None)
                turned_h(p, 1, 0)
                gates(p, 1, 1)
                turned_h(p, 1, 1)
                end_phase(act)

        @block.vector
        def _(dve):
            def lo(dst, src, part):
                return nc.vector.tensor_tensor(dst, src, part.bitcast(F32), ALU.subtract)

            def split_ra(n):
                dve.wait_ge(ra_hi, n + 1)
                lo(w_ra[:, 1], s_ra, w_ra[:, 0]).then_inc(ra_lo, 1)

            def moments(p, u, t, added=None, outputs=None):
                if outputs is not None:
                    dve.wait_ge(y_added, outputs)
                    settle(dve)
                if added is not None:
                    dve.wait_ge(ffn_added, added)
                    settle(dve)
                one = bass.ds(t, 1)
                xs = xacc[:, one, :].rearrange("p a d -> p (a d)")

                def m(a, b):
                    return mom[:, one, a:b].rearrange("p a b -> p (a b)")
                base = ln_n(p, u + t) * 5
                for n in range(2):
                    nc.vector.bn_stats(stats[:, n, :], xs[:, n * HALF:(n + 1) * HALF]).then_inc(ln_chain, 1)
                dve.wait_ge(ln_chain, base + 2)
                settle(dve)
                nc.vector.bn_aggr(mv[:, :], stats[:, :, :]).then_inc(ln_chain, 1)
                dve.wait_ge(ln_chain, base + 3)
                nc.vector.tensor_scalar_add(m(0, 1), mv[:, 1:2], LN_EPS).then_inc(ln_chain, 1)
                nc.vector.tensor_scalar(m(1, 2), mv[:, 0:1], -1.0, None, ALU.mult).then_inc(ln_chain, 1)

            def turned_x(p, u, t, buf, two=False):
                dve.wait_ge(xt_hi, ln_n(p, u + t) + 1)
                lo(xnT[:, buf, 1, :], bxs[buf if two else 0], xnT[:, buf, 0, :]).then_inc(xt_lo, 1)

            def norm_and_up(p, u, load):
                for t in range(0 if load else 2, NT + 3):
                    if t < NT:
                        if load and t % 2 == 0:
                            dve.wait_ge(x_in[t // 2], 16 * (p + 1))
                            settle(dve)
                        moments(p, u, t)
                    if t == NT and p == 0 and load:
                        dve.wait_ge(consts_in, 16 * 8)
                        nc.vector.tensor_scalar(qn_bc[:, :], qn_bc[:, :], QSCALE, None, ALU.mult)\
                          .then_inc(vec_const, 1)
                        dve.wait_ge(vec_const, 1)
                    if t >= 3:
                        turned_x(p, u, t - 3, (t - 3) % 2, two=True)
                    if t >= NT:
                        gates(p, 0 if load else 1, 0, t - NT)

            def gates(p, n, part, stage_):
                first = (0, 3, 8, GATE_STEPS)
                step = [first[stage_]]
                base = half_n(p, n, part) * GATE_STEPS

                def link(ins):
                    step[0] += 1
                    ins.then_inc(gate_chain, 1)
                    dve.wait_ge(gate_chain, base + step[0])
                V = nc.vector
                ts = slice(part * HT, (part + 1) * HT)
                logit, ex, gate = (lgt[:, i, ts] for i in range(3))
                top, total, scale = (gsc[:, i, ts] for i in range(3))

                def per_tile(ap):
                    return ap.rearrange("p (t a) -> p t a", a=1).to_broadcast([P, HT, E])
                if stage_ == 0:
                    dve.wait_ge(h_read, ffn_n(p, n * NT + (part + 1) * HT))
                    link(V.tensor_tensor(logit, hb[:, ts, 0:E],
                                         rb_bc[:, :].rearrange("p (a e) -> p a e", a=1).to_broadcast([P, HT, E]),
                                         ALU.add))
                    link(V.tensor_reduce(top, logit, AX_X, ALU.max))
                    link(V.tensor_tensor(logit, logit, per_tile(top), ALU.subtract))
                if stage_ == 1:
                    dve.wait_ge(gate_exp, half_n(p, n, part) + 1)
                    mine = ex.rearrange("p t (e a) -> p t e a", a=1).to_broadcast([P, HT, E, E])
                    other = ex.rearrange("p t (a e) -> p t a e", a=1).to_broadcast([P, HT, E, E])
                    before = tri[:, :, :].rearrange("p (a e) f -> p a e f", a=1).to_broadcast([P, HT, E, E])
                    link(V.tensor_tensor(cmp[:, 0], other, mine, ALU.is_gt))
                    link(V.tensor_tensor(cmp[:, 1], other, mine, ALU.is_equal))
                    link(V.tensor_tensor(cmp[:, 1], cmp[:, 1], before, ALU.mult))
                    link(V.tensor_tensor(cmp[:, 0], cmp[:, 0], cmp[:, 1], ALU.add))
                    link(V.tensor_reduce(rank[:, ts], cmp[:, 0], AX_X, ALU.add))
                if stage_ == 2:
                    link(V.scalar_tensor_tensor(gate, rank[:, ts], 1.5, ex, ALU.is_lt, ALU.mult))
                    link(V.tensor_reduce(total, gate, AX_X, ALU.add))
                    link(V.reciprocal(scale, total))
                    link(V.tensor_scalar(scale, scale, FFN_SCALE, None, ALU.mult))
                    link(V.tensor_tensor(gate, gate, per_tile(scale), ALU.mult))
                    if part or n or p:
                        dve.wait_ge(hwt_done, half_n(p, n, part))
                    w = gate.rearrange("p t (e a) -> p t e a", a=1).to_broadcast([P, HT, E, R])
                    V.tensor_tensor(hw[:, :].rearrange("p t (e r) -> p t e r", r=R),
                                    hb[:, ts, E:RA].rearrange("p t (e r) -> p t e r", r=R), w,
                                    ALU.mult).then_inc(hw_ready, 1)
                assert step[0] == first[stage_ + 1]

            def turned_h(p, n, part):
                dve.wait_ge(hwt_hi, half_n(p, n, part) + 1)
                s = slice(part * HALF, (part + 1) * HALF)
                lo(hwT[:, 1, s], bhw, hwT[:, 0, s]).then_inc(hwt_lo, 1)

            def ffn_add(p, f, t, pair=0):
                dve.wait_ge(ffn_done, ffn_n(p, f + t) + 1)
                xs = xacc[:, bass.ds(t, 1), :].rearrange("p a (n d) -> p (a n) d", n=2)
                nc.vector.tensor_tensor(xs, bout(pair), xs, ALU.add).then_inc(ffn_added, 1)

            def tokens(p, t):
                V = nc.vector
                dve.wait_ge(z_read, 2 * lat_n(p, t) + 2)
                cs = tok_tab[:, bass.ds(t, 1), 0, :].rearrange("p a w -> p (a w)")
                sn = tok_tab[:, bass.ds(t, 1), 1, :].rearrange("p a w -> p (a w)")
                H = RO // 2
                k0 = QL + L
                V.tensor_tensor(rtmp[:, 0, :], zr[:, k0:ZK], cs, ALU.mult)
                V.tensor_tensor(rtmp[:, 1, 0:H], zr[:, k0 + H:ZK], sn[:, 0:H], ALU.mult)
                V.tensor_tensor(rtmp[:, 1, H:RO], zr[:, k0:k0 + H], sn[:, H:RO], ALU.mult).then_inc(tok_chain, 1)
                dve.wait_ge(lat_lo, 4 * lat_n(p, t) + 1)
                dve.wait_ge(rms_ready, lat_n(p, t) + 2)
                V.scalar_tensor_tensor(zck[:, 0:QL], zr[:, 0:QL], rms[:, 0:1], qn_bc[:, :], ALU.mult, ALU.mult)
                V.scalar_tensor_tensor(zck[:, QL:QL + L], zr[:, QL:QL + L], rms[:, 1:2], kvn_bc[:, :],
                                       ALU.mult, ALU.mult)
                dve.wait_ge(tok_chain, lat_n(p, t) + 1)
                twice = [rtmp[:, n, :].rearrange("p (a w) -> p a w", a=1).to_broadcast([P, 2, RO]) for n in range(2)]
                V.tensor_tensor(zck[:, QL + L:ZK + RO].rearrange("p (a w) -> p a w", a=2),
                                twice[0], twice[1], ALU.add).then_inc(zck_ready, 1)

            def latents(p, t):
                ts = bass.ds(t * P, P)
                n = 4 * lat_n(p, t) + 1
                dve.wait_ge(lat_hi, n + 1)
                one = bass.ds(t, 1)
                lo(lat[:, 1, one, :].rearrange("p a l -> p (a l)"), zck[:, QL:QL + L],
                   lat[:, 0, one, :].rearrange("p a l -> p (a l)")).then_inc(lat_lo, 1)
                dve.wait_ge(lat_hi, n + 3)
                lo(zT[:, 1, :, ts], bt[:, 0:QL].rearrange("p (k t) -> p k t", k=KQ), zT[:, 0, :, ts]).then_inc(lat_lo, 1)
                lo(keyT[:, 1, ts], bt[:, QL:QL + P], keyT[:, 0, ts]).then_inc(lat_lo, 1)
                dve.wait_ge(lat_hi, n + 4)
                lo(ropeT[:, 1, ts], bkk, ropeT[:, 0, ts]).then_inc(lat_lo, 1)

            def tile_step(p, t):
                if t > 1:
                    latents(p, t - 2)
                if t > 0:
                    tokens(p, t - 1)
                if t + 2 < NT:
                    moments(p, NT, t + 2, added=ffn_n(p, t + 3))
                if t + 1 < NT:
                    turned_x(p, NT, t + 1, (t + 1) % 2)
                if t == 0:
                    turned_h(p, 0, 1)
                if t + 3 < NT:
                    ffn_add(p, 0, t + 3)
                if t == NT - 4:
                    split_wpe(p, 0)
                if t == NT - 2 and p == 0:
                    read_fill(p, 0, "w0", PRO[p])
                if t == NT - 1 and p == 0:
                    read_fill(p, 0, "w1", PRO[p])

            def read_fill(p, g, name, ev):
                a, d = ev[name]
                if name[:2] == "pe":
                    return
                dve.wait_ge(q_act, qbase(p, g) + a + 1)
                if name[0] == "q":
                    h = int(name[1]) % 2
                    lo(qT[h][:, 1, :], bank_q, qT[h][:, 0, :]).then_inc(q_dve, 1)
                elif name[0] == "m":
                    h, s = int(name[1]) % 2, slice(int(name[1]) // 2 * HALF, (int(name[1]) // 2 + 1) * HALF)
                    lo(w_out[:, h, 1, s], bank_q, w_out[:, h, 0, s]).then_inc(q_dve, 1)
                else:
                    h = int(name[1])
                    lo(w_q[:, h, 1, :], bank_q[:, 0:QL], w_q[:, h, 0, :]).then_inc(q_dve, 1)

            def maxima(p, g, k, i):
                n = slot_n(p, g, k)
                dve.wait_ge(scores_done, 4 * n + i + 1)
                diagonal = bank_s(i)[:, i * P:(i + 1) * P]
                nc.vector.tensor_tensor(diagonal, diagonal, mask[:, :], ALU.add).then_inc(masked, 1)
                dve.wait_ge(masked, 4 * n + i + 1)
                nc.vector.tensor_reduce(negmax[:, k % 2, i:i + 1], bank_s(i)[:, 0:(i + 1) * P], AX_X, ALU.max,
                                        negate=True).then_inc(max_ready, 1)

            def norms(p, g, k):
                n = slot_n(p, g, k)
                dve.wait_ge(exp_done, 4 * n + NS)
                nc.vector.reciprocal(rrec[:, k % 2, :], rowsum[:, k % 2, :]).then_inc(rec_ready, 1)
                dve.wait_ge(rec_ready, n + 1)
                for i in range(NS):
                    pr = prob[:, k % 2, poff(i):poff(i + 1)]
                    nc.vector.tensor_scalar(pr, pr, rrec[:, k % 2, i:i + 1], None, ALU.mult).then_inc(prob_ready, 1)

            def pt_split(n, i):
                dve.wait_ge(pt_hi, 4 * n + i + 1)
                ap = [pT[:, part, 0:i + 1, i * P:(i + 1) * P] for part in range(2)]
                lo(ap[1], bank_t(i)[:, 0:(i + 1) * P].rearrange("p (j s) -> p j s", s=P), ap[0]).then_inc(pt_lo, 1)

            def y_add(p, g, k, j):
                b, tt, half = y_slot(k, j)
                dve.wait_ge(y_done, y_n(p, g, k) + j + 1)
                xs = xacc[:, b * NS + tt, half * HALF:(half + 1) * HALF]
                nc.vector.tensor_tensor(xs, bank_y(j), xs, ALU.add).then_inc(y_added, 1)

            def o_split(n, k):
                dve.wait_ge(o_hi, n + 1)
                lo(oT[:, k // 2, k % 2, 1, :], bank_pv, oT[:, k // 2, k % 2, 0, :]).then_inc(o_lo, 1)

            def split_wpe(p, g):
                dve.wait_ge(wpe_hi, p * NG + g + 1)
                lo(w_pe[:, 1, :], s_wpe.rearrange("p k n -> p (k n)"), w_pe[:, 0, :]).then_inc(wpe_lo, 1)

            def slot(p, g, k, first=False, last=False, drained=False):
                n, before = slot_n(p, g, k) - 1, (k - 1) % 4
                ev = {} if drained else q_events(p, last)
                turn = not (first and k == 0) and not (drained and k > 0)
                out_ = not first or k == 3

                def fills(place):
                    name = fill_at(p, place, k)
                    if name in ev:
                        read_fill(p, g, name, ev)
                if not drained:
                    maxima(p, g, k, 0)
                    maxima(p, g, k, 1)
                if turn:
                    pt_split(n, 0)
                    pt_split(n, 1)
                if out_:
                    y_add(p, g, k, 0)
                fills("output")
                if not drained:
                    maxima(p, g, k, 2)
                if turn:
                    pt_split(n, 2)
                if out_:
                    y_add(p, g, k, 1)
                fills("second")
                if not drained:
                    maxima(p, g, k, 3)
                if turn:
                    pt_split(n, 3)
                fills("first")
                if k == 1 and not last and not drained:
                    split_wpe(p, g + 1)
                if not drained:
                    norms(p, g, k)
                if out_:
                    y_add(p, g, k, 2)
                fills("third")
                if turn:
                    o_split(n, before)
                fills("values")
                if out_:
                    y_add(p, g, k, 3)

            def body(p, g, first=False, last=False):
                for k in range(4):
                    slot(p, g, k, first, last)

            end_phase(dve)
            dve.sem_inc(lat_lo, 1)
            dve.sem_inc(zck_ready, 1)
            for p in range(NPAIR):
                phases(dve, p, 0)
                if p == 0:
                    split_ra(0)
                norm_and_up(p, 0, True)
                turned_h(p, 0, 0)
                ffn_add(p, 0, 0)
                moments(p, NT, 0, added=ffn_n(p, 1))
                gates(p, 0, 1, 0)
                ffn_add(p, 0, 1, 1)
                moments(p, NT, 1, added=ffn_n(p, 2))
                gates(p, 0, 1, 1)
                turned_x(p, NT, 0, 0)
                ffn_add(p, 0, 2)
                gates(p, 0, 1, 2)
                for t in range(NT):
                    tile_step(p, t)
                latents(p, NT - 2)
                tokens(p, NT - 1)
                read_fill(p, 0, "q0", PRO[p])
                latents(p, NT - 1)
                end_phase(dve)
                phases(dve, p, 1)
                body(p, 0, first=True)
                with dve.Fori(1, NG - 1) as g:
                    body(p, g)
                body(p, NG - 1, last=True)
                for k in range(3):
                    slot(p, NG, k, drained=True)
                    if k < 2:
                        moments(p, 2 * NT, k, outputs=y_n(p, NG, 0) + 4)
                split_ra(p + 1)
                end_phase(dve)
                phases(dve, p, 2)
                norm_and_up(p, 2 * NT, False)
                turned_h(p, 1, 0)
                for t in range(3):
                    gates(p, 1, 1, t)
                    ffn_add(p, NT, t, t % 2)
                ffn_add(p, NT, 3, 1)
                turned_h(p, 1, 1)
                with dve.Fori(HT // 2, HT) as j:
                    ffn_add(p, NT, 2 * j, 0)
                    ffn_add(p, NT, 2 * j + 1, 1)
                end_phase(dve)

        @block.gpsimd
        def _(pool):
            G = nc.gpsimd

            def ln(p, u, t):
                one = bass.ds(t, 1)

                def m(a):
                    return mom[:, one, a:a + 1].rearrange("p a b -> p (a b)")
                pool.wait_ge(ln_chain, 5 * ln_n(p, u + t) + 5)
                G.tensor_tensor(m(2), m(0), neg_half[:, 0:1], ALU.pow).then_inc(pool_chain, 1)
                pool.wait_ge(pool_chain, ln_n(p, u + t) + 1)
                G.tensor_tensor(m(3), m(1), m(2), ALU.mult).then_inc(ln_rstd, 1)

            def lat_weights(n, k, buf):
                pool.wait_ge(wl_hi, n * KD + k + 1)
                one = bass.ds(k, 1)
                G.tensor_tensor(w_lat[:, 1, one, :].rearrange("p a n -> p (a n)"), s_lat[:, buf, :],
                                w_lat[:, 0, one, :].rearrange("p a n -> p (a n)").bitcast(F32),
                                ALU.subtract).then_inc(wl_lo, 1)

            def norms(p, u, weights):
                for t in range(0 if u == 0 else 2, 3):
                    ln(p, u, t)

                def tile(t, buf, three=True):
                    if three:
                        ln(p, u, t + 3)
                    if weights is not None:
                        lat_weights(weights, t, buf)
                with pool.Fori(0, NT // 2 - 2) as j:
                    tile(2 * j, 0)
                    tile(2 * j + 1, 1)
                for t in range(NT - 4, NT):
                    tile(t, t % 2, t + 3 < NT)
                    if t == NT - 3 and (u or p == 0):
                        split_bm(p + (1 if u else 0))

            def split_bm(n):
                pool.wait_ge(bm_hi, n + 1)
                G.tensor_tensor(w_bm[:, 1], s_bm, w_bm[:, 0].bitcast(F32), ALU.subtract).then_inc(bm_lo, 1)

            def rms_norm(p, t):
                pool.wait_ge(ssq_ready, 2 * lat_n(p, t) + 2)
                settle(pool)
                G.tensor_scalar_add(ssq[:, 1, :], ssq[:, 0, :], RMS_EPS).then_inc(rms_chain, 1)
                pool.wait_ge(rms_chain, lat_n(p, t) + 1)
                settle(pool)
                pool.wait_ge(zck_ready, lat_n(p, t) + 1)
                settle(pool)
                G.tensor_tensor(rms[:, :], ssq[:, 1, :], neg_half[:, :], ALU.pow).then_inc(rms_ready, 1)

            def rotate(n, a_wait, first=False):
                step = [4 * n]

                def link(ins):
                    step[0] = step[0] + 1
                    ins.then_inc(rope_chain, 1)
                    pool.wait_ge(rope_chain, step[0])
                    settle(pool)
                pool.wait_ge(q_act, a_wait)
                settle(pool)
                if not first:
                    pool.wait_ge(qst_in, 64 * n)
                    settle(pool)
                link(G.tensor_tensor(rope_f[:, 2, :], rope_f[:, 0, :], pos_tab[:, 0, :], ALU.mult))
                pool.wait_ge(swap_in, 64 * (n + 1))
                settle(pool)
                link(G.tensor_tensor(rope_f[:, 1, :], rope_f[:, 1, :], pos_tab[:, 1, :], ALU.mult))
                link(G.tensor_tensor(rope_r[:, 0, :], rope_f[:, 2, :], rope_f[:, 1, :], ALU.add))
                link(G.tensor_tensor(rope_f[:, 2, :], rope_f[:, 2, :], rope_f[:, 1, :], ALU.add))
                G.tensor_tensor(rope_r[:, 1, :], rope_f[:, 2, :], rope_r[:, 0, :].bitcast(F32),
                                ALU.subtract).then_inc(rope_ready, 1)

            def body(p, g, last=False):
                ev = q_events(p, last)
                n = p * 2 * NG + 2 * g
                rotate(n + 1, qbase(p, g) + ev["pe1"][0] + 1)
                if not last:
                    rotate(n + 2, qbase(p, g) + ev["pe0"][0] + 1)

            end_phase(pool)
            pool.sem_inc(rms_ready, 1)
            G.memset(neg_half[:, :], -0.5).then_inc(half_ready, 1)
            pool.wait_ge(half_ready, 1)
            for p in range(NPAIR):
                phases(pool, p, 0)
                norms(p, 0, 0 if p == 0 else None)
                if p == 0:
                    pool.wait_ge(consts_in, 16 * 8)
                    settle(pool)
                for t in range(3):
                    ln(p, NT, t)
                with pool.Fori(0, NT - 3) as t:
                    rms_norm(p, t)
                    ln(p, NT, t + 3)
                rms_norm(p, NT - 3)
                rms_norm(p, NT - 2)
                rotate(p * 2 * NG, qbase(p, 0) + PRO[p]["pe0"][0] + 1, first=True)
                rms_norm(p, NT - 1)
                end_phase(pool)
                phases(pool, p, 1)
                with pool.Fori(0, NG - 1) as g:
                    body(p, g)
                body(p, NG - 1, last=True)
                for t in range(2):
                    ln(p, 2 * NT, t)
                end_phase(pool)
                phases(pool, p, 2)
                norms(p, 2 * NT, p + 1 if p + 1 < NPAIR else None)
                end_phase(pool)


def kernel(L0_attn_x, L0_attn_wq_a, L0_attn_q_norm_w, L0_attn_wq_b, L0_attn_wkv_a, L0_attn_kv_norm_w,
           L0_attn_wkv_b, L0_attn_wo, L0_ffn_router_w, L0_ffn_router_b, L0_ffn_A, L0_ffn_Bm):
    import numpy as np
    import concourse.bacc as bacc
    from concourse import mybir as mb
    from concourse.bass_utils import run_bass_kernel_spmd

    B, S, D = np.shape(L0_attn_x)
    QL = np.shape(L0_attn_wq_a)[0]
    L = np.shape(L0_attn_kv_norm_w)[0]
    RO = np.shape(L0_attn_wkv_a)[0] - L
    NOPE = 128
    NH = np.shape(L0_attn_wq_b)[0] // (NOPE + RO)
    E, R, _ = np.shape(L0_ffn_A)
    pairs = np.r_[0:RO:2, 1:RO:2]

    wkv_a = np.asarray(L0_attn_wkv_a)
    wkv_a = np.concatenate([wkv_a[:L], wkv_a[L:][pairs]])
    wq_b = np.asarray(L0_attn_wq_b).reshape(NH, NOPE + RO, QL)
    rot = wq_b[:, NOPE:][:, pairs].reshape(NH // 2, 2 * RO, QL)
    wkv_b = np.asarray(L0_attn_wkv_b).reshape(NH, 2 * NOPE, L)

    freq = (1.0 / np.float32(10000.0) ** (np.arange(0, RO, 2, dtype=np.float32) / np.float32(RO))).astype(np.float32)
    ang = np.outer(np.arange(S, dtype=np.float32), freq).astype(np.float32)
    cos, sin = np.cos(ang), np.sin(ang)
    tok = np.stack([np.concatenate([cos, cos], 1), np.concatenate([-sin, sin], 1)], 1)
    pos = np.stack([np.concatenate([cos, cos, cos, cos], 1), np.concatenate([-sin, sin, -sin, sin], 1)], 0)
    row = np.arange(128)
    arrays = {
        "x": np.asarray(L0_attn_x).reshape(B * S, D),
        "wzkv": np.concatenate([np.asarray(L0_attn_wq_a), wkv_a]).T,
        "qnorm": np.asarray(L0_attn_q_norm_w),
        "kvnorm": np.asarray(L0_attn_kv_norm_w),
        "wqn": wq_b[:, :NOPE],
        "wpe": rot.transpose(0, 2, 1),
        "wk": wkv_b[:, :NOPE],
        "wv": wkv_b[:, NOPE:],
        "wo": np.asarray(L0_attn_wo).T.reshape(NH, NOPE, D),
        "ra": np.concatenate([np.asarray(L0_ffn_router_w), np.asarray(L0_ffn_A).reshape(E * R, D)]).T,
        "rb": np.asarray(L0_ffn_router_b),
        "bm": np.asarray(L0_ffn_Bm).transpose(0, 2, 1).reshape(E * R, D),
        "c_ident": np.eye(128, dtype=np.float32),
        "c_mask": np.where(row[None, :] <= row[:, None], 0.0, MASKED).astype(np.float32),
        "c_tri": np.broadcast_to(np.tri(E, k=-1, dtype=np.float32), (128, E, E)),
        "c_tok": tok.reshape(S // 128, 128, 2, RO).transpose(1, 0, 2, 3).reshape(128, S // 128 * 2, RO),
        "c_pos": pos.transpose(2, 0, 1),
    }
    nc = bacc.Bacc("TRN2", target_bir_lowering=False, num_devices=1)
    feeds, args = {}, []
    for name, a in arrays.items():
        a = np.ascontiguousarray(a)
        feeds[f"in_{name}"] = a
        args.append(nc.dram_tensor(f"in_{name}", a.shape, mb.dt.from_np(a.dtype), kind="ExternalInput").ap())
    names = list(arrays)
    out = nc.dram_tensor("out_0", (B * S, D), mb.dt.float32, kind="ExternalOutput").ap()
    kept_out = nc.dram_tensor("kept_out", (NH // 2, 128, 2, 2, D), mb.dt.float32, kind="Internal").ap()
    kept_q = nc.dram_tensor("kept_q", (NH // 2, 128, 2, 2, QL), mb.dt.float32, kind="Internal").ap()
    build_macaron(nc, **dict(zip(names, args)), kept_out=kept_out, kept_q=kept_q, out=out)
    r = run_bass_kernel_spmd(nc, [feeds], core_ids=[0])
    return r.results[0]["out_0"].reshape(B, S, D)
```
